# Optimizing a Trainium2 kernel written in Bass

```python
import numpy as np
import jax
import jax.numpy as jnp

def _softmax(x, axis=-1):
    return jax.nn.softmax(x, axis=axis)

def _gelu(x):
    return jax.nn.gelu(x, approximate=True)

def _silu(x):
    return jax.nn.silu(x)

def _sigmoid(x):
    return jax.nn.sigmoid(x)

def _layernorm(x, axis=-1, eps=1e-05):
    m = jnp.mean(x, axis=axis, keepdims=True)
    v = jnp.var(x, axis=axis, keepdims=True)
    return (x - m) / jnp.sqrt(v + eps)

def _scatter_add(tgt, idx, src, axis=0):
    return tgt.at[idx].add(src)

def _segment_sum(src, seg, n):
    return jax.ops.segment_sum(src, seg, n)
kernel_name = 'mk_gnn_resnorm_d2_gnn_r64_ef301f'

def setup_inputs(seed: int=0):
    np.random.seed(seed)
    _w = jnp.asarray

    def _rec_inputs():
        import jax
        import jax.numpy as jnp
        _gk = jax.random.key(seed)
        x = -0.0003713 + 1 * jax.random.normal(jax.random.fold_in(_gk, 1), (50000, 128), jnp.float32)
        src = jax.random.randint(jax.random.fold_in(_gk, 2), (25000,), 0, 50000, jnp.int32)
        dst = jnp.minimum((50000 * jax.random.uniform(jax.random.fold_in(_gk, 3), (25000,)) ** 2.0).astype(jnp.int32), 49999)
        _o = jnp.argsort(dst, stable=True)
        src = src[_o]
        dst = dst[_o]
        edge_type_200 = jax.random.randint(jax.random.fold_in(_gk, 14), (25000,), 0, 200, jnp.int32)
        return (x, src, dst, edge_type_200)
    x, src, dst, edge_type_200 = _rec_inputs()

    def _L0_gnn_setup():
        import jax, jax.numpy as jnp
        import numpy as np
        N_NODES = 100000
        N_EDGES = 10000
        N_RELS = 200
        D = 128
        RRELU_SLOPE = (1.0 / 8.0 + 1.0 / 3.0) / 2.0

        def rrelu(x):
            return jnp.where(x >= 0, x, x * RRELU_SLOPE)

        def _layer(h, e_h, src, dst, iso_mask, norm, W_r, W_sl, W_el):
            self_msg = jnp.where(iso_mask[:, None], h @ W_el, h @ W_sl)
            msg = (e_h + h[src]) @ W_r
            agg = jax.ops.segment_sum(msg, dst, num_segments=h.shape[0])
            return rrelu(agg * norm + self_msg)
        key = jax.random.key(seed)
        ks = jax.random.split(key, 12)
        inp = {'ent_embed': jax.random.normal(ks[0], (N_NODES, D), dtype=jnp.float32), 'rel_embed': jax.random.normal(ks[1], (N_RELS, D), dtype=jnp.float32), 'norm': jax.random.uniform(ks[2], (N_NODES, 1), dtype=jnp.float32), 'src': jax.random.randint(ks[3], (N_EDGES,), 0, N_NODES), 'dst': jax.random.randint(ks[4], (N_EDGES,), 0, N_NODES), 'rel_id': jax.random.randint(ks[5], (N_EDGES,), 0, N_RELS)}
        scale = 1.0 / np.sqrt(D)
        for i, name in enumerate(['W_r1', 'W_sl1', 'W_el1', 'W_r2', 'W_sl2', 'W_el2']):
            inp[name] = jax.random.uniform(ks[6 + i], (D, D), dtype=jnp.float32, minval=-scale, maxval=scale)
        return inp
    _L0_gnn_all = _L0_gnn_setup()
    _L0_gnn_in = {k: v for k, v in _L0_gnn_all.items() if k in ('rel_embed', 'W_r1', 'W_sl1', 'W_el1', 'W_r2', 'W_sl2', 'W_el2')}
    del _L0_gnn_all

    def _L1_gnn_setup():
        import jax, jax.numpy as jnp
        import numpy as np
        N = 50000
        E = 12500
        HID = 128
        NH = 8
        HD = 16
        FFN = 512
        EPS = 1e-05

        def _layer_norm(x, g, b):
            m = jnp.mean(x, axis=-1, keepdims=True)
            v = jnp.mean((x - m) ** 2, axis=-1, keepdims=True)
            return (x - m) * jax.lax.rsqrt(v + EPS) * g + b

        def _gnn_layer(x, edge_index, Wq, bq, Wk, bk, Wv, bv, Wo, bo, g1, b1, g2, b2, W1, bf1, W2, bf2):
            n = x.shape[0]
            residual = x
            h = _layer_norm(x, g1, b1)
            q = (h @ Wq + bq).reshape(n, NH, HD)
            k = (h @ Wk + bk).reshape(n, NH, HD)
            v = (h @ Wv + bv).reshape(n, NH, HD)
            src, dst = (edge_index[0], edge_index[1])
            deg = jax.ops.segment_sum(jnp.ones(src.shape, x.dtype), dst, num_segments=n)
            loops = jnp.arange(n, dtype=src.dtype)
            s_all = jnp.concatenate([src, loops])
            d_all = jnp.concatenate([dst, loops])
            e = jnp.sum(q[d_all] * k[s_all], axis=-1) / np.sqrt(HD).astype(np.float32)
            m = jax.lax.stop_gradient(jax.ops.segment_max(e, d_all, num_segments=n))
            p = jnp.exp(e - m[d_all])
            z = jax.ops.segment_sum(p, d_all, num_segments=n)
            alpha = p / z[d_all]
            agg = jax.ops.segment_sum(alpha[:, :, None] * v[s_all], d_all, num_segments=n)
            agg = jnp.where(deg[:, None, None] > 0, agg, jnp.zeros_like(agg))
            att = agg.reshape(n, NH * HD) @ Wo + bo
            x = residual + att
            residual = x
            h = _layer_norm(x, g2, b2)
            ffn = jax.nn.gelu(h @ W1 + bf1, approximate=False) @ W2 + bf2
            return residual + ffn
        key = jax.random.key(seed)
        ks = jax.random.split(key, 12)
        s = 0.02
        d = {}
        d['x'] = jax.random.normal(ks[0], (N, HID), jnp.float32)
        d['edge_index'] = jax.random.randint(ks[1], (2, E), 0, N, dtype=jnp.int32)
        d['Wq'] = jax.random.normal(ks[2], (HID, NH * HD), jnp.float32) * s
        d['bq'] = jnp.zeros((NH * HD,), jnp.float32)
        d['Wk'] = jax.random.normal(ks[3], (HID, NH * HD), jnp.float32) * s
        d['bk'] = jnp.zeros((NH * HD,), jnp.float32)
        d['Wv'] = jax.random.normal(ks[4], (HID, NH * HD), jnp.float32) * s
        d['bv'] = jnp.zeros((NH * HD,), jnp.float32)
        d['Wo'] = jax.random.normal(ks[5], (NH * HD, HID), jnp.float32) * s
        d['bo'] = jnp.zeros((HID,), jnp.float32)
        d['g1'] = jnp.ones((HID,), jnp.float32)
        d['b1'] = jnp.zeros((HID,), jnp.float32)
        d['g2'] = jnp.ones((HID,), jnp.float32)
        d['b2'] = jnp.zeros((HID,), jnp.float32)
        d['W1'] = jax.random.normal(ks[6], (HID, FFN), jnp.float32) * s
        d['bf1'] = jnp.zeros((FFN,), jnp.float32)
        d['W2'] = jax.random.normal(ks[7], (FFN, HID), jnp.float32) * s
        d['bf2'] = jnp.zeros((HID,), jnp.float32)
        return d
    _L1_gnn_all = _L1_gnn_setup()
    _L1_gnn_in = {k: v for k, v in _L1_gnn_all.items() if k in ('Wq', 'bq', 'Wk', 'bk', 'Wv', 'bv', 'Wo', 'bo', 'g1', 'b1', 'g2', 'b2', 'W1', 'bf1', 'W2', 'bf2')}
    del _L1_gnn_all
    return {'x': x, 'src': src, 'dst': dst, 'edge_type_200': edge_type_200, 'L0_gnn_rel_embed': _L0_gnn_in['rel_embed'], 'L0_gnn_W_r1': _L0_gnn_in['W_r1'], 'L0_gnn_W_sl1': _L0_gnn_in['W_sl1'], 'L0_gnn_W_el1': _L0_gnn_in['W_el1'], 'L0_gnn_W_r2': _L0_gnn_in['W_r2'], 'L0_gnn_W_sl2': _L0_gnn_in['W_sl2'], 'L0_gnn_W_el2': _L0_gnn_in['W_el2'], 'L1_gnn_Wq': _L1_gnn_in['Wq'], 'L1_gnn_bq': _L1_gnn_in['bq'], 'L1_gnn_Wk': _L1_gnn_in['Wk'], 'L1_gnn_bk': _L1_gnn_in['bk'], 'L1_gnn_Wv': _L1_gnn_in['Wv'], 'L1_gnn_bv': _L1_gnn_in['bv'], 'L1_gnn_Wo': _L1_gnn_in['Wo'], 'L1_gnn_bo': _L1_gnn_in['bo'], 'L1_gnn_g1': _L1_gnn_in['g1'], 'L1_gnn_b1': _L1_gnn_in['b1'], 'L1_gnn_g2': _L1_gnn_in['g2'], 'L1_gnn_b2': _L1_gnn_in['b2'], 'L1_gnn_W1': _L1_gnn_in['W1'], 'L1_gnn_bf1': _L1_gnn_in['bf1'], 'L1_gnn_W2': _L1_gnn_in['W2'], 'L1_gnn_bf2': _L1_gnn_in['bf2']}

def reference(x, src, dst, edge_type_200, L0_gnn_rel_embed, L0_gnn_W_r1, L0_gnn_W_sl1, L0_gnn_W_el1, L0_gnn_W_r2, L0_gnn_W_sl2, L0_gnn_W_el2, L1_gnn_Wq, L1_gnn_bq, L1_gnn_Wk, L1_gnn_bk, L1_gnn_Wv, L1_gnn_bv, L1_gnn_Wo, L1_gnn_bo, L1_gnn_g1, L1_gnn_b1, L1_gnn_g2, L1_gnn_b2, L1_gnn_W1, L1_gnn_bf1, L1_gnn_W2, L1_gnn_bf2):
    import jax
    import jax.numpy as jnp

    def _L0_gnn_ref(ent_embed, rel_embed, norm, src, dst, rel_id, W_r1, W_sl1, W_el1, W_r2, W_sl2, W_el2):
        import jax, jax.numpy as jnp
        import numpy as np
        N_NODES = 100000
        N_EDGES = 10000
        N_RELS = 200
        D = 128
        RRELU_SLOPE = (1.0 / 8.0 + 1.0 / 3.0) / 2.0

        def rrelu(x):
            return jnp.where(x >= 0, x, x * RRELU_SLOPE)

        def _layer(h, e_h, src, dst, iso_mask, norm, W_r, W_sl, W_el):
            self_msg = jnp.where(iso_mask[:, None], h @ W_el, h @ W_sl)
            msg = (e_h + h[src]) @ W_r
            agg = jax.ops.segment_sum(msg, dst, num_segments=h.shape[0])
            return rrelu(agg * norm + self_msg)
        num_nodes = ent_embed.shape[0]
        e_h = rel_embed[rel_id]
        in_deg = jax.ops.segment_sum(jnp.ones_like(dst), dst, num_segments=num_nodes)
        iso_mask = in_deg == 0
        h = ent_embed
        for W_r, W_sl, W_el in [(W_r1, W_sl1, W_el1), (W_r2, W_sl2, W_el2)]:
            h = _layer(h, e_h, src, dst, iso_mask, norm, W_r, W_sl, W_el)
        return h

    def _L1_gnn_ref(x, edge_index, Wq, bq, Wk, bk, Wv, bv, Wo, bo, g1, b1, g2, b2, W1, bf1, W2, bf2):
        import jax, jax.numpy as jnp
        import numpy as np
        N = 50000
        E = 12500
        HID = 128
        NH = 8
        HD = 16
        FFN = 512
        EPS = 1e-05

        def _layer_norm(x, g, b):
            m = jnp.mean(x, axis=-1, keepdims=True)
            v = jnp.mean((x - m) ** 2, axis=-1, keepdims=True)
            return (x - m) * jax.lax.rsqrt(v + EPS) * g + b

        def _gnn_layer(x, edge_index, Wq, bq, Wk, bk, Wv, bv, Wo, bo, g1, b1, g2, b2, W1, bf1, W2, bf2):
            n = x.shape[0]
            residual = x
            h = _layer_norm(x, g1, b1)
            q = (h @ Wq + bq).reshape(n, NH, HD)
            k = (h @ Wk + bk).reshape(n, NH, HD)
            v = (h @ Wv + bv).reshape(n, NH, HD)
            src, dst = (edge_index[0], edge_index[1])
            deg = jax.ops.segment_sum(jnp.ones(src.shape, x.dtype), dst, num_segments=n)
            loops = jnp.arange(n, dtype=src.dtype)
            s_all = jnp.concatenate([src, loops])
            d_all = jnp.concatenate([dst, loops])
            e = jnp.sum(q[d_all] * k[s_all], axis=-1) / np.sqrt(HD).astype(np.float32)
            m = jax.lax.stop_gradient(jax.ops.segment_max(e, d_all, num_segments=n))
            p = jnp.exp(e - m[d_all])
            z = jax.ops.segment_sum(p, d_all, num_segments=n)
            alpha = p / z[d_all]
            agg = jax.ops.segment_sum(alpha[:, :, None] * v[s_all], d_all, num_segments=n)
            agg = jnp.where(deg[:, None, None] > 0, agg, jnp.zeros_like(agg))
            att = agg.reshape(n, NH * HD) @ Wo + bo
            x = residual + att
            residual = x
            h = _layer_norm(x, g2, b2)
            ffn = jax.nn.gelu(h @ W1 + bf1, approximate=False) @ W2 + bf2
            return residual + ffn
        return _gnn_layer(x, edge_index, Wq, bq, Wk, bk, Wv, bv, Wo, bo, g1, b1, g2, b2, W1, bf1, W2, bf2)
    edge_index = jnp.stack([src, dst])
    deg = jnp.maximum(jax.ops.segment_sum(jnp.ones(dst.shape, jnp.float32), dst, num_segments=50000), 1.0)
    deg_isqrt = deg ** (-0.5)
    x = _layernorm(x + _L0_gnn_ref(x, L0_gnn_rel_embed, deg_isqrt[:, None], src, dst, edge_type_200, L0_gnn_W_r1, L0_gnn_W_sl1, L0_gnn_W_el1, L0_gnn_W_r2, L0_gnn_W_sl2, L0_gnn_W_el2), axis=-1)
    x = _layernorm(x + _L1_gnn_ref(x, edge_index, L1_gnn_Wq, L1_gnn_bq, L1_gnn_Wk, L1_gnn_bk, L1_gnn_Wv, L1_gnn_bv, L1_gnn_Wo, L1_gnn_bo, L1_gnn_g1, L1_gnn_b1, L1_gnn_g2, L1_gnn_b2, L1_gnn_W1, L1_gnn_bf1, L1_gnn_W2, L1_gnn_bf2), axis=-1)
    return x

_drawn_inputs = setup_inputs


def setup_inputs(seed=0):
    import zlib

    import numpy as np

    out = dict(_drawn_inputs(seed))
    spreads = {'L1_gnn_bq': (0.0, 0.8),
     'L1_gnn_bk': (0.0, 2.0),
     'L1_gnn_bv': (0.0, 0.8),
     'L1_gnn_bo': (0.0, 0.1),
     'L1_gnn_g1': (1.0, 0.6),
     'L1_gnn_b1': (0.0, 0.8),
     'L1_gnn_g2': (1.0, 0.6),
     'L1_gnn_b2': (0.0, 2.0),
     'L1_gnn_bf1': (0.0, 0.686),
     'L1_gnn_bf2': (0.0, 0.1)}
    factors = {'L1_gnn_Wq': 8.0, 'L1_gnn_Wk': 8.0, 'L1_gnn_Wv': 5.316, 'L1_gnn_Wo': 4.556}
    for name, (base, spread) in spreads.items():
        noise = np.random.default_rng([zlib.crc32(name.encode()), seed]).standard_normal(out[name].shape)
        drawn = base * np.exp(spread * noise) if base else spread * noise
        out[name] = jnp.asarray(drawn.astype(out[name].dtype))
    for name, factor in factors.items():
        out[name] = (out[name] * factor).astype(out[name].dtype)
    return out
```

```python
from contextlib import ExitStack

import concourse.bass as bass
from concourse import mybir

F32 = mybir.dt.float32
I32 = mybir.dt.int32
ALU = mybir.AluOpType
ACT = mybir.ActivationFunctionType
AX_X = mybir.AxisListType.X

P = 128
D = 128
HEADS, HD = 8, 16
FFN = 512
FCH = FFN // P
EPS = 1e-5
SLOPE = (1.0 / 8.0 + 1.0 / 3.0) / 2.0
LOW = 1e30
SKIP = 60000

UN = 8
GT = 4
GROUP = GT * P


class Turn:

    def __init__(self, n, k, b, total, unroll):
        self.n, self.k, self.b, self.total, self.unroll = n, k, b, total, unroll

    def ago(self, lag):
        n = self.n - lag
        if isinstance(n, int) and not 0 <= n < self.total:
            return None
        k = self.k - lag
        return Turn(n, k % self.unroll, self.b + k // self.unroll, self.total, self.unroll)


def over_tiles(eng, total, unroll, lag, step, peeled=1):
    assert lag <= peeled * unroll
    for n in range(peeled * unroll):
        step(Turn(n, n % unroll, n // unroll, total, unroll))
    with eng.Fori(peeled, total // unroll) as b:
        for k in range(unroll):
            step(Turn(b * unroll + k, k, b, total, unroll))
    for n in range(total // unroll * unroll, total + lag):
        step(Turn(n, n % unroll, n // unroll, total, unroll))


class DmaSems(list):

    def __init__(self, sems):
        super().__init__(sems)
        self.before = 0

    def after(self, dmas):
        return self.before + 16 * dmas

    def passed(self, dmas):
        self.before += 16 * dmas


def wait(eng, sem, value):
    if not isinstance(value, int) or value > 0:
        eng.wait_ge(sem, value)


def col(t, j):
    return t[:, bass.ds(j, 1)]


def per_head(t, j):
    return t[:, :, bass.ds(j, 1)].to_broadcast([P, HEADS, HD])


def heads(ap):
    return ap.rearrange("p (h d) -> p h d", h=HEADS)


def gnn_program(nc, x, src, dst, edge_type_200, L0_gnn_rel_embed, L0_gnn_W_r1, L0_gnn_W_sl1, L0_gnn_W_el1,
                L0_gnn_W_r2, L0_gnn_W_sl2, L0_gnn_W_el2, L1_gnn_Wq, L1_gnn_bq, L1_gnn_Wk, L1_gnn_bk,
                L1_gnn_Wv, L1_gnn_bv, L1_gnn_Wo, L1_gnn_bo, L1_gnn_g1, L1_gnn_b1, L1_gnn_g2, L1_gnn_b2,
                L1_gnn_W1, L1_gnn_bf1, L1_gnn_W2, L1_gnn_bf2, out):
    N = x.shape[0]
    E = src.shape[0]
    COLS = 200
    EP = E // COLS
    assert EP * COLS == E and COLS % UN == 0
    ROWS = COLS * P
    RELS = L0_gnn_rel_embed.shape[0]
    NG = -(-N // GROUP)

    def group_rows(n):
        return n * GROUP if not isinstance(n, int) else min(n * GROUP, N - GROUP)

    h1_table = nc.dram_tensor("h1_table", [N, D], F32).ap()
    x1_table = nc.dram_tensor("x1_table", [N, D], F32).ap()
    x2_table = nc.dram_tensor("x2_table", [N, D], F32).ap()
    tile_hx = nc.dram_tensor("tile_hx", [ROWS, 2 * D], F32).ap()
    tile_x1 = nc.dram_tensor("tile_x1", [ROWS, D], F32).ap()
    tile_xv = nc.dram_tensor("tile_xv", [ROWS, 2 * D], F32).ap()
    open_max = nc.dram_tensor("open_max", [2 * P, HEADS], F32).ap()

    root = ExitStack()
    with root:
        uses = {}

        def named(name):
            uses[name] = uses.get(name, 0) + 1
            return f"{name}_{uses[name]}"

        def sb(name, shape, dt=F32, ctx=root):
            return ctx.enter_context(nc.sbuf_tensor(named(name), shape, dt))

        def ps(name, ctx):
            return ctx.enter_context(nc.psum_tensor(named(name), [P, 512], F32))

        in_use = []

        def sem(name, ctx):
            in_use.append(ctx.enter_context(nc.semaphore(named(name))))
            return in_use[-1]

        def program(ctx):
            def clear():
                numbers = sorted(s.num for s in in_use)
                start = numbers[0]
                for n, after_n in zip(numbers, numbers[1:] + [None]):
                    if after_n != n + 1:
                        nc.sync.sem_clear(range(start, n + 1))
                        start = after_n
                nc.all_engine_barrier()
                in_use.clear()

            ctx.callback(clear)
            return ctx.enter_context(nc.Block())

        def sems(name, n, ctx):
            return [sem(f"{name}{k}", ctx) for k in range(n)]

        gathered, gathered_dst, scattered = (DmaSems([sem(f"{name}{k}", root) for k in range(UN)])
                                             for name in ("gathered", "gathered_dst", "scattered"))
        border_gathered, border_scattered = (DmaSems([sem(name, root)]) for name in ("border_gathered", "border_scattered"))
        passed = {engine: sem(f"passed_{engine}", root) for engine in ("sync", "gpsimd", "vector")}
        in_use.clear()

        def gate(eng):
            eng.sem_inc(passed[{nc.sync: "sync", nc.gpsimd: "gpsimd", nc.vector: "vector"}[eng]], 1)

        ident = sb("ident", [P, P])
        ones = sb("ones", [P, COLS])
        eps = sb("eps", [P, 1])
        minus_half = sb("minus_half", [P, GT])
        rel_ids = sb("rel_ids", [P, 2 * P])
        rel = sb("rel", [P, 2, D])
        w_r = [sb(f"w_r{l}", [D, D]) for l in range(2)]
        w_sl = [sb(f"w_sl{l}", [D, D]) for l in range(2)]
        w_el = [sb(f"w_el{l}", [D, D]) for l in range(2)]
        w_vqk = sb("w_vqk", [D, 3 * D])
        bias_vqk = sb("bias_vqk", [P, 4 * D])
        w_o = sb("w_o", [D, D])
        bo_rows = sb("bo_rows", [P, D])
        att_bias = sb("att_bias", [P, D])
        w_1 = sb("w_1", [D, FFN])
        w_2 = sb("w_2", [P, FCH, D])
        bf1 = sb("bf1", [P, FCH])
        bf2 = sb("bf2", [P, 1])
        type_f = sb("type_f", [P, COLS])
        same_prev = sb("same_prev", [P, COLS])
        same_next = sb("same_next", [P, COLS])
        is_end = sb("is_end", [P, COLS])
        keep_x = sb("keep_x", [P, COLS])
        cap_end = sb("cap_end", [P, COLS])
        cap_start = sb("cap_start", [P, COLS])
        in_first = sb("in_first", [P, COLS])
        in_last = sb("in_last", [P, COLS])
        norm = sb("norm", [P, COLS])
        idx = sb("idx", [P, 4, COLS], I32)
        SRC, DST, AT_END, AT_START = range(4)
        border = sb("border", [P, 6], I32)
        WR_FIRST, WR_LAST, RD_FIRST, RD_LAST, POS_FIRST, POS_LAST = range(6)
        after = sb("after", [P, P])
        before = sb("before", [P, P])
        border_norm = sb("border_norm", [P, 1])
        first_last = sb("first_last", [P, 2 * P])
        dst_fl = sb("dst_fl", [P, 2])
        open_acc = sb("open_acc", [P, 2, D])
        caught = sb("caught", [P, D])
        border_h = sb("border_h", [P, D])
        border_x = sb("border_x", [P, D])

        def prepare():
            with ExitStack() as c:
                src_i = sb("src_i", [P, COLS], I32, c)
                dst_i = sb("dst_i", [P, COLS], I32, c)
                type_i = sb("type_i", [P, COLS], I32, c)
                side_i = sb("side_i", [P, 2], I32, c)
                dst_f = sb("dst_f", [P, COLS], F32, c)
                side = sb("side", [P, 2], F32, c)
                first = sb("first", [P, COLS], F32, c)
                last = sb("last", [P, COLS], F32, c)
                real = sb("real", [P, COLS], F32, c)
                is_start = sb("is_start", [P, COLS], F32, c)
                goes = sb("goes", [P, 2], F32, c)
                tmp = sb("tmp", [P, COLS], F32, c)
                count = sb("count", [P, COLS], F32, c)
                pos = sb("pos", [P, COLS], F32, c)
                caught_count = sb("caught_count", [P, 1], F32, c)
                has = sb("has", [P, 2], F32, c)
                has_pos = sb("has_pos", [P, 2], F32, c)
                bcol = sb("bcol", [P, 1], F32, c)
                diag = sb("diag", [P, 2, P], F32, c)
                up = sb("up", [P, P], F32, c)
                down = sb("down", [P, P], F32, c)
                gcol = sb("gcol", [P, 4], F32, c)
                b1_cols = sb("b1_cols", [P, P], F32, c)
                vecs = sb("vecs", [P, 3, D], F32, c)
                bvT = sb("bvT", [P, P], F32, c)
                p_row = ps("p_row", c)
                p_cnt = ps("p_cnt", c)
                p_vqk = ps("p_vqk", c)
                p_bvT = ps("p_bvT", c)
                p_att = ps("p_att", c)
                p_bf1 = ps("p_bf1", c)
                filled = sem("filled", c)
                loaded = sem("loaded", c)
                edges_in = sem("edges_in", c)
                consts = sem("consts", c)
                dve_done = sem("dve_done", c)
                rows_ready = sem("rows_ready", c)
                diag_ready = sem("diag_ready", c)
                masks_ready = sem("masks_ready", c)
                cnt_ready = sem("cnt_ready", c)
                cnt_summed = sem("cnt_summed", c)
                root_ready = sem("root_ready", c)
                vecs_ready = sem("vecs_ready", c)
                b1_ready = sem("b1_ready", c)
                bv_ready = sem("bv_ready", c)
                bvT_ready = sem("bvT_ready", c)
                bvT_copied = sem("bvT_copied", c)
                att_ready = sem("att_ready", c)
                bf1_ready = sem("bf1_ready", c)
                block = program(c)

                @block.gpsimd
                def _(e):
                    e.memset(src_i[:], 0).then_inc(filled, 1)
                    e.memset(dst_i[:], N).then_inc(filled, 1)
                    e.memset(type_i[:], 0).then_inc(filled, 1)
                    e.memset(side_i[:], N).then_inc(filled, 1)
                    e.memset(rel[:], 0.0).then_inc(filled, 1)
                    e.memset(ident[:], 0.0).then_inc(consts, 1)
                    e.memset(up[:], 1.0).then_inc(consts, 1)
                    e.memset(down[:], 1.0).then_inc(consts, 1)
                    e.memset(ones[:], 1.0).then_inc(consts, 1)
                    e.memset(eps[:], EPS).then_inc(consts, 1)
                    e.memset(minus_half[:], -0.5).then_inc(consts, 1)
                    e.iota(rel_ids[:], pattern=[[1, 2 * P]], base=0, channel_multiplier=0,
                           allow_small_or_imprecise_dtypes=True).then_inc(consts, 1)
                    e.iota(pos[:], pattern=[[P, COLS]], base=0, channel_multiplier=1,
                           allow_small_or_imprecise_dtypes=True).then_inc(consts, 1)
                    e.wait_ge(consts, 3)
                    e.affine_select(out=ident[:], in_=ident[:], compare_op=ALU.not_equal, fill=1.0, base=0,
                                    pattern=[[-1, P]], channel_multiplier=1).then_inc(consts, 1)
                    e.affine_select(out=up[:], in_=up[:], compare_op=ALU.is_gt, fill=0.0, base=0,
                                    pattern=[[1, P]], channel_multiplier=-1).then_inc(consts, 1)
                    e.affine_select(out=down[:], in_=down[:], compare_op=ALU.is_gt, fill=0.0, base=0,
                                    pattern=[[-1, P]], channel_multiplier=1).then_inc(consts, 1)

                @block.sync
                def _(e):
                    e.wait_ge(filled, 5)
                    e.dma_start(dst_i[0:EP, :], dst.rearrange("(p j) -> p j", j=COLS)).then_inc(edges_in, 16)
                    e.dma_start(src_i[0:EP, :], src.rearrange("(p j) -> p j", j=COLS)).then_inc(edges_in, 16)
                    e.dma_start(type_i[0:EP, :], edge_type_200.rearrange("(p j) -> p j", j=COLS)).then_inc(edges_in, 16)
                    by_part = dst.rearrange("(p j) -> p j", j=COLS)
                    e.dma_start(side_i[1:EP, 0:1], by_part[0:EP - 1, COLS - 1:COLS], allow_slow_non_contiguous=True).then_inc(edges_in, 16)
                    e.dma_start(side_i[0:EP - 1, 1:2], by_part[1:EP, 0:1], allow_slow_non_contiguous=True).then_inc(edges_in, 16)
                    e.dma_start(rel[:, 0, :], L0_gnn_rel_embed[0:P, :]).then_inc(edges_in, 16)
                    e.dma_start(rel[0:RELS - P, 1, :], L0_gnn_rel_embed[P:RELS, :]).then_inc(edges_in, 16)
                    for t, a in ((w_r[0], L0_gnn_W_r1), (w_sl[0], L0_gnn_W_sl1), (w_el[0], L0_gnn_W_el1),
                                 (w_r[1], L0_gnn_W_r2), (w_sl[1], L0_gnn_W_sl2), (w_el[1], L0_gnn_W_el2)):
                        e.dma_start(t[:], a).then_inc(edges_in, 16)
                    e.wait_ge(edges_in, 13 * 16)

                @block.scalar
                def _(e):
                    for n, a in enumerate((L1_gnn_Wv, L1_gnn_Wq, L1_gnn_Wk)):
                        e.dma_start(w_vqk[:, n * D:(n + 1) * D], a).then_inc(loaded, 16)
                    for n, a in enumerate((L1_gnn_g1, L1_gnn_b1, L1_gnn_g2, L1_gnn_b2)):
                        e.dma_start(gcol[:, n:n + 1], a.rearrange("(p a) -> p a", a=1)).then_inc(loaded, 16)
                    e.dma_start(bf2[:], L1_gnn_bf2.rearrange("(p a) -> p a", a=1)).then_inc(loaded, 16)
                    for n, a in enumerate((L1_gnn_bv, L1_gnn_bq, L1_gnn_bk)):
                        e.dma_start(vecs[:, n, :], a.partition_broadcast(P)).then_inc(loaded, 16)
                    e.dma_start(bo_rows[:], L1_gnn_bo.partition_broadcast(P)).then_inc(loaded, 16)
                    e.dma_start(w_o[:], L1_gnn_Wo).then_inc(loaded, 16)
                    e.dma_start(w_1[:], L1_gnn_W1).then_inc(loaded, 16)
                    e.dma_start(w_2[:], L1_gnn_W2.rearrange("(c p) n -> p c n", p=P)).then_inc(loaded, 16)
                    e.dma_start(bf1[:], L1_gnn_bf1.rearrange("(c p) -> p c", p=P), allow_slow_non_contiguous=True).then_inc(loaded, 16)
                    e.wait_ge(cnt_summed, 2)
                    e.activation(norm[:], count[:], ACT.Sqrt).then_inc(root_ready, 1)
                    e.activation(border_norm[:], caught_count[:], ACT.Sqrt).then_inc(root_ready, 1)

                @block.tensor
                def _(e):
                    e.wait_ge(consts, 11)
                    e.wait_ge(diag_ready, 2)
                    for s in range(2):
                        mm = e.matmul(p_row[:, s * P:(s + 1) * P], ones[:, 0:P], diag[:, s, :], start=True, stop=True)
                    mm.then_inc(rows_ready, 1)
                    e.wait_ge(masks_ready, 1)
                    e.matmul(p_cnt[:, 0:1], after[:], count[:, COLS - 1:COLS], start=True, stop=True).then_inc(cnt_ready, 1)
                    e.wait_ge(b1_ready, 1)
                    e.matmul(p_vqk[:, 0:3 * D], b1_cols[:], w_vqk[:], start=True, stop=True).then_inc(vecs_ready, 1)
                    for ch in range(FCH):
                        mm = e.matmul(p_bf1[:, ch:ch + 1], w_1[:, ch * P:(ch + 1) * P], gcol[:, 3:4], start=True, stop=True)
                    mm.then_inc(bf1_ready, 1)
                    e.wait_ge(bv_ready, 1)
                    e.transpose(p_bvT[:, 0:P], bias_vqk[:, 0:D], ident[:]).then_inc(bvT_ready, 1)
                    e.wait_ge(bvT_copied, 1)
                    e.matmul(p_att[:, 0:D], bvT[:], w_o[:], start=True, stop=True).then_inc(att_ready, 1)

                @block.vector
                def _(e):
                    made = [0]

                    def chain(ins):
                        made[0] += 1
                        ins.then_inc(dve_done, 1)
                        e.wait_ge(dve_done, made[0])

                    e.wait_ge(edges_in, 13 * 16)
                    e.wait_ge(consts, 11)
                    e.tensor_copy(idx[:, SRC, :], src_i[:])
                    e.tensor_copy(type_f[:], type_i[:])
                    e.tensor_copy(side[:], side_i[:])
                    chain(e.tensor_copy(dst_f[:], dst_i[:]))
                    e.tensor_copy(dst_fl[:, 0:1], dst_f[:, 0:1])
                    chain(e.tensor_copy(dst_fl[:, 1:2], dst_f[:, COLS - 1:COLS]))
                    for s in range(2):
                        e.tensor_scalar(diag[:, s, :], ident[:], dst_fl[:, s:s + 1], None, ALU.mult).then_inc(diag_ready, 1)
                    e.memset(same_prev[:, 0:1], 0.0)
                    e.memset(same_next[:, COLS - 1:COLS], 0.0)
                    e.tensor_tensor(same_prev[:, 1:COLS], dst_f[:, 1:COLS], dst_f[:, 0:COLS - 1], ALU.is_equal)
                    e.tensor_tensor(same_next[:, 0:COLS - 1], dst_f[:, 1:COLS], dst_f[:, 0:COLS - 1], ALU.is_equal)
                    e.tensor_tensor(goes[:], side[:], dst_fl[:], ALU.is_equal)
                    e.tensor_scalar(first[:], dst_f[:], dst_fl[:, 0:1], None, ALU.is_equal)
                    e.tensor_scalar(last[:], dst_f[:], dst_fl[:, 1:2], None, ALU.is_equal)
                    e.tensor_scalar(idx[:, DST, :], dst_f[:], float(N - 1), None, ALU.min)
                    chain(e.tensor_scalar(real[:], dst_f[:], float(N), None, ALU.is_lt))
                    e.tensor_copy(keep_x[:], same_next[:])
                    e.tensor_scalar(in_first[:], first[:], -1.0, LOW, ALU.add, ALU.mult)
                    e.tensor_scalar(in_last[:], last[:], -1.0, LOW, ALU.add, ALU.mult)
                    e.tensor_scalar(is_end[:], same_next[:], -1.0, 1.0, ALU.mult, ALU.add)
                    chain(e.tensor_scalar(is_start[:], same_prev[:], -1.0, 1.0, ALU.mult, ALU.add))
                    e.tensor_copy(keep_x[:, COLS - 1:COLS], goes[:, 1:2])
                    e.tensor_scalar(is_end[:, COLS - 1:COLS], goes[:, 1:2], -1.0, 1.0, ALU.mult, ALU.add)
                    chain(e.tensor_scalar(is_start[:, 0:1], goes[:, 0:1], -1.0, 1.0, ALU.mult, ALU.add))
                    for n, (at, seg, cap, write) in enumerate(((is_end, first, cap_end, AT_END),
                                                               (is_start, last, cap_start, AT_START))):
                        chain(e.tensor_tensor(tmp[:], at[:], real[:], ALU.mult))
                        chain(e.scalar_tensor_tensor(out=cap[:], in0=seg[:], scalar=goes[:, n:n + 1], in1=tmp[:],
                                                     op0=ALU.mult, op1=ALU.mult))
                        chain(e.tensor_tensor(tmp[:], tmp[:], cap[:], ALU.subtract))
                        chain(e.scalar_tensor_tensor(out=tmp[:], in0=dst_f[:], scalar=-float(SKIP), in1=tmp[:],
                                                     op0=ALU.add, op1=ALU.mult))
                        chain(e.tensor_scalar(idx[:, write, :], tmp[:], float(SKIP), None, ALU.add))
                        chain(e.tensor_reduce(has[:, n:n + 1], cap[:], AX_X, ALU.add))
                        chain(e.tensor_tensor(tmp[:], cap[:], pos[:], ALU.mult))
                        chain(e.tensor_reduce(has_pos[:, n:n + 1], tmp[:], AX_X, ALU.add))
                        chain(e.scalar_tensor_tensor(out=bcol[:], in0=dst_fl[:, n:n + 1], scalar=-float(SKIP),
                                                     in1=has[:, n:n + 1], op0=ALU.add, op1=ALU.mult))
                        chain(e.tensor_scalar(border[:, WR_FIRST + n:WR_FIRST + n + 1], bcol[:], float(SKIP), None, ALU.add))
                        chain(e.tensor_scalar(border[:, RD_FIRST + n:RD_FIRST + n + 1], dst_fl[:, n:n + 1], float(N - 1), None, ALU.min))
                    chain(e.scalar_tensor_tensor(out=bcol[:], in0=has[:, 0:1], scalar=-float(SKIP), in1=has_pos[:, 0:1],
                                                 op0=ALU.mult, op1=ALU.add))
                    chain(e.tensor_scalar(border[:, POS_FIRST:POS_FIRST + 1], bcol[:], float(SKIP), None, ALU.add))
                    chain(e.tensor_copy(border[:, POS_LAST:POS_LAST + 1], has_pos[:, 1:2]))
                    chain(e.tensor_tensor_scan(count[:], same_prev[:], ones[:], 0.0, ALU.mult, ALU.add))
                    e.wait_ge(rows_ready, 1)
                    chain(e.tensor_copy(first_last[:], p_row[:, 0:2 * P]))
                    chain(e.scalar_tensor_tensor(out=after[:], in0=first_last[:, 0:P], scalar=dst_fl[:, 1:2], in1=up[:],
                                                 op0=ALU.is_equal, op1=ALU.mult))
                    e.scalar_tensor_tensor(out=before[:], in0=first_last[:, P:2 * P], scalar=dst_fl[:, 0:1], in1=down[:],
                                           op0=ALU.is_equal, op1=ALU.mult).then_inc(masks_ready, 1)
                    chain(e.tensor_tensor(tmp[:], cap_end[:], count[:], ALU.mult))
                    chain(e.tensor_reduce(caught_count[:], tmp[:], AX_X, ALU.add))
                    e.wait_ge(cnt_ready, 1)
                    e.tensor_scalar(count[:], count[:], 1.0, None, ALU.max).then_inc(cnt_summed, 1)
                    chain(e.tensor_tensor(caught_count[:], caught_count[:], p_cnt[:, 0:1], ALU.add))
                    e.tensor_scalar(caught_count[:], caught_count[:], 1.0, None, ALU.max).then_inc(cnt_summed, 1)
                    e.wait_ge(root_ready, 2)
                    e.reciprocal(norm[:], norm[:])
                    chain(e.reciprocal(border_norm[:], border_norm[:]))
                    e.wait_ge(loaded, 16 * 16)
                    e.tensor_scalar(b1_cols[:], ones[:, 0:P], gcol[:, 1:2], None, ALU.mult).then_inc(b1_ready, 1)
                    e.wait_ge(vecs_ready, 1)
                    e.tensor_tensor(bias_vqk[:, 0:3 * D], p_vqk[:, 0:3 * D], vecs[:].rearrange("p a d -> p (a d)"), ALU.add)\
                        .then_inc(bv_ready, 1)
                    e.wait_ge(bf1_ready, 1)
                    e.tensor_tensor(bias_vqk[:, 3 * D:4 * D], p_vqk[:, 2 * D:3 * D], vecs[:, 2, :], ALU.add)
                    e.tensor_tensor(bf1[:], bf1[:], p_bf1[:, 0:FCH], ALU.add)
                    e.tensor_scalar(w_vqk[:], w_vqk[:], gcol[:, 0:1], None, ALU.mult)
                    e.tensor_scalar(w_1[:], w_1[:], gcol[:, 2:3], None, ALU.mult)
                    e.wait_ge(bvT_ready, 1)
                    e.tensor_copy(bvT[:], p_bvT[:, 0:P]).then_inc(bvT_copied, 1)
                    e.wait_ge(att_ready, 1)
                    e.tensor_tensor(att_bias[:], p_att[:, 0:D], bo_rows[:], ALU.add)

        def dense():
            with ExitStack() as c:
                XSL = 4
                x_in = sb("x_in", [P, XSL, GROUP], F32, c)
                xT = sb("xT", [P, 2, GROUP], F32, c)
                low1 = sb("low1", [P, 2, GROUP], F32, c)
                low2 = sb("low2", [P, 2, GROUP], F32, c)
                h1T = sb("h1T", [P, 2, GROUP], F32, c)
                h2T = sb("h2T", [P, 2, GROUP], F32, c)
                h1_rows = sb("h1_rows", [P, XSL, GROUP], F32, c)
                xs_rows = sb("xs_rows", [P, XSL, GROUP], F32, c)
                x1_rows = sb("x1_rows", [P, XSL, GROUP], F32, c)
                x2_rows = sb("x2_rows", [P, XSL, GROUP], F32, c)
                stats = sb("stats", [P, 2, GT, 6], F32, c)
                mv = sb("mv", [P, XSL, GT, 2], F32, c)
                var = sb("var", [P, XSL, GT], F32, c)
                rstd = sb("rstd", [P, XSL, GT], F32, c)
                p_x = [ps(f"p_x{s}", c) for s in range(2)]
                p_1, p_2 = ps("p_1", c), ps("p_2", c)
                p_r1 = [ps(f"p_r1{s}", c) for s in range(2)]
                p_r2 = [ps(f"p_r2{s}", c) for s in range(2)]
                x_loaded = sems("x_loaded", XSL, c)
                h1_stored = sems("h1_stored", XSL, c)
                x1_stored = sems("x1_stored", XSL, c)
                x2_stored = sems("x2_stored", XSL, c)
                x_turned = sem("x_turned", c)
                xT_ready = sem("xT_ready", c)
                prod1, prod2 = sem("prod1", c), sem("prod2", c)
                low1_ready, low2_ready = sem("low1_ready", c), sem("low2_ready", c)
                h1T_ready, h2T_ready = sem("h1T_ready", c), sem("h2T_ready", c)
                h1_turned, h2_turned = sem("h1_turned", c), sem("h2_turned", c)
                h1_ready = sem("h1_ready", c)
                sum_ready = sem("sum_ready", c)
                stats_ready = sem("stats_ready", c)
                mv_ready = sem("mv_ready", c)
                var_ready = sem("var_ready", c)
                rstd_ready = sem("rstd_ready", c)
                x1_ready = sem("x1_ready", c)
                x2_ready = sem("x2_ready", c)
                block = program(c)
                LAG = 5

                def rows(table, t):
                    return table[bass.ds(group_rows(t.n), GROUP), :].rearrange("(p a) d -> p (a d)", a=GT)

                @block.sync
                def _(e):
                    def step(t):
                        if (g := t.ago(0)):
                            wait(e, sum_ready, g.n - XSL + 1)
                            gate(e)
                            e.dma_start(x_in[:, g.k, :], rows(x, g)).then_inc(x_loaded[g.k], 16)
                        if (g := t.ago(2)):
                            if isinstance(g.n, int) and g.n == NG - 1:
                                e.wait_ge(h1_stored[(g.n - 1) % XSL], 16 * ((g.n - 1) // XSL + 1))
                            gate(e)
                            e.wait_ge(h1_ready, g.n + 1)
                            gate(e)
                            e.dma_start(rows(h1_table, g), h1_rows[:, g.k, :]).then_inc(h1_stored[g.k], 16)
                        if (g := t.ago(4)):
                            if isinstance(g.n, int) and g.n == NG - 1:
                                e.wait_ge(x1_stored[(g.n - 1) % XSL], 16 * ((g.n - 1) // XSL + 1))
                                gate(e)
                                e.wait_ge(x2_stored[(g.n - 1) % XSL], 16 * ((g.n - 1) // XSL + 1))
                            gate(e)
                            e.wait_ge(x1_ready, g.n + 1)
                            gate(e)
                            e.dma_start(rows(x1_table, g), x1_rows[:, g.k, :]).then_inc(x1_stored[g.k], 16)
                            e.wait_ge(x2_ready, g.n + 1)
                            gate(e)
                            e.dma_start(rows(x2_table, g), x2_rows[:, g.k, :]).then_inc(x2_stored[g.k], 16)

                    over_tiles(e, NG, XSL, LAG, step, peeled=2)
                    for k in range(XSL):
                        for s in (h1_stored, x1_stored, x2_stored):
                            e.wait_ge(s[k], 16 * len(range(k, NG, XSL)))

                @block.tensor
                def _(e):
                    def step(t):
                        if (g := t.ago(0)):
                            s = g.k % 2
                            e.wait_ge(x_loaded[g.k], 16 * (g.b + 1))
                            wait(e, xT_ready, g.n - 1)
                            for a in range(GT):
                                mm = e.transpose(p_x[s][:, a * P:(a + 1) * P], x_in[:, g.k, a * D:(a + 1) * D], ident[:])
                            mm.then_inc(x_turned, 1)
                        if (g := t.ago(1)):
                            s = g.k % 2
                            e.wait_ge(xT_ready, g.n + 1)
                            wait(e, h1T_ready, g.n)
                            e.matmul(p_1[:], w_el[0][:], xT[:, s, :], start=True, stop=True).then_inc(prod1, 1)
                        if (g := t.ago(2)):
                            s = g.k % 2
                            e.wait_ge(h1T_ready, g.n + 1)
                            wait(e, h2T_ready, g.n)
                            e.matmul(p_2[:], w_el[1][:], h1T[:, s, :], start=True, stop=True).then_inc(prod2, 1)
                            wait(e, h1_ready, g.n - 1)
                            for a in range(GT):
                                mm = e.transpose(p_r1[s][:, a * D:(a + 1) * D], h1T[:, s, a * P:(a + 1) * P], ident[:])
                            mm.then_inc(h1_turned, 1)
                        if (g := t.ago(3)):
                            s = g.k % 2
                            e.wait_ge(h2T_ready, g.n + 1)
                            wait(e, sum_ready, g.n - 1)
                            for a in range(GT):
                                mm = e.transpose(p_r2[s][:, a * D:(a + 1) * D], h2T[:, s, a * P:(a + 1) * P], ident[:])
                            mm.then_inc(h2_turned, 1)

                    over_tiles(e, NG, XSL, LAG, step, peeled=2)

                @block.scalar
                def _(e):
                    def step(t):
                        if (g := t.ago(0)):
                            s = g.k % 2
                            e.wait_ge(x_turned, g.n + 1)
                            wait(e, prod1, g.n - 1)
                            e.activation(xT[:, s, :], p_x[s][:], ACT.Copy).then_inc(xT_ready, 1)
                        if (g := t.ago(1)):
                            s = g.k % 2
                            e.wait_ge(prod1, g.n + 1)
                            wait(e, h1T_ready, g.n - 1)
                            e.activation(low1[:, s, :], p_1[:], ACT.Copy, scale=SLOPE).then_inc(low1_ready, 1)
                        if (g := t.ago(2)):
                            s = g.k % 2
                            e.wait_ge(prod2, g.n + 1)
                            wait(e, h2T_ready, g.n - 1)
                            e.activation(low2[:, s, :], p_2[:], ACT.Copy, scale=SLOPE).then_inc(low2_ready, 1)
                            e.wait_ge(h1_turned, g.n + 1)
                            wait(e, h1_stored[g.k], 16 * g.b)
                            e.activation(h1_rows[:, g.k, :], p_r1[s][:], ACT.Copy).then_inc(h1_ready, 1)

                    over_tiles(e, NG, XSL, LAG, step, peeled=2)

                @block.vector
                def _(e):
                    def step(t):
                        if (g := t.ago(1)):
                            s = g.k % 2
                            e.wait_ge(low1_ready, g.n + 1)
                            wait(e, prod2, g.n - 1)
                            wait(e, h1_turned, g.n - 1)
                            e.tensor_tensor(h1T[:, s, :], low1[:, s, :], p_1[:], ALU.max).then_inc(h1T_ready, 1)
                        if (g := t.ago(2)):
                            s = g.k % 2
                            e.wait_ge(low2_ready, g.n + 1)
                            wait(e, h2_turned, g.n - 1)
                            e.tensor_tensor(h2T[:, s, :], low2[:, s, :], p_2[:], ALU.max).then_inc(h2T_ready, 1)
                        if (g := t.ago(3)):
                            s = g.k % 2
                            e.wait_ge(h2_turned, g.n + 1)
                            e.tensor_tensor(xs_rows[:, g.k, :], p_r2[s][:], x_in[:, g.k, :], ALU.add).then_inc(sum_ready, 1)
                            e.wait_ge(sum_ready, g.n + 1)
                            for a in range(GT):
                                st = e.bn_stats(stats[:, s, a, :], xs_rows[:, g.k, a * D:(a + 1) * D])
                            st.then_inc(stats_ready, 1)
                            e.wait_ge(stats_ready, g.n + 1)
                            gate(e)
                            for a in range(GT):
                                st = e.bn_aggr(mv[:, g.k, a, :], stats[:, s, a, :])
                            st.then_inc(mv_ready, 1)
                        if (g := t.ago(4)):
                            e.wait_ge(rstd_ready, g.n + 1)
                            wait(e, x1_stored[g.k], 16 * g.b)
                            for a in range(GT):
                                st = e.tensor_scalar(x1_rows[:, g.k, a * D:(a + 1) * D], xs_rows[:, g.k, a * D:(a + 1) * D],
                                                     mv[:, g.k, a, 0:1], rstd[:, g.k, a:a + 1], ALU.subtract, ALU.mult)
                            st.then_inc(x1_ready, 1)

                    over_tiles(e, NG, XSL, LAG, step, peeled=2)

                @block.gpsimd
                def _(e):
                    def step(t):
                        if (g := t.ago(3)):
                            e.wait_ge(mv_ready, g.n + 1)
                            gate(e)
                            e.tensor_scalar(var[:, g.k, :], mv[:, g.k, :, 1], EPS, None, ALU.add).then_inc(var_ready, 1)
                            e.wait_ge(var_ready, g.n + 1)
                            gate(e)
                            e.tensor_tensor(rstd[:, g.k, :], var[:, g.k, :], minus_half[:], ALU.pow).then_inc(rstd_ready, 1)
                        if (g := t.ago(4)):
                            e.wait_ge(x1_ready, g.n + 1)
                            wait(e, x2_stored[g.k], 16 * g.b)
                            gate(e)
                            e.tensor_tensor(x2_rows[:, g.k, :].rearrange("p (a d) -> p a d", a=GT),
                                            x1_rows[:, g.k, :].rearrange("p (a d) -> p a d", a=GT),
                                            bo_rows[:].unsqueeze(1).to_broadcast([P, GT, D]), ALU.add).then_inc(x2_ready, 1)

                    over_tiles(e, NG, XSL, LAG, step, peeled=2)

        def layer(l):
            table = (x, h1_table)[l]
            target = (h1_table, x1_table)[l]
            with ExitStack() as c:
                x_src = sb("x_src", [P, UN, D], F32, c)
                hx = sb("hx", [P, UN, 2 * D], F32, c)
                x1_out = sb("x1_out", [P, UN, D], F32, c)
                use = sb("use", [P, UN, 3], I32, c)
                hot = sb("hot", [P, 2, 2 * P], F32, c)
                hotT = sb("hotT", [P, 2, 2 * P], F32, c)
                acc_n = sb("acc_n", [P, 2, D], F32, c)
                turned = sb("turned", [P, 2, 2 * P], F32, c)
                low = sb("low", [P, 2, D], F32, c)
                h_out = sb("h_out", [P, 2, D], F32, c)
                xs = sb("xs", [P, 2, D], F32, c)
                stats = sb("stats", [P, 2, 6], F32, c)
                mv = sb("mv", [P, 2, 2], F32, c)
                std = sb("std", [P, 2], F32, c)
                rstd = sb("rstd", [P, 2], F32, c)
                p_hot = [ps(f"p_hot{s}", c) for s in range(2)]
                p_msg = [ps(f"p_msg{s}", c) for s in range(2)]
                p_turn = [ps(f"p_turn{s}", c) for s in range(2)]
                p_h = [ps(f"p_h{s}", c) for s in range(2)]
                src_in = gathered
                dst_in = DmaSems(sems("dst_in", UN, c)) if l else gathered_dst
                stored = sems("stored", UN, c)
                use_ready = sem("use_ready", c)
                hot_ready = sem("hot_ready", c)
                hot_turned = sem("hot_turned", c)
                hotT_ready = sem("hotT_ready", c)
                msg_ready = sem("msg_ready", c)
                cleared = sem("cleared", c)
                acc_ready = sem("acc_ready", c)
                catch_done = sem("catch_done", c)
                acc_n_ready = sem("acc_n_ready", c)
                both_turned = sem("both_turned", c)
                turned_ready = sem("turned_ready", c)
                h_prod = sem("h_prod", c)
                low_ready = sem("low_ready", c)
                h_ready = sem("h_ready", c)
                sum_ready = sem("sum_ready", c)
                stats_ready = sem("stats_ready", c)
                mv_ready = sem("mv_ready", c)
                std_ready = sem("std_ready", c)
                rstd_ready = sem("rstd_ready", c)
                row_ready = sem("row_ready", c) if l else h_ready
                block = program(c)
                OUT_LAG = 4 + l
                LAG = OUT_LAG + 1

                def tile_rows(t, table):
                    return table[bass.ds(t.n * P, P), :]

                @block.gpsimd
                def _(e):
                    def step(t):
                        if (g := t.ago(0)):
                            wait(e, scattered[g.k], scattered.after(g.b))
                            if l == 0:
                                wait(e, stored[g.k], 16 * g.b)
                            wait(e, msg_ready, g.n - UN + 1)
                            gate(e)
                            e.tensor_copy(use[:, g.k, :].unsqueeze(2), idx[:, 0:3, bass.ds(g.n, 1)]).then_inc(use_ready, 1)
                            e.wait_ge(use_ready, g.n + 1)
                            gate(e)
                            e.indirect_dma_start(out=x_src[:, g.k, :], out_offset=None, in_=table,
                                                 in_offset=bass.IndirectOffsetOnAxis(ap=use[:, g.k, SRC:SRC + 1], axis=0))\
                                .then_inc(src_in[g.k], 16)
                            if l == 0:
                                e.indirect_dma_start(out=hx[:, g.k, D:2 * D], out_offset=None, in_=x,
                                                     in_offset=bass.IndirectOffsetOnAxis(ap=use[:, g.k, DST:DST + 1], axis=0))\
                                    .then_inc(dst_in[g.k], 16)
                        if (g := t.ago(OUT_LAG)):
                            e.wait_ge(row_ready, g.n + 1)
                            gate(e)
                            rows_out = hx[:, g.k, 0:D] if l == 0 else x1_out[:, g.k, :]
                            e.indirect_dma_start(out=target, in_=rows_out, in_offset=None,
                                                 out_offset=bass.IndirectOffsetOnAxis(ap=use[:, g.k, AT_END:AT_END + 1], axis=0),
                                                 bounds_check=N - 1, oob_is_err=False).then_inc(scattered[g.k], 16)

                    over_tiles(e, COLS, UN, LAG, step)
                    for k in range(UN):
                        e.wait_ge(scattered[k], scattered.after(COLS // UN))

                @block.sync
                def _(e):
                    def step(t):
                        if l == 1 and (g := t.ago(0)):
                            wait(e, row_ready, g.n - UN + 1)
                            gate(e)
                            wait(e, stored[g.k], 16 * g.b)
                            gate(e)
                            wait(e, scattered[g.k], scattered.after(g.b))
                            gate(e)
                            e.dma_start(hx[:, g.k, :], tile_rows(g, tile_hx)).then_inc(dst_in[g.k], 16)
                        if (g := t.ago(OUT_LAG)):
                            e.wait_ge(row_ready, g.n + 1)
                            if l == 0:
                                e.dma_start(tile_rows(g, tile_hx), hx[:, g.k, :]).then_inc(stored[g.k], 16)
                            else:
                                e.dma_start(tile_rows(g, tile_x1), x1_out[:, g.k, :]).then_inc(stored[g.k], 16)

                    over_tiles(e, COLS, UN, LAG, step)
                    for k in range(UN):
                        e.wait_ge(stored[k], 16 * (COLS // UN))

                @block.tensor
                def _(e):
                    def step(t):
                        if (g := t.ago(0)):
                            s = g.k % 2
                            e.wait_ge(hot_ready, g.n + 1)
                            wait(e, hotT_ready, g.n - 1)
                            for a in range(2):
                                mm = e.transpose(p_hot[s][:, a * P:(a + 1) * P], hot[:, s, a * P:(a + 1) * P], ident[:])
                            mm.then_inc(hot_turned, 1)
                        if (g := t.ago(1)):
                            s = g.k % 2
                            e.wait_ge(hotT_ready, g.n + 1)
                            e.wait_ge(src_in[g.k], src_in.after(g.b + 1))
                            wait(e, acc_ready, g.n - 1)
                            e.matmul(p_msg[s][:, 0:D], hotT[:, s, 0:P], rel[:, 0, :], start=True, stop=False)
                            e.matmul(p_msg[s][:, 0:D], hotT[:, s, P:2 * P], rel[:, 1, :], start=False, stop=False)
                            e.matmul(p_msg[s][:, 0:D], ident[:], x_src[:, g.k, :], start=False, stop=True).then_inc(msg_ready, 1)
                        if (g := t.ago(2)):
                            s = g.k % 2
                            e.wait_ge(acc_n_ready, g.n + 1)
                            e.wait_ge(dst_in[g.k], dst_in.after(g.b + 1))
                            wait(e, turned_ready, g.n - 1)
                            own = hx[:, g.k, D:2 * D] if l == 0 else hx[:, g.k, 0:D]
                            e.transpose(p_turn[s][:, 0:P], acc_n[:, s, :], ident[:])
                            e.transpose(p_turn[s][:, P:2 * P], own, ident[:]).then_inc(both_turned, 1)
                        if (g := t.ago(3)):
                            s = g.k % 2
                            e.wait_ge(turned_ready, g.n + 1)
                            wait(e, h_ready, g.n - 1)
                            e.matmul(p_h[s][:, 0:D], turned[:, s, 0:P], w_r[l][:], start=True, stop=False)
                            e.matmul(p_h[s][:, 0:D], turned[:, s, P:2 * P], w_sl[l][:], start=False, stop=True).then_inc(h_prod, 1)

                    over_tiles(e, COLS, UN, LAG, step)

                @block.scalar
                def _(e):
                    def step(t):
                        if (g := t.ago(0)):
                            s = g.k % 2
                            e.wait_ge(hot_turned, g.n + 1)
                            wait(e, msg_ready, g.n - 1)
                            e.activation(hotT[:, s, :], p_hot[s][:, 0:2 * P], ACT.Copy).then_inc(hotT_ready, 1)
                        if (g := t.ago(2)):
                            s = g.k % 2
                            e.wait_ge(both_turned, g.n + 1)
                            wait(e, h_prod, g.n - 1)
                            e.activation(turned[:, s, :], p_turn[s][:, 0:2 * P], ACT.Copy).then_inc(turned_ready, 1)
                        if (g := t.ago(1)):
                            s = g.k % 2
                            e.wait_ge(acc_ready, g.n + 1)
                            wait(e, both_turned, g.n - 1)
                            e.activation(acc_n[:, s, :], open_acc[:, s, :], ACT.Copy, scale=col(norm, g.n)).then_inc(acc_n_ready, 1)
                        if (g := t.ago(3)):
                            s = g.k % 2
                            e.wait_ge(h_prod, g.n + 1)
                            wait(e, h_ready, g.n - 1)
                            e.activation(low[:, s, :], p_h[s][:, 0:D], ACT.Copy, scale=SLOPE).then_inc(low_ready, 1)
                        if l == 1 and (g := t.ago(4)):
                            s = g.k % 2
                            e.wait_ge(mv_ready, g.n + 1)
                            wait(e, rstd_ready, g.n - 1)
                            e.activation(std[:, s:s + 1], mv[:, s, 1:2], ACT.Sqrt, bias=eps[:]).then_inc(std_ready, 1)

                    over_tiles(e, COLS, UN, LAG, step)

                @block.vector
                def _(e):
                    e.memset(open_acc[:], 0.0).then_inc(cleared, 1)
                    e.memset(caught[:], 0.0).then_inc(cleared, 1)

                    def types(g):
                        s = g.k % 2
                        wait(e, hot_turned, g.n - 1)
                        gate(e)
                        e.tensor_scalar(hot[:, s, :], rel_ids[:], col(type_f, g.n), None, ALU.is_equal).then_inc(hot_ready, 1)

                    def step(t):
                        if (g := t.ago(0)):
                            types(g)
                        if (g := t.ago(1)):
                            s = g.k % 2
                            e.wait_ge(msg_ready, g.n + 1)
                            if isinstance(g.n, int) and g.n == 0:
                                e.wait_ge(cleared, 2)
                            wait(e, acc_n_ready, g.n - 1)
                            wait(e, acc_ready, g.n)
                            wait(e, catch_done, g.n - 1)
                            gate(e)
                            e.scalar_tensor_tensor(out=open_acc[:, s, :], in0=open_acc[:, 1 - s, :], scalar=col(same_prev, g.n),
                                                   in1=p_msg[s][:, 0:D], op0=ALU.mult, op1=ALU.add).then_inc(acc_ready, 1)
                        if (g := t.ago(3)):
                            s = g.k % 2
                            e.wait_ge(low_ready, g.n + 1)
                            if l == 0:
                                e.tensor_tensor(hx[:, g.k, 0:D], low[:, s, :], p_h[s][:, 0:D], ALU.max).then_inc(h_ready, 1)
                            else:
                                e.tensor_tensor(h_out[:, s, :], low[:, s, :], p_h[s][:, 0:D], ALU.max).then_inc(h_ready, 1)
                                e.wait_ge(h_ready, g.n + 1)
                                e.tensor_tensor(xs[:, s, :], h_out[:, s, :], hx[:, g.k, D:2 * D], ALU.add).then_inc(sum_ready, 1)
                        if (g := t.ago(1)):
                            e.wait_ge(acc_ready, g.n + 1)
                            wait(e, catch_done, g.n)
                            gate(e)
                            e.scalar_tensor_tensor(out=caught[:], in0=open_acc[:, g.k % 2, :], scalar=col(cap_end, g.n),
                                                   in1=caught[:], op0=ALU.mult, op1=ALU.add).then_inc(catch_done, 1)
                        if l == 1 and (g := t.ago(3)):
                            s = g.k % 2
                            e.wait_ge(sum_ready, g.n + 1)
                            e.bn_stats(stats[:, s, :], xs[:, s, :]).then_inc(stats_ready, 1)
                        if l == 1 and (g := t.ago(4)):
                            s = g.k % 2
                            e.wait_ge(std_ready, g.n + 1)
                            e.reciprocal(rstd[:, s:s + 1], std[:, s:s + 1]).then_inc(rstd_ready, 1)
                        if l == 1 and (g := t.ago(3)):
                            s = g.k % 2
                            e.wait_ge(stats_ready, g.n + 1)
                            gate(e)
                            e.bn_aggr(mv[:, s, :], stats[:, s, :]).then_inc(mv_ready, 1)
                        if l == 1 and (g := t.ago(4)):
                            s = g.k % 2
                            e.wait_ge(rstd_ready, g.n + 1)
                            e.tensor_scalar(x1_out[:, g.k, :], xs[:, s, :], mv[:, s, 0:1], rstd[:, s:s + 1],
                                            ALU.subtract, ALU.mult).then_inc(row_ready, 1)

                    over_tiles(e, COLS, UN, LAG, step)

            gathered.passed(COLS // UN)
            scattered.passed(COLS // UN)
            if l == 0:
                gathered_dst.passed(COLS // UN)

        def layer_border(l):
            with ExitStack() as c:
                acc = sb("acc", [P, D], F32, c)
                acc_n = sb("acc_n", [P, D], F32, c)
                turned = sb("turned", [P, 2 * P], F32, c)
                low = sb("low", [P, D], F32, c)
                h = sb("h", [P, D], F32, c)
                xs = sb("xs", [P, D], F32, c)
                x1 = sb("x1", [P, D], F32, c)
                stats = sb("stats", [P, 6], F32, c)
                mv = sb("mv", [P, 2], F32, c)
                std = sb("std", [P, 1], F32, c)
                rstd = sb("rstd", [P, 1], F32, c)
                p_open = ps("p_open", c)
                p_turn = ps("p_turn", c)
                p_h = ps("p_h", c)
                x_in = border_gathered
                open_ready = sem("open_ready", c)
                acc_ready = sem("acc_ready", c)
                both_turned = sem("both_turned", c)
                turned_ready = sem("turned_ready", c)
                h_prod = sem("h_prod", c)
                low_ready = sem("low_ready", c)
                std_ready = sem("std_ready", c)
                mv_ready = sem("mv_ready", c)
                dve_done = sem("dve_done", c)
                row_ready = sem("row_ready", c)
                block = program(c)

                @block.gpsimd
                def _(e):
                    if l == 0:
                        e.indirect_dma_start(out=border_x[:], out_offset=None, in_=x,
                                             in_offset=bass.IndirectOffsetOnAxis(ap=border[:, RD_FIRST:RD_FIRST + 1], axis=0))\
                            .then_inc(x_in[0], 16)
                    e.wait_ge(row_ready, 1)
                    where = bass.IndirectOffsetOnAxis(ap=border[:, WR_FIRST:WR_FIRST + 1], axis=0)
                    if l == 0:
                        e.indirect_dma_start(out=h1_table, in_=border_h[:], in_offset=None, out_offset=where,
                                             bounds_check=N - 1, oob_is_err=False).then_inc(border_scattered[0], 16)
                        e.wait_ge(border_scattered[0], border_scattered.after(1))
                    else:
                        e.indirect_dma_start(out=x1_table, in_=x1[:], in_offset=None, out_offset=where,
                                             bounds_check=N - 1, oob_is_err=False).then_inc(border_scattered[0], 16)
                        e.indirect_dma_start(out=tile_x1, in_=x1[:], in_offset=None,
                                             out_offset=bass.IndirectOffsetOnAxis(ap=border[:, POS_FIRST:POS_FIRST + 1], axis=0),
                                             bounds_check=ROWS - 1, oob_is_err=False).then_inc(border_scattered[0], 16)
                        e.wait_ge(border_scattered[0], border_scattered.after(2))

                @block.tensor
                def _(e):
                    e.matmul(p_open[:, 0:D], after[:], open_acc[:, (COLS - 1) % 2, :], start=True, stop=True).then_inc(open_ready, 1)
                    e.wait_ge(acc_ready, 1)
                    if l == 0:
                        e.wait_ge(x_in[0], x_in.after(1))
                    e.transpose(p_turn[:, 0:P], acc_n[:], ident[:])
                    e.transpose(p_turn[:, P:2 * P], (border_x, border_h)[l][:], ident[:]).then_inc(both_turned, 1)
                    e.wait_ge(turned_ready, 1)
                    e.matmul(p_h[:, 0:D], turned[:, 0:P], w_r[l][:], start=True, stop=False)
                    e.matmul(p_h[:, 0:D], turned[:, P:2 * P], w_sl[l][:], start=False, stop=True).then_inc(h_prod, 1)

                @block.scalar
                def _(e):
                    e.wait_ge(both_turned, 1)
                    e.activation(turned[:], p_turn[:, 0:2 * P], ACT.Copy).then_inc(turned_ready, 1)
                    e.wait_ge(h_prod, 1)
                    e.activation(low[:], p_h[:, 0:D], ACT.Copy, scale=SLOPE).then_inc(low_ready, 1)
                    if l == 1:
                        e.wait_ge(mv_ready, 1)
                        e.activation(std[:], mv[:, 1:2], ACT.Sqrt, bias=eps[:]).then_inc(std_ready, 1)

                @block.vector
                def _(e):
                    e.wait_ge(open_ready, 1)
                    e.tensor_tensor(acc[:], p_open[:, 0:D], caught[:], ALU.add).then_inc(dve_done, 1)
                    e.wait_ge(dve_done, 1)
                    e.tensor_scalar(acc_n[:], acc[:], border_norm[:], None, ALU.mult).then_inc(acc_ready, 1)
                    e.wait_ge(low_ready, 1)
                    if l == 0:
                        e.tensor_tensor(border_h[:], low[:], p_h[:, 0:D], ALU.max).then_inc(row_ready, 1)
                        return
                    e.tensor_tensor(h[:], low[:], p_h[:, 0:D], ALU.max).then_inc(dve_done, 1)
                    e.wait_ge(dve_done, 2)
                    e.tensor_tensor(xs[:], h[:], border_x[:], ALU.add).then_inc(dve_done, 1)
                    e.wait_ge(dve_done, 3)
                    e.bn_stats(stats[:], xs[:]).then_inc(dve_done, 1)
                    e.wait_ge(dve_done, 4)
                    e.bn_aggr(mv[:], stats[:]).then_inc(mv_ready, 1)
                    e.wait_ge(std_ready, 1)
                    e.reciprocal(rstd[:], std[:]).then_inc(dve_done, 1)
                    e.wait_ge(dve_done, 5)
                    e.tensor_scalar(x1[:], xs[:], mv[:, 0:1], rstd[:], ALU.subtract, ALU.mult).then_inc(row_ready, 1)

            if l == 0:
                border_gathered.passed(1)
            border_scattered.passed(1 + l)

        def attention(values, logits):
            with ExitStack() as c:
                x_src = sb("x_src", [P, UN, D], F32, c)
                x_end = sb("x_end", [P, UN, D], F32, c)
                at_end = sb("at_end", [P, 2, D], F32, c)
                dst_row = sb("dst_row", [P, UN, 5, D], F32, c)
                X, V, Q, KD, KS = range(5)
                use = sb("use", [P, UN, 1], I32, c)
                x_open = sb("x_open", [P, D], F32, c)
                stats = sb("stats", [P, 2, 2, 6], F32, c)
                mv = sb("mv", [P, 2, 2, 2], F32, c)
                std = sb("std", [P, 2, 2], F32, c)
                rstd = sb("rstd", [P, 2, 2], F32, c)
                shift = sb("shift", [P, 2, 2], F32, c)
                normed = sb("normed", [P, 2, 2, D], F32, c)
                turned = sb("turned", [P, 2, 2 * P], F32, c)
                prod = sb("prod", [P, 2, 2, D], F32, c)
                p_turn = [ps(f"p_turn{s}", c) for s in range(2)]
                p_qk = [ps(f"p_qk{s}", c) for s in range(2)]
                p_v = [ps(f"p_v{s}", c) for s in range(2)]
                open_in = border_gathered
                src_in = gathered
                end_in = sems("end_in", UN, c)
                stored = sems("stored", UN, c)
                use_ready = sem("use_ready", c)
                at_end_ready = sem("at_end_ready", c)
                x_ready = sem("x_ready", c)
                stats_ready = sem("stats_ready", c)
                mv_ready = sem("mv_ready", c)
                std_ready = sem("std_ready", c)
                rstd_ready = sem("rstd_ready", c)
                shift_ready = sem("shift_ready", c)
                normed_ready = sem("normed_ready", c)
                both_turned = sem("both_turned", c)
                turned_ready = sem("turned_ready", c)
                qkv_ready = sem("qkv_ready", c)
                qk_out = sem("qk_out", c)
                v_out = sem("v_out", c)
                prod_ready = sem("prod_ready", c)
                logit_ready = sem("logit_ready", c)
                block = program(c)
                LAG = 5

                def j(g):
                    return COLS - 1 - g.n

                @block.gpsimd
                def _(e):
                    e.indirect_dma_start(out=x_open[:], out_offset=None, in_=x1_table,
                                         in_offset=bass.IndirectOffsetOnAxis(ap=border[:, RD_LAST:RD_LAST + 1], axis=0))\
                        .then_inc(open_in[0], 16)

                    def step(t):
                        if (g := t.ago(0)):
                            wait(e, normed_ready, g.n - UN + 1)
                            gate(e)
                            e.tensor_copy(use[:, g.k, :], col(idx[:, SRC, :], j(g))).then_inc(use_ready, 1)
                            e.wait_ge(use_ready, g.n + 1)
                            gate(e)
                            e.indirect_dma_start(out=x_src[:, g.k, :], out_offset=None, in_=x1_table,
                                                 in_offset=bass.IndirectOffsetOnAxis(ap=use[:, g.k, 0:1], axis=0))\
                                .then_inc(src_in[g.k], 16)

                    over_tiles(e, COLS, UN, LAG, step)

                @block.sync
                def _(e):
                    def step(t):
                        if (g := t.ago(0)):
                            wait(e, at_end_ready, g.n - UN + 1)
                            gate(e)
                            wait(e, stored[g.k], 16 * g.b)
                            gate(e)
                            wait(e, logit_ready, g.n - UN + 1)
                            gate(e)
                            e.dma_start(x_end[:, g.k, :], tile_x1[bass.ds(j(g) * P, P), :]).then_inc(end_in[g.k], 16)
                        if (g := t.ago(4)):
                            e.wait_ge(v_out, g.n + 1)
                            gate(e)
                            e.wait_ge(x_ready, g.n + 1)
                            gate(e)
                            e.dma_start(tile_xv[bass.ds(j(g) * P, P), :],
                                        dst_row[:, g.k, X:V + 1, :].rearrange("p a d -> p (a d)")).then_inc(stored[g.k], 16)

                    over_tiles(e, COLS, UN, LAG, step)
                    for k in range(UN):
                        e.wait_ge(stored[k], 16 * (COLS // UN))

                @block.tensor
                def _(e):
                    def step(t):
                        if (g := t.ago(2)):
                            s = g.k % 2
                            e.wait_ge(normed_ready, g.n + 1)
                            wait(e, turned_ready, g.n - 1)
                            for a in range(2):
                                mm = e.transpose(p_turn[s][:, a * P:(a + 1) * P], normed[:, s, a, :], ident[:])
                            mm.then_inc(both_turned, 1)
                        if (g := t.ago(3)):
                            s = g.k % 2
                            e.wait_ge(turned_ready, g.n + 1)
                            wait(e, qk_out, g.n - 1)
                            wait(e, v_out, g.n - 1)
                            dst_T, src_T = turned[:, s, 0:P], turned[:, s, P:2 * P]
                            e.matmul(p_qk[s][:, 0:2 * D], dst_T, w_vqk[:, D:3 * D], start=True, stop=True)
                            e.matmul(p_v[s][:, 0:D], dst_T, w_vqk[:, 0:D], start=True, stop=True)
                            e.matmul(p_qk[s][:, 2 * D:3 * D], src_T, w_vqk[:, 2 * D:3 * D], start=True, stop=True)
                            e.matmul(p_v[s][:, D:2 * D], src_T, w_vqk[:, 0:D], start=True, stop=True).then_inc(qkv_ready, 1)

                    over_tiles(e, COLS, UN, LAG, step)

                @block.scalar
                def _(e):
                    def step(t):
                        if (g := t.ago(0)):
                            s = g.k % 2
                            e.wait_ge(end_in[g.k], 16 * (g.b + 1))
                            wait(e, x_ready, g.n - 1)
                            e.activation(at_end[:, s, :], x_end[:, g.k, :], ACT.Copy, scale=col(is_end, j(g)))\
                                .then_inc(at_end_ready, 1)
                        if (g := t.ago(2)):
                            s = g.k % 2
                            e.wait_ge(both_turned, g.n + 1)
                            wait(e, qkv_ready, g.n - 1)
                            e.activation(turned[:, s, :], p_turn[s][:, 0:2 * P], ACT.Copy).then_inc(turned_ready, 1)
                        if (g := t.ago(1)):
                            s = g.k % 2
                            e.wait_ge(mv_ready, g.n + 1)
                            wait(e, rstd_ready, g.n - 1)
                            e.activation(std[:, s, :], mv[:, s, :, 1], ACT.Sqrt, bias=eps[:]).then_inc(std_ready, 1)
                        if (g := t.ago(3)):
                            s = g.k % 2
                            e.wait_ge(qkv_ready, g.n + 1)
                            e.activation(dst_row[:, g.k, V, :], p_v[s][:, 0:D], ACT.Copy)
                            e.activation(values[:, bass.ds(j(g), 1), :].rearrange("p a d -> p (a d)"), p_v[s][:, D:2 * D], ACT.Copy)\
                                .then_inc(v_out, 1)
                        if (g := t.ago(1)):
                            s = g.k % 2
                            e.wait_ge(shift_ready, g.n + 1)
                            wait(e, both_turned, g.n - 1)
                            for a, row in ((0, dst_row[:, g.k, X, :]), (1, x_src[:, g.k, :])):
                                ins = e.activation(normed[:, s, a, :], row, ACT.Identity, scale=rstd[:, s, a:a + 1],
                                                   bias=shift[:, s, a:a + 1])
                            ins.then_inc(normed_ready, 1)

                    over_tiles(e, COLS, UN, LAG, step)

                @block.vector
                def _(e):
                    def step(t):
                        if (g := t.ago(0)):
                            s = g.k % 2
                            e.wait_ge(at_end_ready, g.n + 1)
                            if isinstance(g.n, int) and g.n == 0:
                                e.wait_ge(open_in[0], open_in.after(1))
                                before_row = x_open[:]
                            else:
                                before_row = dst_row[:, (g.k - 1) % UN, X, :]
                            wait(e, x_ready, g.n)
                            gate(e)
                            e.scalar_tensor_tensor(out=dst_row[:, g.k, X, :], in0=before_row, scalar=col(keep_x, j(g)),
                                                   in1=at_end[:, s, :], op0=ALU.mult, op1=ALU.add).then_inc(x_ready, 1)
                        if (g := t.ago(3)):
                            s = g.k % 2
                            e.wait_ge(qkv_ready, g.n + 1)
                            e.tensor_tensor(dst_row[:, g.k, Q:KS + 1, :].rearrange("p a d -> p (a d)"),
                                            p_qk[s][:, 0:3 * D], bias_vqk[:, D:4 * D], ALU.add).then_inc(qk_out, 1)
                        if (g := t.ago(0)):
                            s = g.k % 2
                            e.wait_ge(x_ready, g.n + 1)
                            e.wait_ge(src_in[g.k], src_in.after(g.b + 1))
                            e.bn_stats(stats[:, s, 0, :], dst_row[:, g.k, X, :])
                            e.bn_stats(stats[:, s, 1, :], x_src[:, g.k, :]).then_inc(stats_ready, 1)
                        if (g := t.ago(3)):
                            s = g.k % 2
                            e.wait_ge(qk_out, g.n + 1)
                            e.tensor_tensor(prod[:, s, :, :], dst_row[:, g.k, KD:KS + 1, :],
                                            dst_row[:, g.k, Q:Q + 1, :].to_broadcast([P, 2, D]), ALU.mult).then_inc(prod_ready, 1)
                        if (g := t.ago(0)):
                            s = g.k % 2
                            e.wait_ge(stats_ready, g.n + 1)
                            wait(e, shift_ready, g.n - 1)
                            wait(e, std_ready, g.n - 1)
                            gate(e)
                            for a in range(2):
                                ins = e.bn_aggr(mv[:, s, a, :], stats[:, s, a, :])
                            ins.then_inc(mv_ready, 1)
                        if (g := t.ago(3)):
                            s = g.k % 2
                            e.wait_ge(prod_ready, g.n + 1)
                            gate(e)
                            e.tensor_reduce(logits[:, :, bass.ds(j(g), 1)].rearrange("p h a -> p (h a)"),
                                            prod[:, s, :, :].rearrange("p a (h d) -> p (a h) d", h=HEADS), AX_X, ALU.add)\
                                .then_inc(logit_ready, 1)
                        if (g := t.ago(1)):
                            s = g.k % 2
                            e.wait_ge(std_ready, g.n + 1)
                            wait(e, normed_ready, g.n - 1)
                            e.reciprocal(rstd[:, s, :], std[:, s, :]).then_inc(rstd_ready, 1)
                            e.wait_ge(rstd_ready, g.n + 1)
                            e.scalar_tensor_tensor(out=shift[:, s, :], in0=mv[:, s, :, 0], scalar=-1.0, in1=rstd[:, s, :],
                                                   op0=ALU.mult, op1=ALU.mult).then_inc(shift_ready, 1)

                    over_tiles(e, COLS, UN, LAG, step)

            gathered.passed(COLS // UN)
            border_gathered.passed(1)

        def softmax(logits, weight, z_inv, self_weight, border_z):
            SCALE = 1.0 / HD ** 0.5
            with ExitStack() as c:
                both = sb("both", [P, HEADS, COLS], F32, c)
                gap_prev = sb("gap_prev", [P, HEADS, COLS], F32, c)
                gap_next = sb("gap_next", [P, HEADS, COLS], F32, c)
                top = z_inv
                top_next = self_weight
                sides = sb("sides", [P, 2, HEADS], F32, c)
                all_sides = sb("all_sides", [P, 2 * P, HEADS], F32, c)
                miss = sb("miss", [P, 2, 2 * P], F32, c)
                cand = sb("cand", [P, HEADS, 2 * P], F32, c)
                top_side = sb("top_side", [P, 2, HEADS], F32, c)
                dve_done = sem("dve_done", c)
                sides_ready = sem("sides_ready", c)
                sides_out = sem("sides_out", c)
                sides_in = sem("sides_in", c)
                gaps_ready = sem("gaps_ready", c)
                exp_done = sem("exp_done", c)
                block = program(c)
                self_logit, edge_logit = logits[:, 0:HEADS, :], logits[:, HEADS:2 * HEADS, :]

                def flat(t):
                    return t[:].rearrange("p h j -> p (h j)")

                def over_heads(mask):
                    return mask[:].unsqueeze(1).to_broadcast([P, HEADS, COLS])

                @block.sync
                def _(e):
                    e.wait_ge(sides_ready, 1)
                    for s in range(2):
                        e.dma_start(open_max[s * P:(s + 1) * P, :], sides[:, s, :]).then_inc(sides_out, 16)
                    e.wait_ge(sides_out, 32)
                    e.dma_start(all_sides[:].rearrange("p q h -> p (q h)"),
                                open_max.rearrange("q h -> (q h)").partition_broadcast(P)).then_inc(sides_in, 16)

                @block.scalar
                def _(e):
                    e.wait_ge(gaps_ready, 1)
                    e.activation(flat(weight), flat(both), ACT.Exp, scale=SCALE).then_inc(exp_done, 1)
                    e.activation(flat(self_weight), flat(gap_prev), ACT.Exp, scale=SCALE).then_inc(exp_done, 1)

                @block.vector
                def _(e):
                    made = [0]

                    def chain(ins):
                        made[0] += 1
                        ins.then_inc(dve_done, 1)
                        e.wait_ge(dve_done, made[0])

                    e.tensor_scalar(gap_prev[:], over_heads(same_prev), -1.0, LOW, ALU.add, ALU.mult)
                    e.tensor_scalar(gap_next[:], over_heads(same_next), -1.0, LOW, ALU.add, ALU.mult)
                    chain(e.tensor_tensor(both[:], self_logit, edge_logit, ALU.max))
                    e.tensor_tensor_scan(flat(top), flat(gap_prev), flat(both), -LOW, ALU.add, ALU.max)
                    chain(e.tensor_tensor_scan(flat(top_next)[:, ::-1], flat(gap_next)[:, ::-1], flat(both)[:, ::-1], -LOW,
                                               ALU.add, ALU.max))
                    e.tensor_copy(sides[:, 0, :], top_next[:, :, 0])
                    e.tensor_copy(sides[:, 1, :], top[:, :, COLS - 1]).then_inc(sides_ready, 1)
                    e.wait_ge(sides_ready, 1)
                    chain(e.tensor_tensor(flat(top), flat(top), flat(top_next), ALU.max))
                    for s in range(2):
                        ins = e.tensor_scalar(miss[:, s, :], first_last[:], dst_fl[:, s:s + 1], None, ALU.is_equal)
                    chain(ins)
                    e.wait_ge(sides_in, 16)
                    for s in range(2):
                        chain(e.tensor_scalar(miss[:, s, :], miss[:, s, :], -1.0, LOW, ALU.add, ALU.mult))
                        chain(e.tensor_tensor(cand[:], all_sides[:].rearrange("p q h -> p h q"),
                                              miss[:, s, :].unsqueeze(1).to_broadcast([P, HEADS, 2 * P]), ALU.add))
                        chain(e.tensor_reduce(top_side[:, s, :], cand[:], AX_X, ALU.max))
                    for s, inside in enumerate((in_first, in_last)):
                        for h in range(HEADS):
                            ins = e.scalar_tensor_tensor(out=top[:, h, :], in0=inside[:], scalar=top_side[:, s, h:h + 1],
                                                         in1=top[:, h, :], op0=ALU.add, op1=ALU.max)
                        chain(ins)
                    e.tensor_tensor(both[:], edge_logit, top[:], ALU.subtract)
                    e.tensor_tensor(gap_prev[:], self_logit, top[:], ALU.subtract).then_inc(gaps_ready, 1)
                    chain(e.tensor_copy(gap_next[:], over_heads(same_next)))
                    e.wait_ge(exp_done, 2)
                    z = z_inv
                    chain(e.tensor_tensor_scan(flat(z)[:, ::-1], flat(gap_next)[:, ::-1], flat(weight)[:, ::-1], 0.0,
                                               ALU.mult, ALU.add))
                    chain(e.tensor_tensor(both[:], z[:], over_heads(cap_start), ALU.mult))
                    e.tensor_reduce(border_z[:, 0, :], both[:], AX_X, ALU.add)
                    e.tensor_copy(border_z[:, 1, :], z[:, :, 0])
                    chain(e.tensor_tensor(gap_prev[:], self_weight[:], over_heads(cap_start), ALU.mult))
                    e.tensor_reduce(border_z[:, 2, :], gap_prev[:], AX_X, ALU.add)
                    chain(e.tensor_tensor(flat(z), flat(z), flat(self_weight), ALU.add))
                    chain(e.tensor_scalar(flat(z), flat(z), 1e-30, None, ALU.max))
                    chain(e.reciprocal(flat(z_inv), flat(z)))
                    chain(e.tensor_tensor(flat(self_weight), flat(self_weight), flat(z_inv), ALU.mult))

        def weighted(values, weight, z_inv, self_weight):
            with ExitStack() as c:
                xv = sb("xv", [P, UN, 2 * D], F32, c)
                use = sb("use", [P, UN, 1], I32, c)
                x_bias = sb("x_bias", [P, UN, D], F32, c)
                own = sb("own", [P, 2, D], F32, c)
                wv = sb("wv", [P, 2, D], F32, c)
                scaled = sb("scaled", [P, 2, D], F32, c)
                attT = sb("attT", [P, 2, P], F32, c)
                x2_out = sb("x2_out", [P, UN, D], F32, c)
                p_sum = [ps(f"p_sum{s}", c) for s in range(2)]
                p_out = [ps(f"p_out{s}", c) for s in range(2)]
                xv_in = sems("xv_in", UN, c)
                use_ready = sem("use_ready", c)
                x_bias_ready = sem("x_bias_ready", c)
                own_ready = sem("own_ready", c)
                cleared = sem("cleared", c)
                wv_ready = sem("wv_ready", c)
                acc_ready = sem("acc_ready", c)
                catch_done = sem("catch_done", c)
                scaled_ready = sem("scaled_ready", c)
                sum_ready = sem("sum_ready", c)
                attT_ready = sem("attT_ready", c)
                prod_ready = sem("prod_ready", c)
                row_ready = sem("row_ready", c)
                block = program(c)
                LAG = 4

                def j(g):
                    return COLS - 1 - g.n

                @block.sync
                def _(e):
                    def step(t):
                        if (g := t.ago(0)):
                            wait(e, row_ready, g.n - UN + 1)
                            gate(e)
                            wait(e, scattered[g.k], scattered.after(g.b))
                            gate(e)
                            e.dma_start(xv[:, g.k, :], tile_xv[bass.ds(j(g) * P, P), :]).then_inc(xv_in[g.k], 16)

                    over_tiles(e, COLS, UN, LAG, step)

                @block.gpsimd
                def _(e):
                    def step(t):
                        if (g := t.ago(0)):
                            s = g.k % 2
                            e.wait_ge(xv_in[g.k], 16 * (g.b + 1))
                            gate(e)
                            e.tensor_copy(use[:, g.k, :], col(idx[:, AT_START, :], j(g))).then_inc(use_ready, 1)
                            wait(e, sum_ready, g.n - 1)
                            gate(e)
                            e.tensor_tensor(heads(own[:, s, :]), heads(xv[:, g.k, D:2 * D]), per_head(self_weight, j(g)), ALU.mult)\
                                .then_inc(own_ready, 1)
                            e.tensor_tensor(x_bias[:, g.k, :], xv[:, g.k, 0:D], att_bias[:], ALU.add).then_inc(x_bias_ready, 1)
                        if (g := t.ago(2)):
                            e.wait_ge(use_ready, g.n + 1)
                            e.wait_ge(row_ready, g.n + 1)
                            gate(e)
                            e.indirect_dma_start(out=x2_table, in_=x2_out[:, g.k, :], in_offset=None,
                                                 out_offset=bass.IndirectOffsetOnAxis(ap=use[:, g.k, 0:1], axis=0),
                                                 bounds_check=N - 1, oob_is_err=False).then_inc(scattered[g.k], 16)

                    over_tiles(e, COLS, UN, LAG, step)
                    for k in range(UN):
                        e.wait_ge(scattered[k], scattered.after(COLS // UN))

                @block.vector
                def _(e):
                    e.memset(open_acc[:], 0.0).then_inc(cleared, 1)
                    e.memset(caught[:], 0.0).then_inc(cleared, 1)

                    def step(t):
                        if (g := t.ago(0)):
                            s = g.k % 2
                            wait(e, acc_ready, g.n - 1)
                            gate(e)
                            e.tensor_tensor(heads(wv[:, s, :]), heads(values[:, bass.ds(j(g), 1), :].rearrange("p a d -> p (a d)")),
                                            per_head(weight, j(g)), ALU.mult).then_inc(wv_ready, 1)
                        if (g := t.ago(2)):
                            s = g.k % 2
                            e.wait_ge(prod_ready, g.n + 1)
                            e.wait_ge(x_bias_ready, g.n + 1)
                            e.tensor_tensor(x2_out[:, g.k, :], p_out[s][:, 0:D], x_bias[:, g.k, :], ALU.add).then_inc(row_ready, 1)
                        if (g := t.ago(0)):
                            s = g.k % 2
                            e.wait_ge(wv_ready, g.n + 1)
                            if isinstance(g.n, int) and g.n == 0:
                                e.wait_ge(cleared, 2)
                            wait(e, acc_ready, g.n)
                            wait(e, scaled_ready, g.n - 1)
                            wait(e, catch_done, g.n - 1)
                            gate(e)
                            e.scalar_tensor_tensor(out=open_acc[:, s, :], in0=open_acc[:, 1 - s, :], scalar=col(same_next, j(g)),
                                                   in1=wv[:, s, :], op0=ALU.mult, op1=ALU.add).then_inc(acc_ready, 1)
                            e.wait_ge(acc_ready, g.n + 1)
                            wait(e, sum_ready, g.n - 1)
                            gate(e)
                            e.tensor_tensor(heads(scaled[:, s, :]), heads(open_acc[:, s, :]), per_head(z_inv, j(g)), ALU.mult)\
                                .then_inc(scaled_ready, 1)
                            wait(e, catch_done, g.n)
                            gate(e)
                            e.scalar_tensor_tensor(out=caught[:], in0=open_acc[:, s, :], scalar=col(cap_start, j(g)),
                                                   in1=caught[:], op0=ALU.mult, op1=ALU.add).then_inc(catch_done, 1)

                    over_tiles(e, COLS, UN, LAG, step)

                @block.tensor
                def _(e):
                    def step(t):
                        if (g := t.ago(1)):
                            s = g.k % 2
                            e.wait_ge(scaled_ready, g.n + 1)
                            e.wait_ge(own_ready, g.n + 1)
                            wait(e, attT_ready, g.n - 1)
                            e.matmul(p_sum[s][:, 0:P], scaled[:, s, :], ident[:], start=True, stop=False)
                            e.matmul(p_sum[s][:, 0:P], own[:, s, :], ident[:], start=False, stop=True).then_inc(sum_ready, 1)
                        if (g := t.ago(2)):
                            s = g.k % 2
                            e.wait_ge(attT_ready, g.n + 1)
                            wait(e, row_ready, g.n - 1)
                            e.matmul(p_out[s][:, 0:D], attT[:, s, :], w_o[:], start=True, stop=True).then_inc(prod_ready, 1)

                    over_tiles(e, COLS, UN, LAG, step)

                @block.scalar
                def _(e):
                    def step(t):
                        if (g := t.ago(1)):
                            s = g.k % 2
                            e.wait_ge(sum_ready, g.n + 1)
                            wait(e, prod_ready, g.n - 1)
                            e.activation(attT[:, s, :], p_sum[s][:, 0:P], ACT.Copy).then_inc(attT_ready, 1)

                    over_tiles(e, COLS, UN, LAG, step)

            scattered.passed(COLS // UN)

        def weighted_border(border_z):
            with ExitStack() as c:
                xv = sb("xv", [P, 2 * D], F32, c)
                acc = sb("acc", [P, D], F32, c)
                own = sb("own", [P, D], F32, c)
                z = sb("z", [P, HEADS], F32, c)
                x_bias = sb("x_bias", [P, D], F32, c)
                attT = sb("attT", [P, P], F32, c)
                x2 = sb("x2", [P, D], F32, c)
                p_open = ps("p_open", c)
                p_z = ps("p_z", c)
                p_turn = ps("p_turn", c)
                p_out = ps("p_out", c)
                xv_in = border_gathered
                open_ready = sem("open_ready", c)
                dve_done = sem("dve_done", c)
                att_ready = sem("att_ready", c)
                att_turned = sem("att_turned", c)
                attT_ready = sem("attT_ready", c)
                prod_ready = sem("prod_ready", c)
                row_ready = sem("row_ready", c)
                block = program(c)

                @block.gpsimd
                def _(e):
                    e.indirect_dma_start(out=xv[:], out_offset=None, in_=tile_xv,
                                         in_offset=bass.IndirectOffsetOnAxis(ap=border[:, POS_LAST:POS_LAST + 1], axis=0))\
                        .then_inc(xv_in[0], 16)
                    e.wait_ge(row_ready, 1)
                    e.indirect_dma_start(out=x2_table, in_=x2[:], in_offset=None,
                                         out_offset=bass.IndirectOffsetOnAxis(ap=border[:, WR_LAST:WR_LAST + 1], axis=0),
                                         bounds_check=N - 1, oob_is_err=False).then_inc(border_scattered[0], 16)
                    e.wait_ge(border_scattered[0], border_scattered.after(1))

                @block.tensor
                def _(e):
                    e.matmul(p_open[:, 0:D], before[:], open_acc[:, (COLS - 1) % 2, :], start=True, stop=True)
                    e.matmul(p_z[:, 0:HEADS], before[:], border_z[:, 1, :], start=True, stop=True).then_inc(open_ready, 1)
                    e.wait_ge(att_ready, 1)
                    e.transpose(p_turn[:, 0:P], acc[:], ident[:]).then_inc(att_turned, 1)
                    e.wait_ge(attT_ready, 1)
                    e.matmul(p_out[:, 0:D], attT[:], w_o[:], start=True, stop=True).then_inc(prod_ready, 1)

                @block.scalar
                def _(e):
                    e.wait_ge(att_turned, 1)
                    e.activation(attT[:], p_turn[:, 0:P], ACT.Copy).then_inc(attT_ready, 1)

                @block.vector
                def _(e):
                    made = [0]

                    def chain(ins):
                        made[0] += 1
                        ins.then_inc(dve_done, 1)
                        e.wait_ge(dve_done, made[0])

                    def wide(w):
                        return w.unsqueeze(2).to_broadcast([P, HEADS, HD])

                    e.wait_ge(open_ready, 1)
                    e.wait_ge(xv_in[0], xv_in.after(1))
                    chain(e.tensor_tensor(acc[:], caught[:], p_open[:, 0:D], ALU.add))
                    chain(e.tensor_tensor(z[:], border_z[:, 0, :], p_z[:, 0:HEADS], ALU.add))
                    chain(e.tensor_tensor(z[:], z[:], border_z[:, 2, :], ALU.add))
                    chain(e.tensor_scalar(z[:], z[:], 1e-30, None, ALU.max))
                    chain(e.reciprocal(z[:], z[:]))
                    chain(e.tensor_tensor(heads(own[:]), heads(xv[:, D:2 * D]), wide(border_z[:, 2, :]), ALU.mult))
                    chain(e.tensor_tensor(acc[:], acc[:], own[:], ALU.add))
                    e.tensor_tensor(heads(acc[:]), heads(acc[:]), wide(z[:]), ALU.mult).then_inc(att_ready, 1)
                    chain(e.tensor_tensor(x_bias[:], xv[:, 0:D], att_bias[:], ALU.add))
                    e.wait_ge(prod_ready, 1)
                    e.tensor_tensor(x2[:], p_out[:, 0:D], x_bias[:], ALU.add).then_inc(row_ready, 1)

        def ffn():
            with ExitStack() as c:
                XSL = 4
                x1_in = sb("x1_in", [P, XSL, GROUP], F32, c)
                x2_in = sb("x2_in", [P, XSL, GROUP], F32, c)
                both = sb("both", [P, XSL, GROUP], F32, c)
                normed = sb("normed", [P, 2, GROUP], F32, c)
                nT = sb("nT", [P, 2, GROUP], F32, c)
                g_T = sb("g_T", [P, 2, FCH, GROUP], F32, c)
                yT = sb("yT", [P, 2, GROUP], F32, c)
                ys = sb("ys", [P, XSL, GROUP], F32, c)
                res = sb("res", [P, XSL, GROUP], F32, c)
                stats = sb("stats", [P, 2, GT, 6], F32, c)
                mv = sb("mv", [P, XSL, GT, 2], F32, c)
                var = sb("var", [P, XSL, GT], F32, c)
                rstd = sb("rstd", [P, XSL, GT], F32, c)
                stats2 = sb("stats2", [P, 2, GT, 6], F32, c)
                mv2 = sb("mv2", [P, XSL, GT, 2], F32, c)
                var2 = sb("var2", [P, XSL, GT], F32, c)
                rstd2 = sb("rstd2", [P, XSL, GT], F32, c)
                p_n = ps("p_n", c)
                p_f = [ps(f"p_f{s}", c) for s in range(4)]
                p_y = ps("p_y", c)
                p_r = [ps(f"p_r{s}", c) for s in range(2)]
                x1_loaded = sems("x1_loaded", XSL, c)
                x2_loaded = sems("x2_loaded", XSL, c)
                stored = sems("stored", XSL, c)
                both_ready = sem("both_ready", c)
                stats_ready = sem("stats_ready", c)
                mv_ready = sem("mv_ready", c)
                var_ready = sem("var_ready", c)
                rstd_ready = sem("rstd_ready", c)
                normed_ready = sem("normed_ready", c)
                n_turned = sem("n_turned", c)
                nT_ready = sem("nT_ready", c)
                f_prod = sem("f_prod", c)
                gelu_ready = sem("gelu_ready", c)
                y_prod = sem("y_prod", c)
                yT_ready = sem("yT_ready", c)
                y_turned = sem("y_turned", c)
                sum_ready = sem("sum_ready", c)
                stats2_ready = sem("stats2_ready", c)
                mv2_ready = sem("mv2_ready", c)
                var2_ready = sem("var2_ready", c)
                rstd2_ready = sem("rstd2_ready", c)
                res_ready = sem("res_ready", c)
                block = program(c)
                LAG = 6

                def rows(table, t):
                    return table[bass.ds(group_rows(t.n), GROUP), :].rearrange("(p a) d -> p (a d)", a=GT)

                @block.sync
                def _(e):
                    def step(t):
                        if (g := t.ago(0)):
                            wait(e, both_ready, g.n - XSL + 1)
                            gate(e)
                            wait(e, normed_ready, g.n - XSL + 1)
                            gate(e)
                            e.dma_start(x2_in[:, g.k, :], rows(x2_table, g)).then_inc(x2_loaded[g.k], 16)
                            e.dma_start(x1_in[:, g.k, :], rows(x1_table, g)).then_inc(x1_loaded[g.k], 16)
                        if (g := t.ago(6)):
                            if isinstance(g.n, int) and g.n == NG - 1:
                                e.wait_ge(stored[(g.n - 1) % XSL], 16 * ((g.n - 1) // XSL + 1))
                            gate(e)
                            e.wait_ge(res_ready, g.n + 1)
                            gate(e)
                            e.dma_start(rows(out, g), res[:, g.k, :]).then_inc(stored[g.k], 16)

                    over_tiles(e, NG, XSL, LAG, step, peeled=3)
                    for k in range(XSL):
                        e.wait_ge(stored[k], 16 * len(range(k, NG, XSL)))

                @block.gpsimd
                def _(e):
                    def step(t):
                        if (g := t.ago(0)):
                            e.wait_ge(mv_ready, g.n + 1)
                            gate(e)
                            e.tensor_scalar(var[:, g.k, :], mv[:, g.k, :, 1], EPS, None, ALU.add).then_inc(var_ready, 1)
                            e.wait_ge(var_ready, g.n + 1)
                            gate(e)
                            e.tensor_tensor(rstd[:, g.k, :], var[:, g.k, :], minus_half[:], ALU.pow).then_inc(rstd_ready, 1)
                            e.wait_ge(x1_loaded[g.k], 16 * (g.b + 1))
                            e.wait_ge(x2_loaded[g.k], 16 * (g.b + 1))
                            wait(e, sum_ready, g.n - XSL + 1)
                            gate(e)
                            e.tensor_tensor(both[:, g.k, :], x1_in[:, g.k, :], x2_in[:, g.k, :], ALU.add).then_inc(both_ready, 1)
                        if (g := t.ago(4)):
                            e.wait_ge(mv2_ready, g.n + 1)
                            gate(e)
                            e.tensor_scalar(var2[:, g.k, :], mv2[:, g.k, :, 1], EPS, None, ALU.add).then_inc(var2_ready, 1)
                            e.wait_ge(var2_ready, g.n + 1)
                            gate(e)
                            e.tensor_tensor(rstd2[:, g.k, :], var2[:, g.k, :], minus_half[:], ALU.pow).then_inc(rstd2_ready, 1)

                    over_tiles(e, NG, XSL, LAG, step, peeled=3)

                @block.tensor
                def _(e):
                    def turn_in(g):
                        e.wait_ge(normed_ready, g.n + 1)
                        wait(e, nT_ready, g.n)
                        for a in range(GT):
                            mm = e.transpose(p_n[:, a * P:(a + 1) * P], normed[:, g.k % 2, a * D:(a + 1) * D], ident[:])
                        mm.then_inc(n_turned, 1)

                    def step(t):
                        if (g := t.ago(2)):
                            s = g.k % 2
                            e.wait_ge(nT_ready, g.n + 1)
                            for ch in range(FCH):
                                wait(e, gelu_ready, FCH * g.n + ch - 3)
                                e.matmul(p_f[ch][:], w_1[:, ch * P:(ch + 1) * P], nT[:, s, :], start=True, stop=True)\
                                    .then_inc(f_prod, 1)
                        if (g := t.ago(1)):
                            turn_in(g)
                        if (g := t.ago(3)):
                            s = g.k % 2
                            wait(e, yT_ready, g.n)
                            for ch in range(FCH):
                                e.wait_ge(gelu_ready, FCH * g.n + ch + 1)
                                mm = e.matmul(p_y[:], w_2[:, ch, :], g_T[:, s, ch, :], start=(ch == 0), stop=(ch == FCH - 1))
                            mm.then_inc(y_prod, 1)
                        if (g := t.ago(4)):
                            s = g.k % 2
                            e.wait_ge(yT_ready, g.n + 1)
                            wait(e, sum_ready, g.n - 1)
                            for a in range(GT):
                                mm = e.transpose(p_r[s][:, a * D:(a + 1) * D], yT[:, s, a * P:(a + 1) * P], ident[:])
                            mm.then_inc(y_turned, 1)

                    over_tiles(e, NG, XSL, LAG, step, peeled=3)

                @block.scalar
                def _(e):
                    def step(t):
                        if (g := t.ago(3)):
                            s = g.k % 2
                            e.wait_ge(y_prod, g.n + 1)
                            wait(e, y_turned, g.n - 1)
                            e.activation(yT[:, s, :], p_y[:], ACT.Identity, bias=bf2[:]).then_inc(yT_ready, 1)
                        if (g := t.ago(1)):
                            s = g.k % 2
                            e.wait_ge(n_turned, g.n + 1)
                            wait(e, f_prod, FCH * (g.n - 1))
                            e.activation(nT[:, s, :], p_n[:], ACT.Copy).then_inc(nT_ready, 1)
                        if (g := t.ago(2)):
                            s = g.k % 2
                            for ch in range(FCH):
                                e.wait_ge(f_prod, FCH * g.n + ch + 1)
                                if ch == 0:
                                    wait(e, y_prod, g.n - 1)
                                e.activation(g_T[:, s, ch, :], p_f[ch][:], ACT.Gelu, bias=bf1[:, ch:ch + 1]).then_inc(gelu_ready, 1)

                    over_tiles(e, NG, XSL, LAG, step, peeled=3)

                @block.vector
                def _(e):
                    def norm_rows(into, rows_in, mean, scale, ready):
                        for a in range(GT):
                            ins = e.tensor_scalar(into[:, a * D:(a + 1) * D], rows_in[:, a * D:(a + 1) * D],
                                                  mean[:, a, 0:1], scale[:, a:a + 1], ALU.subtract, ALU.mult)
                        ins.then_inc(ready, 1)

                    def step(t):
                        if (g := t.ago(0)):
                            s = g.k % 2
                            e.wait_ge(x2_loaded[g.k], 16 * (g.b + 1))
                            for a in range(GT):
                                ins = e.bn_stats(stats[:, s, a, :], x2_in[:, g.k, a * D:(a + 1) * D])
                            ins.then_inc(stats_ready, 1)
                            e.wait_ge(stats_ready, g.n + 1)
                            gate(e)
                            for a in range(GT):
                                ins = e.bn_aggr(mv[:, g.k, a, :], stats[:, s, a, :])
                            ins.then_inc(mv_ready, 1)
                        if (g := t.ago(4)):
                            s = g.k % 2
                            e.wait_ge(y_turned, g.n + 1)
                            e.wait_ge(both_ready, g.n + 1)
                            e.tensor_tensor(ys[:, g.k, :], p_r[s][:], both[:, g.k, :], ALU.add).then_inc(sum_ready, 1)
                            e.wait_ge(sum_ready, g.n + 1)
                            for a in range(GT):
                                ins = e.bn_stats(stats2[:, s, a, :], ys[:, g.k, a * D:(a + 1) * D])
                            ins.then_inc(stats2_ready, 1)
                            e.wait_ge(stats2_ready, g.n + 1)
                            gate(e)
                            for a in range(GT):
                                ins = e.bn_aggr(mv2[:, g.k, a, :], stats2[:, s, a, :])
                            ins.then_inc(mv2_ready, 1)
                        if (g := t.ago(0)):
                            s = g.k % 2
                            e.wait_ge(rstd_ready, g.n + 1)
                            wait(e, n_turned, g.n - 1)
                            norm_rows(normed[:, s, :], x2_in[:, g.k, :], mv[:, g.k], rstd[:, g.k], normed_ready)
                        if (g := t.ago(5)):
                            e.wait_ge(rstd2_ready, g.n + 1)
                            wait(e, stored[g.k], 16 * g.b)
                            norm_rows(res[:, g.k, :], ys[:, g.k, :], mv2[:, g.k], rstd2[:, g.k], res_ready)

                    over_tiles(e, NG, XSL, LAG, step, peeled=3)

        prepare()
        dense()
        for l in range(2):
            layer(l)
            layer_border(l)
        with ExitStack() as att:
            logits = sb("logits", [P, 2 * HEADS, COLS], F32, att)
            weight = sb("weight", [P, HEADS, COLS], F32, att)
            z_inv = sb("z_inv", [P, HEADS, COLS], F32, att)
            self_weight = sb("self_weight", [P, HEADS, COLS], F32, att)
            border_z = sb("border_z", [P, 3, HEADS], F32, att)
            values = sb("values", [P, COLS, D], F32, att)
            attention(values, logits)
            softmax(logits, weight, z_inv, self_weight, border_z)
            weighted(values, weight, z_inv, self_weight)
            weighted_border(border_z)
        ffn()


_INS = ['x', 'src', 'dst', 'edge_type_200', 'L0_gnn_rel_embed', 'L0_gnn_W_r1', 'L0_gnn_W_sl1', 'L0_gnn_W_el1',
        'L0_gnn_W_r2', 'L0_gnn_W_sl2', 'L0_gnn_W_el2', 'L1_gnn_Wq', 'L1_gnn_bq', 'L1_gnn_Wk', 'L1_gnn_bk',
        'L1_gnn_Wv', 'L1_gnn_bv', 'L1_gnn_Wo', 'L1_gnn_bo', 'L1_gnn_g1', 'L1_gnn_b1', 'L1_gnn_g2', 'L1_gnn_b2',
        'L1_gnn_W1', 'L1_gnn_bf1', 'L1_gnn_W2', 'L1_gnn_bf2']


def kernel(**inputs):
    import numpy as _np
    import concourse.bacc as _bacc
    from concourse import mybir as _mybir
    from concourse.bass_utils import run_bass_kernel_spmd as _run

    nc = _bacc.Bacc("TRN2", target_bir_lowering=False, num_devices=1)
    arrays, args = {}, []
    for name in _INS:
        a = _np.ascontiguousarray(inputs[name])
        arrays[f"in_{name}_dram"] = a
        args.append(nc.dram_tensor(f"in_{name}_dram", a.shape, _mybir.dt.from_np(a.dtype), kind="ExternalInput").ap())
    out = nc.dram_tensor("out_0_dram", inputs['x'].shape, _mybir.dt.float32, kind="ExternalOutput").ap()
    gnn_program(nc, *args, out)
    r = _run(nc, [arrays], core_ids=[0])
    return r.results[0]["out_0_dram"]
```

```python
from contextlib import ExitStack

import concourse.bass as bass
from concourse import mybir

F32 = mybir.dt.float32
I32 = mybir.dt.int32
ALU = mybir.AluOpType
ACT = mybir.ActivationFunctionType
AX_X = mybir.AxisListType.X

P = 128
D = 128
HEADS, HD = 8, 16
FFN = 512
FCH = FFN // P
EPS = 1e-5
SLOPE = (1.0 / 8.0 + 1.0 / 3.0) / 2.0
LOW = 1e30
SKIP = 60000

MUN = 20
UN = 10
GUN = 8
GT = 4
GROUP = GT * P


class Turn:

    def __init__(self, n, k, b, total, unroll):
        self.n, self.k, self.b, self.total, self.unroll = n, k, b, total, unroll

    def ago(self, lag):
        n = self.n - lag
        if isinstance(n, int) and not 0 <= n < self.total:
            return None
        k = self.k - lag
        return Turn(n, k % self.unroll, self.b + k // self.unroll, self.total, self.unroll)


def over_tiles(eng, total, unroll, lag, step, peeled=1):
    assert lag <= peeled * unroll
    for n in range(peeled * unroll):
        step(Turn(n, n % unroll, n // unroll, total, unroll))
    with eng.Fori(peeled, total // unroll) as b:
        for k in range(unroll):
            step(Turn(b * unroll + k, k, b, total, unroll))
    for n in range(total // unroll * unroll, total + lag):
        step(Turn(n, n % unroll, n // unroll, total, unroll))


class DmaSems(list):

    def __init__(self, sems):
        super().__init__(sems)
        self.before = 0

    def after(self, dmas):
        return self.before + 16 * dmas

    def passed(self, dmas):
        self.before += 16 * dmas


def wait(eng, sem, value):
    if not isinstance(value, int) or value > 0:
        eng.wait_ge(sem, value)


def col(t, j):
    return t[:, bass.ds(j, 1)]


def per_head(t, j):
    return t[:, :, bass.ds(j, 1)].to_broadcast([P, HEADS, HD])


def heads(ap):
    return ap.rearrange("p (h d) -> p h d", h=HEADS)


def gnn_program(nc, x, src, dst, edge_type_200, L0_gnn_rel_embed, L0_gnn_W_r1, L0_gnn_W_sl1, L0_gnn_W_el1,
                L0_gnn_W_r2, L0_gnn_W_sl2, L0_gnn_W_el2, L1_gnn_Wq, L1_gnn_bq, L1_gnn_Wk, L1_gnn_bk,
                L1_gnn_Wv, L1_gnn_bv, L1_gnn_Wo, L1_gnn_bo, L1_gnn_g1, L1_gnn_b1, L1_gnn_g2, L1_gnn_b2,
                L1_gnn_W1, L1_gnn_bf1, L1_gnn_W2, L1_gnn_bf2, out):
    N = x.shape[0]
    E = src.shape[0]
    COLS = 200
    EP = E // COLS
    assert EP * COLS == E and COLS % MUN == 0 and COLS % UN == 0
    ROWS = COLS * P
    RELS = L0_gnn_rel_embed.shape[0]
    NG = -(-N // GROUP)

    def group_rows(n):
        return n * GROUP if not isinstance(n, int) else min(n * GROUP, N - GROUP)

    h1_table = nc.dram_tensor("h1_table", [N, D], F32).ap()
    x1_table = nc.dram_tensor("x1_table", [N, D], F32).ap()
    x2_table = nc.dram_tensor("x2_table", [N, D], F32).ap()
    tile_hx = nc.dram_tensor("tile_hx", [ROWS, 2 * D], F32).ap()
    tile_x1 = nc.dram_tensor("tile_x1", [ROWS, D], F32).ap()
    tile_xv = nc.dram_tensor("tile_xv", [ROWS, 2 * D], F32).ap()
    open_max = nc.dram_tensor("open_max", [2 * P, HEADS], F32).ap()

    root = ExitStack()
    with root:
        uses = {}

        def named(name):
            uses[name] = uses.get(name, 0) + 1
            return f"{name}_{uses[name]}"

        def sb(name, shape, dt=F32, ctx=root):
            return ctx.enter_context(nc.sbuf_tensor(named(name), shape, dt))

        def ps(name, ctx):
            return ctx.enter_context(nc.psum_tensor(named(name), [P, 512], F32))

        in_use = []

        def sem(name, ctx):
            in_use.append(ctx.enter_context(nc.semaphore(named(name))))
            return in_use[-1]

        def program(ctx):
            def clear():
                numbers = sorted(s.num for s in in_use)
                start = numbers[0]
                for n, after_n in zip(numbers, numbers[1:] + [None]):
                    if after_n != n + 1:
                        nc.sync.sem_clear(range(start, n + 1))
                        start = after_n
                nc.all_engine_barrier()
                in_use.clear()

            ctx.callback(clear)
            return ctx.enter_context(nc.Block())

        def sems(name, n, ctx):
            return [sem(f"{name}{k}", ctx) for k in range(n)]

        gathered, gathered_dst, scattered = (DmaSems([sem(f"{name}{k}", root) for k in range(MUN)])
                                             for name in ("gathered", "gathered_dst", "scattered"))
        x1_gathered, x2_scattered = (DmaSems([sem(f"{name}{k}", root) for k in range(UN)])
                                     for name in ("x1_gathered", "x2_scattered"))
        border_gathered, border_scattered = (DmaSems([sem(name, root)]) for name in ("border_gathered", "border_scattered"))
        passed = {engine: sem(f"passed_{engine}", root) for engine in ("sync", "gpsimd", "vector")}
        in_use.clear()

        def gate(eng):
            eng.sem_inc(passed[{nc.sync: "sync", nc.gpsimd: "gpsimd", nc.vector: "vector"}[eng]], 1)

        ident = sb("ident", [P, P])
        ones = sb("ones", [P, COLS])
        eps = sb("eps", [P, 1])
        minus_half = sb("minus_half", [P, GT])
        rel_ids = sb("rel_ids", [P, 2 * P])
        rel = sb("rel", [P, 2, D])
        w_r = [sb(f"w_r{l}", [D, D]) for l in range(2)]
        w_sl = [sb(f"w_sl{l}", [D, D]) for l in range(2)]
        w_el = [sb(f"w_el{l}", [D, D]) for l in range(2)]
        w_vqk = sb("w_vqk", [D, 3 * D])
        bias_vqk = sb("bias_vqk", [P, 4 * D])
        w_o = sb("w_o", [D, D])
        bo_rows = sb("bo_rows", [P, D])
        att_bias = sb("att_bias", [P, D])
        w_1 = sb("w_1", [D, FFN])
        w_2 = sb("w_2", [P, FCH, D])
        bf1 = sb("bf1", [P, FCH])
        bf2 = sb("bf2", [P, 1])
        type_f = sb("type_f", [P, COLS])
        same_prev = sb("same_prev", [P, COLS])
        same_next = sb("same_next", [P, COLS])
        is_end = sb("is_end", [P, COLS])
        keep_x = sb("keep_x", [P, COLS])
        cap_end = sb("cap_end", [P, COLS])
        cap_start = sb("cap_start", [P, COLS])
        in_first = sb("in_first", [P, COLS])
        in_last = sb("in_last", [P, COLS])
        norm = sb("norm", [P, COLS])
        idx = sb("idx", [P, 4, COLS], I32)
        SRC, DST, AT_END, AT_START = range(4)
        border = sb("border", [P, 6], I32)
        WR_FIRST, WR_LAST, RD_FIRST, RD_LAST, POS_FIRST, POS_LAST = range(6)
        after = sb("after", [P, P])
        before = sb("before", [P, P])
        border_norm = sb("border_norm", [P, 1])
        first_last = sb("first_last", [P, 2 * P])
        dst_fl = sb("dst_fl", [P, 2])
        open_acc = sb("open_acc", [P, 2, D])
        caught = sb("caught", [P, D])
        border_h = sb("border_h", [P, D])
        border_x = sb("border_x", [P, D])

        def prepare():
            with ExitStack() as c:
                src_i = sb("src_i", [P, COLS], I32, c)
                dst_i = sb("dst_i", [P, COLS], I32, c)
                type_i = sb("type_i", [P, COLS], I32, c)
                side_i = sb("side_i", [P, 2], I32, c)
                dst_f = sb("dst_f", [P, COLS], F32, c)
                side = sb("side", [P, 2], F32, c)
                first = sb("first", [P, COLS], F32, c)
                last = sb("last", [P, COLS], F32, c)
                real = sb("real", [P, COLS], F32, c)
                is_start = sb("is_start", [P, COLS], F32, c)
                goes = sb("goes", [P, 2], F32, c)
                tmp = sb("tmp", [P, COLS], F32, c)
                count = sb("count", [P, COLS], F32, c)
                pos = sb("pos", [P, COLS], F32, c)
                caught_count = sb("caught_count", [P, 1], F32, c)
                has = sb("has", [P, 2], F32, c)
                has_pos = sb("has_pos", [P, 2], F32, c)
                bcol = sb("bcol", [P, 1], F32, c)
                diag = sb("diag", [P, 2, P], F32, c)
                up = sb("up", [P, P], F32, c)
                down = sb("down", [P, P], F32, c)
                gcol = sb("gcol", [P, 4], F32, c)
                b1_cols = sb("b1_cols", [P, P], F32, c)
                vecs = sb("vecs", [P, 3, D], F32, c)
                bvT = sb("bvT", [P, P], F32, c)
                p_row = ps("p_row", c)
                p_cnt = ps("p_cnt", c)
                p_vqk = ps("p_vqk", c)
                p_bvT = ps("p_bvT", c)
                p_att = ps("p_att", c)
                p_bf1 = ps("p_bf1", c)
                filled = sem("filled", c)
                loaded = sem("loaded", c)
                edges_in = sem("edges_in", c)
                consts = sem("consts", c)
                dve_done = sem("dve_done", c)
                rows_ready = sem("rows_ready", c)
                diag_ready = sem("diag_ready", c)
                masks_ready = sem("masks_ready", c)
                cnt_ready = sem("cnt_ready", c)
                cnt_summed = sem("cnt_summed", c)
                root_ready = sem("root_ready", c)
                vecs_ready = sem("vecs_ready", c)
                b1_ready = sem("b1_ready", c)
                bv_ready = sem("bv_ready", c)
                bvT_ready = sem("bvT_ready", c)
                bvT_copied = sem("bvT_copied", c)
                att_ready = sem("att_ready", c)
                bf1_ready = sem("bf1_ready", c)
                block = program(c)

                @block.gpsimd
                def _(e):
                    e.memset(src_i[:], 0).then_inc(filled, 1)
                    e.memset(dst_i[:], N).then_inc(filled, 1)
                    e.memset(type_i[:], 0).then_inc(filled, 1)
                    e.memset(side_i[:], N).then_inc(filled, 1)
                    e.memset(rel[:], 0.0).then_inc(filled, 1)
                    e.memset(ident[:], 0.0).then_inc(consts, 1)
                    e.memset(up[:], 1.0).then_inc(consts, 1)
                    e.memset(down[:], 1.0).then_inc(consts, 1)
                    e.memset(ones[:], 1.0).then_inc(consts, 1)
                    e.memset(eps[:], EPS).then_inc(consts, 1)
                    e.memset(minus_half[:], -0.5).then_inc(consts, 1)
                    e.iota(rel_ids[:], pattern=[[1, 2 * P]], base=0, channel_multiplier=0,
                           allow_small_or_imprecise_dtypes=True).then_inc(consts, 1)
                    e.iota(pos[:], pattern=[[P, COLS]], base=0, channel_multiplier=1,
                           allow_small_or_imprecise_dtypes=True).then_inc(consts, 1)
                    e.wait_ge(consts, 3)
                    e.affine_select(out=ident[:], in_=ident[:], compare_op=ALU.not_equal, fill=1.0, base=0,
                                    pattern=[[-1, P]], channel_multiplier=1).then_inc(consts, 1)
                    e.affine_select(out=up[:], in_=up[:], compare_op=ALU.is_gt, fill=0.0, base=0,
                                    pattern=[[1, P]], channel_multiplier=-1).then_inc(consts, 1)
                    e.affine_select(out=down[:], in_=down[:], compare_op=ALU.is_gt, fill=0.0, base=0,
                                    pattern=[[-1, P]], channel_multiplier=1).then_inc(consts, 1)

                @block.sync
                def _(e):
                    e.wait_ge(filled, 5)
                    e.dma_start(dst_i[0:EP, :], dst.rearrange("(p j) -> p j", j=COLS)).then_inc(edges_in, 16)
                    e.dma_start(src_i[0:EP, :], src.rearrange("(p j) -> p j", j=COLS)).then_inc(edges_in, 16)
                    e.dma_start(type_i[0:EP, :], edge_type_200.rearrange("(p j) -> p j", j=COLS)).then_inc(edges_in, 16)
                    by_part = dst.rearrange("(p j) -> p j", j=COLS)
                    e.dma_start(side_i[1:EP, 0:1], by_part[0:EP - 1, COLS - 1:COLS], allow_slow_non_contiguous=True).then_inc(edges_in, 16)
                    e.dma_start(side_i[0:EP - 1, 1:2], by_part[1:EP, 0:1], allow_slow_non_contiguous=True).then_inc(edges_in, 16)
                    e.dma_start(rel[:, 0, :], L0_gnn_rel_embed[0:P, :]).then_inc(edges_in, 16)
                    e.dma_start(rel[0:RELS - P, 1, :], L0_gnn_rel_embed[P:RELS, :]).then_inc(edges_in, 16)
                    for t, a in ((w_r[0], L0_gnn_W_r1), (w_sl[0], L0_gnn_W_sl1), (w_el[0], L0_gnn_W_el1),
                                 (w_r[1], L0_gnn_W_r2), (w_sl[1], L0_gnn_W_sl2), (w_el[1], L0_gnn_W_el2)):
                        e.dma_start(t[:], a).then_inc(edges_in, 16)
                    e.wait_ge(edges_in, 13 * 16)

                @block.scalar
                def _(e):
                    for n, a in enumerate((L1_gnn_Wv, L1_gnn_Wq, L1_gnn_Wk)):
                        e.dma_start(w_vqk[:, n * D:(n + 1) * D], a).then_inc(loaded, 16)
                    for n, a in enumerate((L1_gnn_g1, L1_gnn_b1, L1_gnn_g2, L1_gnn_b2)):
                        e.dma_start(gcol[:, n:n + 1], a.rearrange("(p a) -> p a", a=1)).then_inc(loaded, 16)
                    e.dma_start(bf2[:], L1_gnn_bf2.rearrange("(p a) -> p a", a=1)).then_inc(loaded, 16)
                    for n, a in enumerate((L1_gnn_bv, L1_gnn_bq, L1_gnn_bk)):
                        e.dma_start(vecs[:, n, :], a.partition_broadcast(P)).then_inc(loaded, 16)
                    e.dma_start(bo_rows[:], L1_gnn_bo.partition_broadcast(P)).then_inc(loaded, 16)
                    e.dma_start(w_o[:], L1_gnn_Wo).then_inc(loaded, 16)
                    e.dma_start(w_1[:], L1_gnn_W1).then_inc(loaded, 16)
                    e.dma_start(w_2[:], L1_gnn_W2.rearrange("(c p) n -> p c n", p=P)).then_inc(loaded, 16)
                    e.dma_start(bf1[:], L1_gnn_bf1.rearrange("(c p) -> p c", p=P), allow_slow_non_contiguous=True).then_inc(loaded, 16)
                    e.wait_ge(cnt_summed, 2)
                    e.activation(norm[:], count[:], ACT.Sqrt).then_inc(root_ready, 1)
                    e.activation(border_norm[:], caught_count[:], ACT.Sqrt).then_inc(root_ready, 1)

                @block.tensor
                def _(e):
                    e.wait_ge(consts, 11)
                    e.wait_ge(diag_ready, 2)
                    for s in range(2):
                        mm = e.matmul(p_row[:, s * P:(s + 1) * P], ones[:, 0:P], diag[:, s, :], start=True, stop=True)
                    mm.then_inc(rows_ready, 1)
                    e.wait_ge(masks_ready, 1)
                    e.matmul(p_cnt[:, 0:1], after[:], count[:, COLS - 1:COLS], start=True, stop=True).then_inc(cnt_ready, 1)
                    e.wait_ge(b1_ready, 1)
                    e.matmul(p_vqk[:, 0:3 * D], b1_cols[:], w_vqk[:], start=True, stop=True).then_inc(vecs_ready, 1)
                    for ch in range(FCH):
                        mm = e.matmul(p_bf1[:, ch:ch + 1], w_1[:, ch * P:(ch + 1) * P], gcol[:, 3:4], start=True, stop=True)
                    mm.then_inc(bf1_ready, 1)
                    e.wait_ge(bv_ready, 1)
                    e.transpose(p_bvT[:, 0:P], bias_vqk[:, 0:D], ident[:]).then_inc(bvT_ready, 1)
                    e.wait_ge(bvT_copied, 1)
                    e.matmul(p_att[:, 0:D], bvT[:], w_o[:], start=True, stop=True).then_inc(att_ready, 1)

                @block.vector
                def _(e):
                    made = [0]

                    def chain(ins):
                        made[0] += 1
                        ins.then_inc(dve_done, 1)
                        e.wait_ge(dve_done, made[0])

                    e.wait_ge(edges_in, 13 * 16)
                    e.wait_ge(consts, 11)
                    e.tensor_copy(idx[:, SRC, :], src_i[:])
                    e.tensor_copy(type_f[:], type_i[:])
                    e.tensor_copy(side[:], side_i[:])
                    chain(e.tensor_copy(dst_f[:], dst_i[:]))
                    e.tensor_copy(dst_fl[:, 0:1], dst_f[:, 0:1])
                    chain(e.tensor_copy(dst_fl[:, 1:2], dst_f[:, COLS - 1:COLS]))
                    for s in range(2):
                        e.tensor_scalar(diag[:, s, :], ident[:], dst_fl[:, s:s + 1], None, ALU.mult).then_inc(diag_ready, 1)
                    e.memset(same_prev[:, 0:1], 0.0)
                    e.memset(same_next[:, COLS - 1:COLS], 0.0)
                    e.tensor_tensor(same_prev[:, 1:COLS], dst_f[:, 1:COLS], dst_f[:, 0:COLS - 1], ALU.is_equal)
                    e.tensor_tensor(same_next[:, 0:COLS - 1], dst_f[:, 1:COLS], dst_f[:, 0:COLS - 1], ALU.is_equal)
                    e.tensor_tensor(goes[:], side[:], dst_fl[:], ALU.is_equal)
                    e.tensor_scalar(first[:], dst_f[:], dst_fl[:, 0:1], None, ALU.is_equal)
                    e.tensor_scalar(last[:], dst_f[:], dst_fl[:, 1:2], None, ALU.is_equal)
                    e.tensor_scalar(idx[:, DST, :], dst_f[:], float(N - 1), None, ALU.min)
                    chain(e.tensor_scalar(real[:], dst_f[:], float(N), None, ALU.is_lt))
                    e.tensor_copy(keep_x[:], same_next[:])
                    e.tensor_scalar(in_first[:], first[:], -1.0, LOW, ALU.add, ALU.mult)
                    e.tensor_scalar(in_last[:], last[:], -1.0, LOW, ALU.add, ALU.mult)
                    e.tensor_scalar(is_end[:], same_next[:], -1.0, 1.0, ALU.mult, ALU.add)
                    chain(e.tensor_scalar(is_start[:], same_prev[:], -1.0, 1.0, ALU.mult, ALU.add))
                    e.tensor_copy(keep_x[:, COLS - 1:COLS], goes[:, 1:2])
                    e.tensor_scalar(is_end[:, COLS - 1:COLS], goes[:, 1:2], -1.0, 1.0, ALU.mult, ALU.add)
                    chain(e.tensor_scalar(is_start[:, 0:1], goes[:, 0:1], -1.0, 1.0, ALU.mult, ALU.add))
                    for n, (at, seg, cap, write) in enumerate(((is_end, first, cap_end, AT_END),
                                                               (is_start, last, cap_start, AT_START))):
                        chain(e.tensor_tensor(tmp[:], at[:], real[:], ALU.mult))
                        chain(e.scalar_tensor_tensor(out=cap[:], in0=seg[:], scalar=goes[:, n:n + 1], in1=tmp[:],
                                                     op0=ALU.mult, op1=ALU.mult))
                        chain(e.tensor_tensor(tmp[:], tmp[:], cap[:], ALU.subtract))
                        chain(e.scalar_tensor_tensor(out=tmp[:], in0=dst_f[:], scalar=-float(SKIP), in1=tmp[:],
                                                     op0=ALU.add, op1=ALU.mult))
                        chain(e.tensor_scalar(idx[:, write, :], tmp[:], float(SKIP), None, ALU.add))
                        chain(e.tensor_reduce(has[:, n:n + 1], cap[:], AX_X, ALU.add))
                        chain(e.tensor_tensor(tmp[:], cap[:], pos[:], ALU.mult))
                        chain(e.tensor_reduce(has_pos[:, n:n + 1], tmp[:], AX_X, ALU.add))
                        chain(e.scalar_tensor_tensor(out=bcol[:], in0=dst_fl[:, n:n + 1], scalar=-float(SKIP),
                                                     in1=has[:, n:n + 1], op0=ALU.add, op1=ALU.mult))
                        chain(e.tensor_scalar(border[:, WR_FIRST + n:WR_FIRST + n + 1], bcol[:], float(SKIP), None, ALU.add))
                        chain(e.tensor_scalar(border[:, RD_FIRST + n:RD_FIRST + n + 1], dst_fl[:, n:n + 1], float(N - 1), None, ALU.min))
                    chain(e.scalar_tensor_tensor(out=bcol[:], in0=has[:, 0:1], scalar=-float(SKIP), in1=has_pos[:, 0:1],
                                                 op0=ALU.mult, op1=ALU.add))
                    chain(e.tensor_scalar(border[:, POS_FIRST:POS_FIRST + 1], bcol[:], float(SKIP), None, ALU.add))
                    chain(e.tensor_copy(border[:, POS_LAST:POS_LAST + 1], has_pos[:, 1:2]))
                    chain(e.tensor_tensor_scan(count[:], same_prev[:], ones[:], 0.0, ALU.mult, ALU.add))
                    e.wait_ge(rows_ready, 1)
                    chain(e.tensor_copy(first_last[:], p_row[:, 0:2 * P]))
                    chain(e.scalar_tensor_tensor(out=after[:], in0=first_last[:, 0:P], scalar=dst_fl[:, 1:2], in1=up[:],
                                                 op0=ALU.is_equal, op1=ALU.mult))
                    e.scalar_tensor_tensor(out=before[:], in0=first_last[:, P:2 * P], scalar=dst_fl[:, 0:1], in1=down[:],
                                           op0=ALU.is_equal, op1=ALU.mult).then_inc(masks_ready, 1)
                    chain(e.tensor_tensor(tmp[:], cap_end[:], count[:], ALU.mult))
                    chain(e.tensor_reduce(caught_count[:], tmp[:], AX_X, ALU.add))
                    e.wait_ge(cnt_ready, 1)
                    e.tensor_scalar(count[:], count[:], 1.0, None, ALU.max).then_inc(cnt_summed, 1)
                    chain(e.tensor_tensor(caught_count[:], caught_count[:], p_cnt[:, 0:1], ALU.add))
                    e.tensor_scalar(caught_count[:], caught_count[:], 1.0, None, ALU.max).then_inc(cnt_summed, 1)
                    e.wait_ge(root_ready, 2)
                    e.reciprocal(norm[:], norm[:])
                    chain(e.reciprocal(border_norm[:], border_norm[:]))
                    e.wait_ge(loaded, 16 * 16)
                    e.tensor_scalar(b1_cols[:], ones[:, 0:P], gcol[:, 1:2], None, ALU.mult).then_inc(b1_ready, 1)
                    e.wait_ge(vecs_ready, 1)
                    e.tensor_tensor(bias_vqk[:, 0:3 * D], p_vqk[:, 0:3 * D], vecs[:].rearrange("p a d -> p (a d)"), ALU.add)\
                        .then_inc(bv_ready, 1)
                    e.wait_ge(bf1_ready, 1)
                    e.tensor_tensor(bias_vqk[:, 3 * D:4 * D], p_vqk[:, 2 * D:3 * D], vecs[:, 2, :], ALU.add)
                    e.tensor_tensor(bf1[:], bf1[:], p_bf1[:, 0:FCH], ALU.add)
                    e.tensor_scalar(w_vqk[:], w_vqk[:], gcol[:, 0:1], None, ALU.mult)
                    e.tensor_scalar(w_1[:], w_1[:], gcol[:, 2:3], None, ALU.mult)
                    e.wait_ge(bvT_ready, 1)
                    e.tensor_copy(bvT[:], p_bvT[:, 0:P]).then_inc(bvT_copied, 1)
                    e.wait_ge(att_ready, 1)
                    e.tensor_tensor(att_bias[:], p_att[:, 0:D], bo_rows[:], ALU.add)

        def dense():
            with ExitStack() as c:
                x_in = sb("x_in", [P, GUN, GROUP], F32, c)
                xT = sb("xT", [P, 2, GROUP], F32, c)
                low1 = sb("low1", [P, 2, GROUP], F32, c)
                low2 = sb("low2", [P, 2, GROUP], F32, c)
                h1T = sb("h1T", [P, 2, GROUP], F32, c)
                h2T = sb("h2T", [P, 2, GROUP], F32, c)
                h1_rows = sb("h1_rows", [P, GUN, GROUP], F32, c)
                xs_rows = sb("xs_rows", [P, GUN, GROUP], F32, c)
                x1_rows = sb("x1_rows", [P, GUN, GROUP], F32, c)
                x2_rows = sb("x2_rows", [P, GUN, GROUP], F32, c)
                stats = sb("stats", [P, 2, GT, 6], F32, c)
                mv = sb("mv", [P, GUN, GT, 2], F32, c)
                var = sb("var", [P, GUN, GT], F32, c)
                rstd = sb("rstd", [P, GUN, GT], F32, c)
                p_x = [ps(f"p_x{s}", c) for s in range(2)]
                p_1, p_2 = ps("p_1", c), ps("p_2", c)
                p_r1 = [ps(f"p_r1{s}", c) for s in range(2)]
                p_r2 = [ps(f"p_r2{s}", c) for s in range(2)]
                x_loaded = sems("x_loaded", GUN, c)
                h1_stored = sems("h1_stored", GUN, c)
                x1_stored = sems("x1_stored", GUN, c)
                x2_stored = sems("x2_stored", GUN, c)
                x_turned = sem("x_turned", c)
                xT_ready = sem("xT_ready", c)
                prod1, prod2 = sem("prod1", c), sem("prod2", c)
                low1_ready, low2_ready = sem("low1_ready", c), sem("low2_ready", c)
                h1T_ready, h2T_ready = sem("h1T_ready", c), sem("h2T_ready", c)
                h1_turned, h2_turned = sem("h1_turned", c), sem("h2_turned", c)
                h1_ready = sem("h1_ready", c)
                sum_ready = sem("sum_ready", c)
                stats_ready = sem("stats_ready", c)
                mv_ready = sem("mv_ready", c)
                var_ready = sem("var_ready", c)
                rstd_ready = sem("rstd_ready", c)
                x1_ready = sem("x1_ready", c)
                x2_ready = sem("x2_ready", c)
                block = program(c)
                LAG = 6

                def rows(table, t):
                    return table[bass.ds(group_rows(t.n), GROUP), :].rearrange("(p a) d -> p (a d)", a=GT)

                @block.sync
                def _(e):
                    def step(t):
                        if (g := t.ago(0)):
                            wait(e, sum_ready, g.n - GUN + 1)
                            for stored in (h1_stored, x1_stored, x2_stored):
                                gate(e)
                                wait(e, stored[g.k], 16 * g.b)
                            gate(e)
                            e.dma_start(x_in[:, g.k, :], rows(x, g)).then_inc(x_loaded[g.k], 16)
                        if (g := t.ago(4)):
                            if isinstance(g.n, int) and g.n == NG - 1:
                                e.wait_ge(h1_stored[(g.n - 1) % GUN], 16 * ((g.n - 1) // GUN + 1))
                            gate(e)
                            e.wait_ge(h1_ready, g.n + 1)
                            gate(e)
                            e.dma_start(rows(h1_table, g), h1_rows[:, g.k, :]).then_inc(h1_stored[g.k], 16)
                        if (g := t.ago(6)):
                            if isinstance(g.n, int) and g.n == NG - 1:
                                e.wait_ge(x1_stored[(g.n - 1) % GUN], 16 * ((g.n - 1) // GUN + 1))
                                gate(e)
                                e.wait_ge(x2_stored[(g.n - 1) % GUN], 16 * ((g.n - 1) // GUN + 1))
                            gate(e)
                            e.wait_ge(x1_ready, g.n + 1)
                            gate(e)
                            e.dma_start(rows(x1_table, g), x1_rows[:, g.k, :]).then_inc(x1_stored[g.k], 16)
                            e.wait_ge(x2_ready, g.n + 1)
                            gate(e)
                            e.dma_start(rows(x2_table, g), x2_rows[:, g.k, :]).then_inc(x2_stored[g.k], 16)

                    over_tiles(e, NG, GUN, LAG, step)
                    for k in range(GUN):
                        for s in (h1_stored, x1_stored, x2_stored):
                            e.wait_ge(s[k], 16 * len(range(k, NG, GUN)))

                @block.tensor
                def _(e):
                    def step(t):
                        if (g := t.ago(0)):
                            s = g.k % 2
                            e.wait_ge(x_loaded[g.k], 16 * (g.b + 1))
                            wait(e, xT_ready, g.n - 1)
                            for a in range(GT):
                                mm = e.transpose(p_x[s][:, a * P:(a + 1) * P], x_in[:, g.k, a * D:(a + 1) * D], ident[:])
                            mm.then_inc(x_turned, 1)
                        if (g := t.ago(1)):
                            s = g.k % 2
                            e.wait_ge(xT_ready, g.n + 1)
                            wait(e, h1T_ready, g.n)
                            e.matmul(p_1[:], w_el[0][:], xT[:, s, :], start=True, stop=True).then_inc(prod1, 1)
                        if (g := t.ago(2)):
                            s = g.k % 2
                            e.wait_ge(h1T_ready, g.n + 1)
                            wait(e, h2T_ready, g.n)
                            e.matmul(p_2[:], w_el[1][:], h1T[:, s, :], start=True, stop=True).then_inc(prod2, 1)
                            wait(e, h1_ready, g.n - 1)
                            for a in range(GT):
                                mm = e.transpose(p_r1[s][:, a * D:(a + 1) * D], h1T[:, s, a * P:(a + 1) * P], ident[:])
                            mm.then_inc(h1_turned, 1)
                        if (g := t.ago(3)):
                            s = g.k % 2
                            e.wait_ge(h2T_ready, g.n + 1)
                            wait(e, sum_ready, g.n - 1)
                            for a in range(GT):
                                mm = e.transpose(p_r2[s][:, a * D:(a + 1) * D], h2T[:, s, a * P:(a + 1) * P], ident[:])
                            mm.then_inc(h2_turned, 1)

                    over_tiles(e, NG, GUN, LAG, step)

                @block.scalar
                def _(e):
                    def step(t):
                        if (g := t.ago(0)):
                            s = g.k % 2
                            e.wait_ge(x_turned, g.n + 1)
                            wait(e, prod1, g.n - 1)
                            e.activation(xT[:, s, :], p_x[s][:], ACT.Copy).then_inc(xT_ready, 1)
                        if (g := t.ago(1)):
                            s = g.k % 2
                            e.wait_ge(prod1, g.n + 1)
                            wait(e, h1T_ready, g.n - 1)
                            e.activation(low1[:, s, :], p_1[:], ACT.Copy, scale=SLOPE).then_inc(low1_ready, 1)
                        if (g := t.ago(2)):
                            s = g.k % 2
                            e.wait_ge(prod2, g.n + 1)
                            wait(e, h2T_ready, g.n - 1)
                            e.activation(low2[:, s, :], p_2[:], ACT.Copy, scale=SLOPE).then_inc(low2_ready, 1)
                            e.wait_ge(h1_turned, g.n + 1)
                            e.activation(h1_rows[:, g.k, :], p_r1[s][:], ACT.Copy).then_inc(h1_ready, 1)

                    over_tiles(e, NG, GUN, LAG, step)

                @block.vector
                def _(e):
                    def step(t):
                        if (g := t.ago(1)):
                            s = g.k % 2
                            e.wait_ge(low1_ready, g.n + 1)
                            wait(e, prod2, g.n - 1)
                            wait(e, h1_turned, g.n - 1)
                            e.tensor_tensor(h1T[:, s, :], low1[:, s, :], p_1[:], ALU.max).then_inc(h1T_ready, 1)
                        if (g := t.ago(2)):
                            s = g.k % 2
                            e.wait_ge(low2_ready, g.n + 1)
                            wait(e, h2_turned, g.n - 1)
                            e.tensor_tensor(h2T[:, s, :], low2[:, s, :], p_2[:], ALU.max).then_inc(h2T_ready, 1)
                        if (g := t.ago(3)):
                            s = g.k % 2
                            e.wait_ge(h2_turned, g.n + 1)
                            e.tensor_tensor(xs_rows[:, g.k, :], p_r2[s][:], x_in[:, g.k, :], ALU.add).then_inc(sum_ready, 1)
                            e.wait_ge(sum_ready, g.n + 1)
                            for a in range(GT):
                                st = e.bn_stats(stats[:, s, a, :], xs_rows[:, g.k, a * D:(a + 1) * D])
                            st.then_inc(stats_ready, 1)
                            e.wait_ge(stats_ready, g.n + 1)
                            gate(e)
                            for a in range(GT):
                                st = e.bn_aggr(mv[:, g.k, a, :], stats[:, s, a, :])
                            st.then_inc(mv_ready, 1)
                        if (g := t.ago(4)):
                            e.wait_ge(rstd_ready, g.n + 1)
                            for a in range(GT):
                                st = e.tensor_scalar(x1_rows[:, g.k, a * D:(a + 1) * D], xs_rows[:, g.k, a * D:(a + 1) * D],
                                                     mv[:, g.k, a, 0:1], rstd[:, g.k, a:a + 1], ALU.subtract, ALU.mult)
                            st.then_inc(x1_ready, 1)

                    over_tiles(e, NG, GUN, LAG, step)

                @block.gpsimd
                def _(e):
                    def step(t):
                        if (g := t.ago(3)):
                            e.wait_ge(mv_ready, g.n + 1)
                            gate(e)
                            e.tensor_scalar(var[:, g.k, :], mv[:, g.k, :, 1], EPS, None, ALU.add).then_inc(var_ready, 1)
                            e.wait_ge(var_ready, g.n + 1)
                            gate(e)
                            e.tensor_tensor(rstd[:, g.k, :], var[:, g.k, :], minus_half[:], ALU.pow).then_inc(rstd_ready, 1)
                        if (g := t.ago(4)):
                            e.wait_ge(x1_ready, g.n + 1)
                            gate(e)
                            e.tensor_tensor(x2_rows[:, g.k, :].rearrange("p (a d) -> p a d", a=GT),
                                            x1_rows[:, g.k, :].rearrange("p (a d) -> p a d", a=GT),
                                            bo_rows[:].unsqueeze(1).to_broadcast([P, GT, D]), ALU.add).then_inc(x2_ready, 1)

                    over_tiles(e, NG, GUN, LAG, step)

        def layer(l):
            table = (x, h1_table)[l]
            target = (h1_table, x1_table)[l]
            with ExitStack() as c:
                x_src = sb("x_src", [P, MUN, D], F32, c)
                hx = sb("hx", [P, MUN, 2 * D], F32, c)
                x1_out = sb("x1_out", [P, MUN, D], F32, c)
                use = sb("use", [P, MUN, 3], I32, c)
                hot = sb("hot", [P, 2, 2 * P], F32, c)
                hotT = sb("hotT", [P, 2, 2 * P], F32, c)
                acc_n = sb("acc_n", [P, 2, D], F32, c)
                turned = sb("turned", [P, 2, 2 * P], F32, c)
                h_raw = sb("h_raw", [P, 2, D], F32, c)
                h_out = sb("h_out", [P, 2, D], F32, c)
                xs = sb("xs", [P, 4, D], F32, c)
                stats = sb("stats", [P, 2, 6], F32, c)
                mv = sb("mv", [P, 4, 2], F32, c)
                std = sb("std", [P, 2], F32, c)
                rstd = sb("rstd", [P, 2], F32, c)
                p_hot = [ps(f"p_hot{s}", c) for s in range(2)]
                p_msg = [ps(f"p_msg{s}", c) for s in range(2)]
                p_turn = [ps(f"p_turn{s}", c) for s in range(2)]
                p_h = [ps(f"p_h{s}", c) for s in range(2)]
                src_in = gathered
                dst_in = DmaSems(sems("dst_in", MUN, c)) if l else gathered_dst
                stored = sems("stored", MUN, c)
                use_ready = sem("use_ready", c)
                hot_ready = sem("hot_ready", c)
                hot_turned = sem("hot_turned", c)
                hotT_ready = sem("hotT_ready", c)
                msg_ready = sem("msg_ready", c)
                cleared = sem("cleared", c)
                acc_ready = sem("acc_ready", c)
                catch_done = sem("catch_done", c)
                acc_n_ready = sem("acc_n_ready", c)
                both_turned = sem("both_turned", c)
                turned_ready = sem("turned_ready", c)
                h_prod = sem("h_prod", c)
                raw_ready = sem("raw_ready", c)
                h_ready = sem("h_ready", c)
                sum_ready = sem("sum_ready", c)
                stats_ready = sem("stats_ready", c)
                mv_ready = sem("mv_ready", c)
                std_ready = sem("std_ready", c)
                rstd_ready = sem("rstd_ready", c)
                row_ready = sem("row_ready", c) if l else h_ready
                block = program(c)
                OUT_LAG = 11 + 2 * l
                LAG = OUT_LAG + 1

                def tile_rows(t, table):
                    return table[bass.ds(t.n * P, P), :]

                @block.gpsimd
                def _(e):
                    def step(t):
                        if (g := t.ago(0)):
                            wait(e, scattered[g.k], scattered.after(g.b))
                            if l == 0:
                                wait(e, stored[g.k], 16 * g.b)
                            wait(e, msg_ready, g.n - MUN + 1)
                            gate(e)
                            e.tensor_copy(use[:, g.k, :].unsqueeze(2), idx[:, 0:3, bass.ds(g.n, 1)]).then_inc(use_ready, 1)
                            e.wait_ge(use_ready, g.n + 1)
                            gate(e)
                            e.indirect_dma_start(out=x_src[:, g.k, :], out_offset=None, in_=table,
                                                 in_offset=bass.IndirectOffsetOnAxis(ap=use[:, g.k, SRC:SRC + 1], axis=0))\
                                .then_inc(src_in[g.k], 16)
                            if l == 0:
                                e.indirect_dma_start(out=hx[:, g.k, D:2 * D], out_offset=None, in_=x,
                                                     in_offset=bass.IndirectOffsetOnAxis(ap=use[:, g.k, DST:DST + 1], axis=0))\
                                    .then_inc(dst_in[g.k], 16)
                        if (g := t.ago(OUT_LAG)):
                            e.wait_ge(row_ready, g.n + 1)
                            gate(e)
                            rows_out = hx[:, g.k, 0:D] if l == 0 else x1_out[:, g.k, :]
                            e.indirect_dma_start(out=target, in_=rows_out, in_offset=None,
                                                 out_offset=bass.IndirectOffsetOnAxis(ap=use[:, g.k, AT_END:AT_END + 1], axis=0),
                                                 bounds_check=N - 1, oob_is_err=False).then_inc(scattered[g.k], 16)

                    over_tiles(e, COLS, MUN, LAG, step)
                    for k in range(MUN):
                        e.wait_ge(scattered[k], scattered.after(COLS // MUN))

                @block.sync
                def _(e):
                    def step(t):
                        if l == 1 and (g := t.ago(0)):
                            wait(e, row_ready, g.n - MUN + 1)
                            gate(e)
                            wait(e, stored[g.k], 16 * g.b)
                            gate(e)
                            wait(e, scattered[g.k], scattered.after(g.b))
                            gate(e)
                            e.dma_start(hx[:, g.k, :], tile_rows(g, tile_hx)).then_inc(dst_in[g.k], 16)
                        if (g := t.ago(OUT_LAG)):
                            e.wait_ge(row_ready, g.n + 1)
                            if l == 0:
                                e.dma_start(tile_rows(g, tile_hx), hx[:, g.k, :]).then_inc(stored[g.k], 16)
                            else:
                                e.dma_start(tile_rows(g, tile_x1), x1_out[:, g.k, :]).then_inc(stored[g.k], 16)

                    over_tiles(e, COLS, MUN, LAG, step)
                    for k in range(MUN):
                        e.wait_ge(stored[k], 16 * (COLS // MUN))

                @block.tensor
                def _(e):
                    def step(t):
                        if (g := t.ago(1)):
                            s = g.k % 2
                            e.wait_ge(hot_ready, g.n + 1)
                            wait(e, hotT_ready, g.n - 1)
                            for a in range(2):
                                mm = e.transpose(p_hot[s][:, a * P:(a + 1) * P], hot[:, s, a * P:(a + 1) * P], ident[:])
                            mm.then_inc(hot_turned, 1)
                        if (g := t.ago(3)):
                            s = g.k % 2
                            e.wait_ge(hotT_ready, g.n + 1)
                            e.wait_ge(src_in[g.k], src_in.after(g.b + 1))
                            wait(e, acc_ready, g.n - 1)
                            e.matmul(p_msg[s][:, 0:D], hotT[:, s, 0:P], rel[:, 0, :], start=True, stop=False)
                            e.matmul(p_msg[s][:, 0:D], hotT[:, s, P:2 * P], rel[:, 1, :], start=False, stop=False)
                            e.matmul(p_msg[s][:, 0:D], ident[:], x_src[:, g.k, :], start=False, stop=True).then_inc(msg_ready, 1)
                        if (g := t.ago(6)):
                            s = g.k % 2
                            e.wait_ge(acc_n_ready, g.n + 1)
                            e.wait_ge(dst_in[g.k], dst_in.after(g.b + 1))
                            wait(e, turned_ready, g.n - 1)
                            own = hx[:, g.k, D:2 * D] if l == 0 else hx[:, g.k, 0:D]
                            e.transpose(p_turn[s][:, 0:P], acc_n[:, s, :], ident[:])
                            e.transpose(p_turn[s][:, P:2 * P], own, ident[:]).then_inc(both_turned, 1)
                        if (g := t.ago(8)):
                            s = g.k % 2
                            e.wait_ge(turned_ready, g.n + 1)
                            wait(e, raw_ready, g.n - 1)
                            e.matmul(p_h[s][:, 0:D], turned[:, s, 0:P], w_r[l][:], start=True, stop=False)
                            e.matmul(p_h[s][:, 0:D], turned[:, s, P:2 * P], w_sl[l][:], start=False, stop=True).then_inc(h_prod, 1)

                    over_tiles(e, COLS, MUN, LAG, step)

                @block.scalar
                def _(e):
                    def step(t):
                        if (g := t.ago(2)):
                            s = g.k % 2
                            e.wait_ge(hot_turned, g.n + 1)
                            wait(e, msg_ready, g.n - 1)
                            e.activation(hotT[:, s, :], p_hot[s][:, 0:2 * P], ACT.Copy).then_inc(hotT_ready, 1)
                        if (g := t.ago(5)):
                            s = g.k % 2
                            e.wait_ge(acc_ready, g.n + 1)
                            wait(e, both_turned, g.n - 1)
                            e.activation(acc_n[:, s, :], open_acc[:, s, :], ACT.Copy, scale=col(norm, g.n)).then_inc(acc_n_ready, 1)
                        if (g := t.ago(7)):
                            s = g.k % 2
                            e.wait_ge(both_turned, g.n + 1)
                            wait(e, h_prod, g.n - 1)
                            e.activation(turned[:, s, :], p_turn[s][:, 0:2 * P], ACT.Copy).then_inc(turned_ready, 1)
                        if (g := t.ago(9)):
                            s = g.k % 2
                            e.wait_ge(h_prod, g.n + 1)
                            wait(e, h_ready, g.n - 1)
                            e.activation(h_raw[:, s, :], p_h[s][:, 0:D], ACT.Copy).then_inc(raw_ready, 1)
                        if l == 1 and (g := t.ago(11)):
                            s = g.k % 2
                            e.wait_ge(mv_ready, g.n + 1)
                            wait(e, rstd_ready, g.n - 1)
                            e.activation(std[:, s:s + 1], mv[:, g.k % 4, 1:2], ACT.Sqrt, bias=eps[:]).then_inc(std_ready, 1)

                    over_tiles(e, COLS, MUN, LAG, step)

                @block.vector
                def _(e):
                    e.memset(open_acc[:], 0.0).then_inc(cleared, 1)
                    e.memset(caught[:], 0.0).then_inc(cleared, 1)

                    def step(t):
                        if (g := t.ago(10)):
                            s = g.k % 2
                            e.wait_ge(raw_ready, g.n + 1)
                            gate(e)
                            if l == 1:
                                wait(e, sum_ready, g.n - 1)
                            h_rows = hx[:, g.k, 0:D] if l == 0 else h_out[:, s, :]
                            e.scalar_tensor_tensor(out=h_rows, in0=h_raw[:, s, :], scalar=SLOPE, in1=h_raw[:, s, :],
                                                   op0=ALU.mult, op1=ALU.max).then_inc(h_ready, 1)
                        if l == 1 and (g := t.ago(12)):
                            s = g.k % 2
                            e.wait_ge(std_ready, g.n + 1)
                            wait(e, row_ready, g.n - 1)
                            e.reciprocal(rstd[:, s:s + 1], std[:, s:s + 1]).then_inc(rstd_ready, 1)
                        if (g := t.ago(4)):
                            s = g.k % 2
                            e.wait_ge(msg_ready, g.n + 1)
                            if isinstance(g.n, int) and g.n == 0:
                                e.wait_ge(cleared, 2)
                            wait(e, acc_n_ready, g.n - 1)
                            wait(e, acc_ready, g.n)
                            wait(e, catch_done, g.n - 1)
                            gate(e)
                            e.scalar_tensor_tensor(out=open_acc[:, s, :], in0=open_acc[:, 1 - s, :], scalar=col(same_prev, g.n),
                                                   in1=p_msg[s][:, 0:D], op0=ALU.mult, op1=ALU.add).then_inc(acc_ready, 1)
                        if l == 1 and (g := t.ago(10)):
                            s = g.k % 2
                            e.wait_ge(h_ready, g.n + 1)
                            wait(e, row_ready, g.n - 3)
                            e.tensor_tensor(xs[:, g.k % 4, :], h_out[:, s, :], hx[:, g.k, D:2 * D], ALU.add).then_inc(sum_ready, 1)
                        if l == 1 and (g := t.ago(12)):
                            s = g.k % 2
                            e.wait_ge(rstd_ready, g.n + 1)
                            e.tensor_scalar(x1_out[:, g.k, :], xs[:, g.k % 4, :], mv[:, g.k % 4, 0:1], rstd[:, s:s + 1],
                                            ALU.subtract, ALU.mult).then_inc(row_ready, 1)
                        if l == 1 and (g := t.ago(10)):
                            s = g.k % 2
                            e.wait_ge(sum_ready, g.n + 1)
                            e.bn_stats(stats[:, s, :], xs[:, g.k % 4, :]).then_inc(stats_ready, 1)
                        if (g := t.ago(0)):
                            s = g.k % 2
                            wait(e, hot_turned, g.n - 1)
                            gate(e)
                            e.tensor_scalar(hot[:, s, :], rel_ids[:], col(type_f, g.n), None, ALU.is_equal).then_inc(hot_ready, 1)
                        if l == 1 and (g := t.ago(10)):
                            s = g.k % 2
                            e.wait_ge(stats_ready, g.n + 1)
                            gate(e)
                            e.bn_aggr(mv[:, g.k % 4, :], stats[:, s, :]).then_inc(mv_ready, 1)
                        if (g := t.ago(4)):
                            e.wait_ge(acc_ready, g.n + 1)
                            wait(e, catch_done, g.n)
                            gate(e)
                            e.scalar_tensor_tensor(out=caught[:], in0=open_acc[:, g.k % 2, :], scalar=col(cap_end, g.n),
                                                   in1=caught[:], op0=ALU.mult, op1=ALU.add).then_inc(catch_done, 1)

                    over_tiles(e, COLS, MUN, LAG, step)

            gathered.passed(COLS // MUN)
            scattered.passed(COLS // MUN)
            if l == 0:
                gathered_dst.passed(COLS // MUN)

        def layer_border(l):
            with ExitStack() as c:
                acc = sb("acc", [P, D], F32, c)
                acc_n = sb("acc_n", [P, D], F32, c)
                turned = sb("turned", [P, 2 * P], F32, c)
                low = sb("low", [P, D], F32, c)
                h = sb("h", [P, D], F32, c)
                xs = sb("xs", [P, D], F32, c)
                x1 = sb("x1", [P, D], F32, c)
                stats = sb("stats", [P, 6], F32, c)
                mv = sb("mv", [P, 2], F32, c)
                std = sb("std", [P, 1], F32, c)
                rstd = sb("rstd", [P, 1], F32, c)
                p_open = ps("p_open", c)
                p_turn = ps("p_turn", c)
                p_h = ps("p_h", c)
                x_in = border_gathered
                open_ready = sem("open_ready", c)
                acc_ready = sem("acc_ready", c)
                both_turned = sem("both_turned", c)
                turned_ready = sem("turned_ready", c)
                h_prod = sem("h_prod", c)
                low_ready = sem("low_ready", c)
                std_ready = sem("std_ready", c)
                mv_ready = sem("mv_ready", c)
                dve_done = sem("dve_done", c)
                row_ready = sem("row_ready", c)
                block = program(c)

                @block.gpsimd
                def _(e):
                    if l == 0:
                        e.indirect_dma_start(out=border_x[:], out_offset=None, in_=x,
                                             in_offset=bass.IndirectOffsetOnAxis(ap=border[:, RD_FIRST:RD_FIRST + 1], axis=0))\
                            .then_inc(x_in[0], 16)
                    e.wait_ge(row_ready, 1)
                    where = bass.IndirectOffsetOnAxis(ap=border[:, WR_FIRST:WR_FIRST + 1], axis=0)
                    if l == 0:
                        e.indirect_dma_start(out=h1_table, in_=border_h[:], in_offset=None, out_offset=where,
                                             bounds_check=N - 1, oob_is_err=False).then_inc(border_scattered[0], 16)
                        e.wait_ge(border_scattered[0], border_scattered.after(1))
                    else:
                        e.indirect_dma_start(out=x1_table, in_=x1[:], in_offset=None, out_offset=where,
                                             bounds_check=N - 1, oob_is_err=False).then_inc(border_scattered[0], 16)
                        e.indirect_dma_start(out=tile_x1, in_=x1[:], in_offset=None,
                                             out_offset=bass.IndirectOffsetOnAxis(ap=border[:, POS_FIRST:POS_FIRST + 1], axis=0),
                                             bounds_check=ROWS - 1, oob_is_err=False).then_inc(border_scattered[0], 16)
                        e.wait_ge(border_scattered[0], border_scattered.after(2))

                @block.tensor
                def _(e):
                    e.matmul(p_open[:, 0:D], after[:], open_acc[:, (COLS - 1) % 2, :], start=True, stop=True).then_inc(open_ready, 1)
                    e.wait_ge(acc_ready, 1)
                    if l == 0:
                        e.wait_ge(x_in[0], x_in.after(1))
                    e.transpose(p_turn[:, 0:P], acc_n[:], ident[:])
                    e.transpose(p_turn[:, P:2 * P], (border_x, border_h)[l][:], ident[:]).then_inc(both_turned, 1)
                    e.wait_ge(turned_ready, 1)
                    e.matmul(p_h[:, 0:D], turned[:, 0:P], w_r[l][:], start=True, stop=False)
                    e.matmul(p_h[:, 0:D], turned[:, P:2 * P], w_sl[l][:], start=False, stop=True).then_inc(h_prod, 1)

                @block.scalar
                def _(e):
                    e.wait_ge(both_turned, 1)
                    e.activation(turned[:], p_turn[:, 0:2 * P], ACT.Copy).then_inc(turned_ready, 1)
                    e.wait_ge(h_prod, 1)
                    e.activation(low[:], p_h[:, 0:D], ACT.Copy, scale=SLOPE).then_inc(low_ready, 1)
                    if l == 1:
                        e.wait_ge(mv_ready, 1)
                        e.activation(std[:], mv[:, 1:2], ACT.Sqrt, bias=eps[:]).then_inc(std_ready, 1)

                @block.vector
                def _(e):
                    e.wait_ge(open_ready, 1)
                    e.tensor_tensor(acc[:], p_open[:, 0:D], caught[:], ALU.add).then_inc(dve_done, 1)
                    e.wait_ge(dve_done, 1)
                    e.tensor_scalar(acc_n[:], acc[:], border_norm[:], None, ALU.mult).then_inc(acc_ready, 1)
                    e.wait_ge(low_ready, 1)
                    if l == 0:
                        e.tensor_tensor(border_h[:], low[:], p_h[:, 0:D], ALU.max).then_inc(row_ready, 1)
                        return
                    e.tensor_tensor(h[:], low[:], p_h[:, 0:D], ALU.max).then_inc(dve_done, 1)
                    e.wait_ge(dve_done, 2)
                    e.tensor_tensor(xs[:], h[:], border_x[:], ALU.add).then_inc(dve_done, 1)
                    e.wait_ge(dve_done, 3)
                    e.bn_stats(stats[:], xs[:]).then_inc(dve_done, 1)
                    e.wait_ge(dve_done, 4)
                    e.bn_aggr(mv[:], stats[:]).then_inc(mv_ready, 1)
                    e.wait_ge(std_ready, 1)
                    e.reciprocal(rstd[:], std[:]).then_inc(dve_done, 1)
                    e.wait_ge(dve_done, 5)
                    e.tensor_scalar(x1[:], xs[:], mv[:, 0:1], rstd[:], ALU.subtract, ALU.mult).then_inc(row_ready, 1)

            if l == 0:
                border_gathered.passed(1)
            border_scattered.passed(1 + l)

        def attention(values, logits):
            with ExitStack() as c:
                x_src = sb("x_src", [P, UN, D], F32, c)
                x_end = sb("x_end", [P, UN, D], F32, c)
                at_end = sb("at_end", [P, 2, D], F32, c)
                xv_dst = sb("xv_dst", [P, UN, 2, D], F32, c)
                qk = sb("qk", [P, 2, 3, D], F32, c)
                use = sb("use", [P, UN, 1], I32, c)
                x_open = sb("x_open", [P, D], F32, c)
                stats = sb("stats", [P, 2, 2, 6], F32, c)
                mv = sb("mv", [P, 4, 2, 2], F32, c)
                std = sb("std", [P, 2, 2], F32, c)
                rstd = sb("rstd", [P, 2, 2], F32, c)
                shift = sb("shift", [P, 2, 2], F32, c)
                normed = sb("normed", [P, 2, 2, D], F32, c)
                turned = sb("turned", [P, 2, 2 * P], F32, c)
                prod = sb("prod", [P, 2, 2, D], F32, c)
                p_turn = [ps(f"p_turn{s}", c) for s in range(2)]
                p_qk = [ps(f"p_qk{s}", c) for s in range(2)]
                p_v = [ps(f"p_v{s}", c) for s in range(2)]
                open_in = border_gathered
                src_in = x1_gathered
                end_in = sems("end_in", UN, c)
                stored = sems("stored", UN, c)
                use_ready = sem("use_ready", c)
                at_end_ready = sem("at_end_ready", c)
                x_ready = sem("x_ready", c)
                stats_ready = sem("stats_ready", c)
                mv_ready = sem("mv_ready", c)
                std_ready = sem("std_ready", c)
                rstd_ready = sem("rstd_ready", c)
                shift_ready = sem("shift_ready", c)
                normed_ready = sem("normed_ready", c)
                both_turned = sem("both_turned", c)
                turned_ready = sem("turned_ready", c)
                qkv_ready = sem("qkv_ready", c)
                qk_out = sem("qk_out", c)
                v_out = sem("v_out", c)
                prod_ready = sem("prod_ready", c)
                logit_ready = sem("logit_ready", c)
                block = program(c)
                LAG = 11

                def j(g):
                    return COLS - 1 - g.n

                @block.gpsimd
                def _(e):
                    e.indirect_dma_start(out=x_open[:], out_offset=None, in_=x1_table,
                                         in_offset=bass.IndirectOffsetOnAxis(ap=border[:, RD_LAST:RD_LAST + 1], axis=0))\
                        .then_inc(open_in[0], 16)

                    def step(t):
                        if (g := t.ago(0)):
                            wait(e, normed_ready, g.n - UN + 1)
                            gate(e)
                            e.tensor_copy(use[:, g.k, :], col(idx[:, SRC, :], j(g))).then_inc(use_ready, 1)
                            e.wait_ge(use_ready, g.n + 1)
                            gate(e)
                            e.indirect_dma_start(out=x_src[:, g.k, :], out_offset=None, in_=x1_table,
                                                 in_offset=bass.IndirectOffsetOnAxis(ap=use[:, g.k, 0:1], axis=0))\
                                .then_inc(src_in[g.k], 16)

                    over_tiles(e, COLS, UN, LAG, step, peeled=2)

                @block.sync
                def _(e):
                    def step(t):
                        if (g := t.ago(10)):
                            e.wait_ge(v_out, g.n + 1)
                            gate(e)
                            e.wait_ge(x_ready, g.n + 1)
                            gate(e)
                            e.dma_start(tile_xv[bass.ds(j(g) * P, P), :],
                                        xv_dst[:, g.k, :, :].rearrange("p a d -> p (a d)")).then_inc(stored[g.k], 16)
                        if (g := t.ago(0)):
                            wait(e, at_end_ready, g.n - UN + 1)
                            gate(e)
                            e.dma_start(x_end[:, g.k, :], tile_x1[bass.ds(j(g) * P, P), :]).then_inc(end_in[g.k], 16)

                    over_tiles(e, COLS, UN, LAG, step, peeled=2)
                    for k in range(UN):
                        e.wait_ge(stored[k], 16 * (COLS // UN))

                @block.tensor
                def _(e):
                    def step(t):
                        if (g := t.ago(8)):
                            s = g.k % 2
                            e.wait_ge(turned_ready, g.n + 1)
                            wait(e, qk_out, g.n - 1)
                            wait(e, v_out, g.n - 1)
                            dst_T, src_T = turned[:, s, 0:P], turned[:, s, P:2 * P]
                            e.matmul(p_qk[s][:, 0:2 * D], dst_T, w_vqk[:, D:3 * D], start=True, stop=True)
                            e.matmul(p_v[s][:, 0:D], dst_T, w_vqk[:, 0:D], start=True, stop=True)
                            e.matmul(p_qk[s][:, 2 * D:3 * D], src_T, w_vqk[:, 2 * D:3 * D], start=True, stop=True)
                            e.matmul(p_v[s][:, D:2 * D], src_T, w_vqk[:, 0:D], start=True, stop=True).then_inc(qkv_ready, 1)
                        if (g := t.ago(6)):
                            s = g.k % 2
                            e.wait_ge(normed_ready, g.n + 1)
                            wait(e, turned_ready, g.n - 1)
                            for a in range(2):
                                mm = e.transpose(p_turn[s][:, a * P:(a + 1) * P], normed[:, s, a, :], ident[:])
                            mm.then_inc(both_turned, 1)

                    over_tiles(e, COLS, UN, LAG, step, peeled=2)

                @block.scalar
                def _(e):
                    def step(t):
                        if (g := t.ago(1)):
                            s = g.k % 2
                            e.wait_ge(end_in[g.k], 16 * (g.b + 1))
                            wait(e, x_ready, g.n - 1)
                            e.activation(at_end[:, s, :], x_end[:, g.k, :], ACT.Copy, scale=col(is_end, j(g)))\
                                .then_inc(at_end_ready, 1)
                        if (g := t.ago(3)):
                            s = g.k % 2
                            e.wait_ge(mv_ready, g.n + 1)
                            wait(e, rstd_ready, g.n - 1)
                            e.activation(std[:, s, :], mv[:, g.k % 4, :, 1], ACT.Sqrt, bias=eps[:]).then_inc(std_ready, 1)
                        if (g := t.ago(5)):
                            s = g.k % 2
                            e.wait_ge(shift_ready, g.n + 1)
                            wait(e, both_turned, g.n - 1)
                            for a, row in ((0, xv_dst[:, g.k, 0, :]), (1, x_src[:, g.k, :])):
                                ins = e.activation(normed[:, s, a, :], row, ACT.Identity, scale=rstd[:, s, a:a + 1],
                                                   bias=shift[:, s, a:a + 1])
                            ins.then_inc(normed_ready, 1)
                        if (g := t.ago(7)):
                            s = g.k % 2
                            e.wait_ge(both_turned, g.n + 1)
                            wait(e, qkv_ready, g.n - 1)
                            e.activation(turned[:, s, :], p_turn[s][:, 0:2 * P], ACT.Copy).then_inc(turned_ready, 1)
                        if (g := t.ago(9)):
                            s = g.k % 2
                            e.wait_ge(qkv_ready, g.n + 1)
                            e.activation(xv_dst[:, g.k, 1, :], p_v[s][:, 0:D], ACT.Copy)
                            e.activation(values[:, bass.ds(j(g), 1), :].rearrange("p a d -> p (a d)"), p_v[s][:, D:2 * D], ACT.Copy)\
                                .then_inc(v_out, 1)

                    over_tiles(e, COLS, UN, LAG, step, peeled=2)

                @block.vector
                def _(e):
                    def step(t):
                        if (g := t.ago(4)):
                            s = g.k % 2
                            e.wait_ge(std_ready, g.n + 1)
                            wait(e, normed_ready, g.n - 1)
                            e.reciprocal(rstd[:, s, :], std[:, s, :]).then_inc(rstd_ready, 1)
                        if (g := t.ago(9)):
                            s = g.k % 2
                            e.wait_ge(qkv_ready, g.n + 1)
                            wait(e, prod_ready, g.n - 1)
                            e.tensor_tensor(qk[:, s, :, :].rearrange("p a d -> p (a d)"),
                                            p_qk[s][:, 0:3 * D], bias_vqk[:, D:4 * D], ALU.add).then_inc(qk_out, 1)
                        if (g := t.ago(4)):
                            s = g.k % 2
                            e.wait_ge(rstd_ready, g.n + 1)
                            e.scalar_tensor_tensor(out=shift[:, s, :], in0=mv[:, g.k % 4, :, 0], scalar=-1.0, in1=rstd[:, s, :],
                                                   op0=ALU.mult, op1=ALU.mult).then_inc(shift_ready, 1)
                        if (g := t.ago(2)):
                            s = g.k % 2
                            e.wait_ge(at_end_ready, g.n + 1)
                            if isinstance(g.n, int) and g.n == 0:
                                e.wait_ge(open_in[0], open_in.after(1))
                                before_row = x_open[:]
                            else:
                                before_row = xv_dst[:, (g.k - 1) % UN, 0, :]
                            wait(e, stored[g.k], 16 * g.b)
                            wait(e, x_ready, g.n)
                            gate(e)
                            e.scalar_tensor_tensor(out=xv_dst[:, g.k, 0, :], in0=before_row, scalar=col(keep_x, j(g)),
                                                   in1=at_end[:, s, :], op0=ALU.mult, op1=ALU.add).then_inc(x_ready, 1)
                        if (g := t.ago(9)):
                            s = g.k % 2
                            e.wait_ge(qk_out, g.n + 1)
                            wait(e, logit_ready, g.n - 1)
                            e.tensor_tensor(prod[:, s, :, :], qk[:, s, 1:3, :],
                                            qk[:, s, 0:1, :].to_broadcast([P, 2, D]), ALU.mult).then_inc(prod_ready, 1)
                        if (g := t.ago(2)):
                            s = g.k % 2
                            e.wait_ge(x_ready, g.n + 1)
                            e.wait_ge(src_in[g.k], src_in.after(g.b + 1))
                            wait(e, mv_ready, g.n - 1)
                            e.bn_stats(stats[:, s, 0, :], xv_dst[:, g.k, 0, :])
                            e.bn_stats(stats[:, s, 1, :], x_src[:, g.k, :]).then_inc(stats_ready, 1)
                        if (g := t.ago(9)):
                            s = g.k % 2
                            e.wait_ge(prod_ready, g.n + 1)
                            gate(e)
                            e.tensor_reduce(logits[:, :, bass.ds(j(g), 1)].rearrange("p h a -> p (h a)"),
                                            prod[:, s, :, :].rearrange("p a (h d) -> p (a h) d", h=HEADS), AX_X, ALU.add)\
                                .then_inc(logit_ready, 1)
                        if (g := t.ago(2)):
                            s = g.k % 2
                            e.wait_ge(stats_ready, g.n + 1)
                            wait(e, shift_ready, g.n - 3)
                            wait(e, std_ready, g.n - 3)
                            gate(e)
                            for a in range(2):
                                ins = e.bn_aggr(mv[:, g.k % 4, a, :], stats[:, s, a, :])
                            ins.then_inc(mv_ready, 1)

                    over_tiles(e, COLS, UN, LAG, step, peeled=2)

            x1_gathered.passed(COLS // UN)
            border_gathered.passed(1)

        def softmax(logits, weight, z_inv, self_weight, border_z):
            SCALE = 1.0 / HD ** 0.5
            with ExitStack() as c:
                both = sb("both", [P, HEADS, COLS], F32, c)
                gap_prev = sb("gap_prev", [P, HEADS, COLS], F32, c)
                gap_next = sb("gap_next", [P, HEADS, COLS], F32, c)
                top = z_inv
                top_next = self_weight
                sides = sb("sides", [P, 2, HEADS], F32, c)
                all_sides = sb("all_sides", [P, 2 * P, HEADS], F32, c)
                miss = sb("miss", [P, 2, 2 * P], F32, c)
                cand = sb("cand", [P, HEADS, 2 * P], F32, c)
                top_side = sb("top_side", [P, 2, HEADS], F32, c)
                dve_done = sem("dve_done", c)
                sides_ready = sem("sides_ready", c)
                sides_out = sem("sides_out", c)
                sides_in = sem("sides_in", c)
                gaps_ready = sem("gaps_ready", c)
                exp_done = sem("exp_done", c)
                block = program(c)
                self_logit, edge_logit = logits[:, 0:HEADS, :], logits[:, HEADS:2 * HEADS, :]

                def flat(t):
                    return t[:].rearrange("p h j -> p (h j)")

                def over_heads(mask):
                    return mask[:].unsqueeze(1).to_broadcast([P, HEADS, COLS])

                @block.sync
                def _(e):
                    e.wait_ge(sides_ready, 1)
                    for s in range(2):
                        e.dma_start(open_max[s * P:(s + 1) * P, :], sides[:, s, :]).then_inc(sides_out, 16)
                    e.wait_ge(sides_out, 32)
                    e.dma_start(all_sides[:].rearrange("p q h -> p (q h)"),
                                open_max.rearrange("q h -> (q h)").partition_broadcast(P)).then_inc(sides_in, 16)

                @block.scalar
                def _(e):
                    e.wait_ge(gaps_ready, 1)
                    e.activation(flat(weight), flat(both), ACT.Exp, scale=SCALE).then_inc(exp_done, 1)
                    e.activation(flat(self_weight), flat(gap_prev), ACT.Exp, scale=SCALE).then_inc(exp_done, 1)

                @block.vector
                def _(e):
                    made = [0]

                    def chain(ins):
                        made[0] += 1
                        ins.then_inc(dve_done, 1)
                        e.wait_ge(dve_done, made[0])

                    e.tensor_scalar(gap_prev[:], over_heads(same_prev), -1.0, LOW, ALU.add, ALU.mult)
                    e.tensor_scalar(gap_next[:], over_heads(same_next), -1.0, LOW, ALU.add, ALU.mult)
                    chain(e.tensor_tensor(both[:], self_logit, edge_logit, ALU.max))
                    e.tensor_tensor_scan(flat(top), flat(gap_prev), flat(both), -LOW, ALU.add, ALU.max)
                    chain(e.tensor_tensor_scan(flat(top_next)[:, ::-1], flat(gap_next)[:, ::-1], flat(both)[:, ::-1], -LOW,
                                               ALU.add, ALU.max))
                    e.tensor_copy(sides[:, 0, :], top_next[:, :, 0])
                    e.tensor_copy(sides[:, 1, :], top[:, :, COLS - 1]).then_inc(sides_ready, 1)
                    e.wait_ge(sides_ready, 1)
                    chain(e.tensor_tensor(flat(top), flat(top), flat(top_next), ALU.max))
                    for s in range(2):
                        ins = e.tensor_scalar(miss[:, s, :], first_last[:], dst_fl[:, s:s + 1], None, ALU.is_equal)
                    chain(ins)
                    e.wait_ge(sides_in, 16)
                    for s in range(2):
                        chain(e.tensor_scalar(miss[:, s, :], miss[:, s, :], -1.0, LOW, ALU.add, ALU.mult))
                        chain(e.tensor_tensor(cand[:], all_sides[:].rearrange("p q h -> p h q"),
                                              miss[:, s, :].unsqueeze(1).to_broadcast([P, HEADS, 2 * P]), ALU.add))
                        chain(e.tensor_reduce(top_side[:, s, :], cand[:], AX_X, ALU.max))
                    for s, inside in enumerate((in_first, in_last)):
                        for h in range(HEADS):
                            ins = e.scalar_tensor_tensor(out=top[:, h, :], in0=inside[:], scalar=top_side[:, s, h:h + 1],
                                                         in1=top[:, h, :], op0=ALU.add, op1=ALU.max)
                        chain(ins)
                    e.tensor_tensor(both[:], edge_logit, top[:], ALU.subtract)
                    e.tensor_tensor(gap_prev[:], self_logit, top[:], ALU.subtract).then_inc(gaps_ready, 1)
                    chain(e.tensor_copy(gap_next[:], over_heads(same_next)))
                    e.wait_ge(exp_done, 2)
                    z = z_inv
                    chain(e.tensor_tensor_scan(flat(z)[:, ::-1], flat(gap_next)[:, ::-1], flat(weight)[:, ::-1], 0.0,
                                               ALU.mult, ALU.add))
                    chain(e.tensor_tensor(both[:], z[:], over_heads(cap_start), ALU.mult))
                    e.tensor_reduce(border_z[:, 0, :], both[:], AX_X, ALU.add)
                    e.tensor_copy(border_z[:, 1, :], z[:, :, 0])
                    chain(e.tensor_tensor(gap_prev[:], self_weight[:], over_heads(cap_start), ALU.mult))
                    e.tensor_reduce(border_z[:, 2, :], gap_prev[:], AX_X, ALU.add)
                    chain(e.tensor_tensor(flat(z), flat(z), flat(self_weight), ALU.add))
                    chain(e.tensor_scalar(flat(z), flat(z), 1e-30, None, ALU.max))
                    chain(e.reciprocal(flat(z_inv), flat(z)))
                    chain(e.tensor_tensor(flat(self_weight), flat(self_weight), flat(z_inv), ALU.mult))

        def weighted(values, weight, z_inv, self_weight):
            with ExitStack() as c:
                xv = sb("xv", [P, UN, 2 * D], F32, c)
                use = sb("use", [P, UN, 1], I32, c)
                x_bias = sb("x_bias", [P, UN, D], F32, c)
                own = sb("own", [P, 2, D], F32, c)
                wv = sb("wv", [P, 2, D], F32, c)
                scaled = sb("scaled", [P, 2, D], F32, c)
                attT = sb("attT", [P, 2, P], F32, c)
                x2_out = sb("x2_out", [P, UN, D], F32, c)
                p_sum = [ps(f"p_sum{s}", c) for s in range(2)]
                p_out = [ps(f"p_out{s}", c) for s in range(2)]
                xv_in = sems("xv_in", UN, c)
                use_ready = sem("use_ready", c)
                x_bias_ready = sem("x_bias_ready", c)
                own_ready = sem("own_ready", c)
                cleared = sem("cleared", c)
                wv_ready = sem("wv_ready", c)
                acc_ready = sem("acc_ready", c)
                catch_done = sem("catch_done", c)
                scaled_ready = sem("scaled_ready", c)
                sum_ready = sem("sum_ready", c)
                attT_ready = sem("attT_ready", c)
                prod_ready = sem("prod_ready", c)
                row_ready = sem("row_ready", c)
                block = program(c)
                LAG = 7

                def j(g):
                    return COLS - 1 - g.n

                @block.sync
                def _(e):
                    def step(t):
                        if (g := t.ago(0)):
                            wait(e, row_ready, g.n - UN + 1)
                            gate(e)
                            wait(e, x2_scattered[g.k], x2_scattered.after(g.b))
                            gate(e)
                            e.dma_start(xv[:, g.k, :], tile_xv[bass.ds(j(g) * P, P), :]).then_inc(xv_in[g.k], 16)

                    over_tiles(e, COLS, UN, LAG, step)

                @block.gpsimd
                def _(e):
                    def step(t):
                        if (g := t.ago(0)):
                            e.wait_ge(xv_in[g.k], 16 * (g.b + 1))
                            gate(e)
                            e.tensor_copy(use[:, g.k, :], col(idx[:, AT_START, :], j(g))).then_inc(use_ready, 1)
                            e.tensor_tensor(x_bias[:, g.k, :], xv[:, g.k, 0:D], att_bias[:], ALU.add).then_inc(x_bias_ready, 1)
                        if (g := t.ago(6)):
                            e.wait_ge(use_ready, g.n + 1)
                            e.wait_ge(row_ready, g.n + 1)
                            gate(e)
                            e.indirect_dma_start(out=x2_table, in_=x2_out[:, g.k, :], in_offset=None,
                                                 out_offset=bass.IndirectOffsetOnAxis(ap=use[:, g.k, 0:1], axis=0),
                                                 bounds_check=N - 1, oob_is_err=False).then_inc(x2_scattered[g.k], 16)

                    over_tiles(e, COLS, UN, LAG, step)
                    for k in range(UN):
                        e.wait_ge(x2_scattered[k], x2_scattered.after(COLS // UN))

                @block.vector
                def _(e):
                    e.memset(open_acc[:], 0.0).then_inc(cleared, 1)
                    e.memset(caught[:], 0.0).then_inc(cleared, 1)

                    def step(t):
                        if (g := t.ago(0)):
                            s = g.k % 2
                            wait(e, acc_ready, g.n - 1)
                            gate(e)
                            e.tensor_tensor(heads(wv[:, s, :]), heads(values[:, bass.ds(j(g), 1), :].rearrange("p a d -> p (a d)")),
                                            per_head(weight, j(g)), ALU.mult).then_inc(wv_ready, 1)
                        if (g := t.ago(1)):
                            s = g.k % 2
                            e.wait_ge(acc_ready, g.n + 1)
                            wait(e, sum_ready, g.n - 1)
                            gate(e)
                            e.tensor_tensor(heads(scaled[:, s, :]), heads(open_acc[:, s, :]), per_head(z_inv, j(g)), ALU.mult)\
                                .then_inc(scaled_ready, 1)
                        if (g := t.ago(0)):
                            s = g.k % 2
                            e.wait_ge(wv_ready, g.n + 1)
                            if isinstance(g.n, int) and g.n == 0:
                                e.wait_ge(cleared, 2)
                            wait(e, acc_ready, g.n)
                            wait(e, scaled_ready, g.n - 1)
                            wait(e, catch_done, g.n - 1)
                            gate(e)
                            e.scalar_tensor_tensor(out=open_acc[:, s, :], in0=open_acc[:, 1 - s, :], scalar=col(same_next, j(g)),
                                                   in1=wv[:, s, :], op0=ALU.mult, op1=ALU.add).then_inc(acc_ready, 1)
                        if (g := t.ago(5)):
                            s = g.k % 2
                            e.wait_ge(prod_ready, g.n + 1)
                            e.wait_ge(x_bias_ready, g.n + 1)
                            e.tensor_tensor(x2_out[:, g.k, :], p_out[s][:, 0:D], x_bias[:, g.k, :], ALU.add).then_inc(row_ready, 1)
                        if (g := t.ago(1)):
                            s = g.k % 2
                            e.wait_ge(xv_in[g.k], 16 * (g.b + 1))
                            gate(e)
                            e.tensor_tensor(heads(own[:, s, :]), heads(xv[:, g.k, D:2 * D]), per_head(self_weight, j(g)), ALU.mult)\
                                .then_inc(own_ready, 1)
                        if (g := t.ago(0)):
                            s = g.k % 2
                            e.wait_ge(acc_ready, g.n + 1)
                            wait(e, catch_done, g.n)
                            gate(e)
                            e.scalar_tensor_tensor(out=caught[:], in0=open_acc[:, s, :], scalar=col(cap_start, j(g)),
                                                   in1=caught[:], op0=ALU.mult, op1=ALU.add).then_inc(catch_done, 1)

                    over_tiles(e, COLS, UN, LAG, step)

                @block.tensor
                def _(e):
                    def step(t):
                        if (g := t.ago(2)):
                            s = g.k % 2
                            e.wait_ge(scaled_ready, g.n + 1)
                            e.wait_ge(own_ready, g.n + 1)
                            wait(e, attT_ready, g.n - 1)
                            e.matmul(p_sum[s][:, 0:P], scaled[:, s, :], ident[:], start=True, stop=False)
                            e.matmul(p_sum[s][:, 0:P], own[:, s, :], ident[:], start=False, stop=True).then_inc(sum_ready, 1)
                        if (g := t.ago(4)):
                            s = g.k % 2
                            e.wait_ge(attT_ready, g.n + 1)
                            wait(e, row_ready, g.n - 1)
                            e.matmul(p_out[s][:, 0:D], attT[:, s, :], w_o[:], start=True, stop=True).then_inc(prod_ready, 1)

                    over_tiles(e, COLS, UN, LAG, step)

                @block.scalar
                def _(e):
                    def step(t):
                        if (g := t.ago(3)):
                            s = g.k % 2
                            e.wait_ge(sum_ready, g.n + 1)
                            wait(e, prod_ready, g.n - 1)
                            e.activation(attT[:, s, :], p_sum[s][:, 0:P], ACT.Copy).then_inc(attT_ready, 1)

                    over_tiles(e, COLS, UN, LAG, step)

            x2_scattered.passed(COLS // UN)

        def weighted_border(border_z):
            with ExitStack() as c:
                xv = sb("xv", [P, 2 * D], F32, c)
                acc = sb("acc", [P, D], F32, c)
                own = sb("own", [P, D], F32, c)
                z = sb("z", [P, HEADS], F32, c)
                x_bias = sb("x_bias", [P, D], F32, c)
                attT = sb("attT", [P, P], F32, c)
                x2 = sb("x2", [P, D], F32, c)
                p_open = ps("p_open", c)
                p_z = ps("p_z", c)
                p_turn = ps("p_turn", c)
                p_out = ps("p_out", c)
                xv_in = border_gathered
                open_ready = sem("open_ready", c)
                dve_done = sem("dve_done", c)
                att_ready = sem("att_ready", c)
                att_turned = sem("att_turned", c)
                attT_ready = sem("attT_ready", c)
                prod_ready = sem("prod_ready", c)
                row_ready = sem("row_ready", c)
                block = program(c)

                @block.gpsimd
                def _(e):
                    e.indirect_dma_start(out=xv[:], out_offset=None, in_=tile_xv,
                                         in_offset=bass.IndirectOffsetOnAxis(ap=border[:, POS_LAST:POS_LAST + 1], axis=0))\
                        .then_inc(xv_in[0], 16)
                    e.wait_ge(row_ready, 1)
                    e.indirect_dma_start(out=x2_table, in_=x2[:], in_offset=None,
                                         out_offset=bass.IndirectOffsetOnAxis(ap=border[:, WR_LAST:WR_LAST + 1], axis=0),
                                         bounds_check=N - 1, oob_is_err=False).then_inc(border_scattered[0], 16)
                    e.wait_ge(border_scattered[0], border_scattered.after(1))

                @block.tensor
                def _(e):
                    e.matmul(p_open[:, 0:D], before[:], open_acc[:, (COLS - 1) % 2, :], start=True, stop=True)
                    e.matmul(p_z[:, 0:HEADS], before[:], border_z[:, 1, :], start=True, stop=True).then_inc(open_ready, 1)
                    e.wait_ge(att_ready, 1)
                    e.transpose(p_turn[:, 0:P], acc[:], ident[:]).then_inc(att_turned, 1)
                    e.wait_ge(attT_ready, 1)
                    e.matmul(p_out[:, 0:D], attT[:], w_o[:], start=True, stop=True).then_inc(prod_ready, 1)

                @block.scalar
                def _(e):
                    e.wait_ge(att_turned, 1)
                    e.activation(attT[:], p_turn[:, 0:P], ACT.Copy).then_inc(attT_ready, 1)

                @block.vector
                def _(e):
                    made = [0]

                    def chain(ins):
                        made[0] += 1
                        ins.then_inc(dve_done, 1)
                        e.wait_ge(dve_done, made[0])

                    def wide(w):
                        return w.unsqueeze(2).to_broadcast([P, HEADS, HD])

                    e.wait_ge(open_ready, 1)
                    e.wait_ge(xv_in[0], xv_in.after(1))
                    chain(e.tensor_tensor(acc[:], caught[:], p_open[:, 0:D], ALU.add))
                    chain(e.tensor_tensor(z[:], border_z[:, 0, :], p_z[:, 0:HEADS], ALU.add))
                    chain(e.tensor_tensor(z[:], z[:], border_z[:, 2, :], ALU.add))
                    chain(e.tensor_scalar(z[:], z[:], 1e-30, None, ALU.max))
                    chain(e.reciprocal(z[:], z[:]))
                    chain(e.tensor_tensor(heads(own[:]), heads(xv[:, D:2 * D]), wide(border_z[:, 2, :]), ALU.mult))
                    chain(e.tensor_tensor(acc[:], acc[:], own[:], ALU.add))
                    e.tensor_tensor(heads(acc[:]), heads(acc[:]), wide(z[:]), ALU.mult).then_inc(att_ready, 1)
                    chain(e.tensor_tensor(x_bias[:], xv[:, 0:D], att_bias[:], ALU.add))
                    e.wait_ge(prod_ready, 1)
                    e.tensor_tensor(x2[:], p_out[:, 0:D], x_bias[:], ALU.add).then_inc(row_ready, 1)

        def ffn():
            with ExitStack() as c:
                x1_in = sb("x1_in", [P, GUN, GROUP], F32, c)
                x2_in = sb("x2_in", [P, GUN, GROUP], F32, c)
                both = sb("both", [P, GUN, GROUP], F32, c)
                normed = sb("normed", [P, 2, GROUP], F32, c)
                nT = sb("nT", [P, 2, GROUP], F32, c)
                g_T = sb("g_T", [P, 2, FCH, GROUP], F32, c)
                yT = sb("yT", [P, 2, GROUP], F32, c)
                ys = sb("ys", [P, GUN, GROUP], F32, c)
                res = sb("res", [P, GUN, GROUP], F32, c)
                stats = sb("stats", [P, 2, GT, 6], F32, c)
                mv = sb("mv", [P, GUN, GT, 2], F32, c)
                var = sb("var", [P, GUN, GT], F32, c)
                rstd = sb("rstd", [P, GUN, GT], F32, c)
                stats2 = sb("stats2", [P, 2, GT, 6], F32, c)
                mv2 = sb("mv2", [P, GUN, GT, 2], F32, c)
                var2 = sb("var2", [P, GUN, GT], F32, c)
                rstd2 = sb("rstd2", [P, GUN, GT], F32, c)
                p_n = ps("p_n", c)
                p_f = [ps(f"p_f{s}", c) for s in range(4)]
                p_y = ps("p_y", c)
                p_r = [ps(f"p_r{s}", c) for s in range(2)]
                x1_loaded = sems("x1_loaded", GUN, c)
                x2_loaded = sems("x2_loaded", GUN, c)
                stored = sems("stored", GUN, c)
                both_ready = sem("both_ready", c)
                stats_ready = sem("stats_ready", c)
                mv_ready = sem("mv_ready", c)
                var_ready = sem("var_ready", c)
                rstd_ready = sem("rstd_ready", c)
                normed_ready = sem("normed_ready", c)
                n_turned = sem("n_turned", c)
                nT_ready = sem("nT_ready", c)
                f_prod = sem("f_prod", c)
                gelu_ready = sem("gelu_ready", c)
                y_prod = sem("y_prod", c)
                yT_ready = sem("yT_ready", c)
                y_turned = sem("y_turned", c)
                sum_ready = sem("sum_ready", c)
                stats2_ready = sem("stats2_ready", c)
                mv2_ready = sem("mv2_ready", c)
                var2_ready = sem("var2_ready", c)
                rstd2_ready = sem("rstd2_ready", c)
                res_ready = sem("res_ready", c)
                block = program(c)
                LAG = 7

                def rows(table, t):
                    return table[bass.ds(group_rows(t.n), GROUP), :].rearrange("(p a) d -> p (a d)", a=GT)

                @block.sync
                def _(e):
                    def step(t):
                        if (g := t.ago(0)):
                            wait(e, both_ready, g.n - GUN + 1)
                            gate(e)
                            wait(e, normed_ready, g.n - GUN + 1)
                            gate(e)
                            wait(e, stored[g.k], 16 * g.b)
                            gate(e)
                            e.dma_start(x2_in[:, g.k, :], rows(x2_table, g)).then_inc(x2_loaded[g.k], 16)
                            e.dma_start(x1_in[:, g.k, :], rows(x1_table, g)).then_inc(x1_loaded[g.k], 16)
                        if (g := t.ago(7)):
                            if isinstance(g.n, int) and g.n == NG - 1:
                                e.wait_ge(stored[(g.n - 1) % GUN], 16 * ((g.n - 1) // GUN + 1))
                            gate(e)
                            e.wait_ge(res_ready, g.n + 1)
                            gate(e)
                            e.dma_start(rows(out, g), res[:, g.k, :]).then_inc(stored[g.k], 16)

                    over_tiles(e, NG, GUN, LAG, step)
                    for k in range(GUN):
                        e.wait_ge(stored[k], 16 * len(range(k, NG, GUN)))

                @block.gpsimd
                def _(e):
                    def step(t):
                        if (g := t.ago(0)):
                            e.wait_ge(mv_ready, g.n + 1)
                            gate(e)
                            e.tensor_scalar(var[:, g.k, :], mv[:, g.k, :, 1], EPS, None, ALU.add).then_inc(var_ready, 1)
                            e.wait_ge(var_ready, g.n + 1)
                            gate(e)
                            e.tensor_tensor(rstd[:, g.k, :], var[:, g.k, :], minus_half[:], ALU.pow).then_inc(rstd_ready, 1)
                            e.wait_ge(x1_loaded[g.k], 16 * (g.b + 1))
                            e.wait_ge(x2_loaded[g.k], 16 * (g.b + 1))
                            wait(e, sum_ready, g.n - GUN + 1)
                            gate(e)
                            e.tensor_tensor(both[:, g.k, :], x1_in[:, g.k, :], x2_in[:, g.k, :], ALU.add).then_inc(both_ready, 1)
                        if (g := t.ago(4)):
                            e.wait_ge(mv2_ready, g.n + 1)
                            gate(e)
                            e.tensor_scalar(var2[:, g.k, :], mv2[:, g.k, :, 1], EPS, None, ALU.add).then_inc(var2_ready, 1)
                            e.wait_ge(var2_ready, g.n + 1)
                            gate(e)
                            e.tensor_tensor(rstd2[:, g.k, :], var2[:, g.k, :], minus_half[:], ALU.pow).then_inc(rstd2_ready, 1)

                    over_tiles(e, NG, GUN, LAG, step)

                @block.tensor
                def _(e):
                    def turn_in(g):
                        e.wait_ge(normed_ready, g.n + 1)
                        wait(e, nT_ready, g.n)
                        for a in range(GT):
                            mm = e.transpose(p_n[:, a * P:(a + 1) * P], normed[:, g.k % 2, a * D:(a + 1) * D], ident[:])
                        mm.then_inc(n_turned, 1)

                    def step(t):
                        if (g := t.ago(2)):
                            s = g.k % 2
                            e.wait_ge(nT_ready, g.n + 1)
                            for ch in range(FCH):
                                wait(e, gelu_ready, FCH * g.n + ch - 3)
                                e.matmul(p_f[ch][:], w_1[:, ch * P:(ch + 1) * P], nT[:, s, :], start=True, stop=True)\
                                    .then_inc(f_prod, 1)
                        if (g := t.ago(1)):
                            turn_in(g)
                        if (g := t.ago(3)):
                            s = g.k % 2
                            wait(e, yT_ready, g.n)
                            for ch in range(FCH):
                                e.wait_ge(gelu_ready, FCH * g.n + ch + 1)
                                mm = e.matmul(p_y[:], w_2[:, ch, :], g_T[:, s, ch, :], start=(ch == 0), stop=(ch == FCH - 1))
                            mm.then_inc(y_prod, 1)
                        if (g := t.ago(4)):
                            s = g.k % 2
                            e.wait_ge(yT_ready, g.n + 1)
                            wait(e, sum_ready, g.n - 1)
                            for a in range(GT):
                                mm = e.transpose(p_r[s][:, a * D:(a + 1) * D], yT[:, s, a * P:(a + 1) * P], ident[:])
                            mm.then_inc(y_turned, 1)

                    over_tiles(e, NG, GUN, LAG, step)

                @block.scalar
                def _(e):
                    def step(t):
                        if (g := t.ago(3)):
                            s = g.k % 2
                            e.wait_ge(y_prod, g.n + 1)
                            wait(e, y_turned, g.n - 1)
                            e.activation(yT[:, s, :], p_y[:], ACT.Identity, bias=bf2[:]).then_inc(yT_ready, 1)
                        if (g := t.ago(1)):
                            s = g.k % 2
                            e.wait_ge(n_turned, g.n + 1)
                            wait(e, f_prod, FCH * (g.n - 1))
                            e.activation(nT[:, s, :], p_n[:], ACT.Copy).then_inc(nT_ready, 1)
                        if (g := t.ago(2)):
                            s = g.k % 2
                            for ch in range(FCH):
                                e.wait_ge(f_prod, FCH * g.n + ch + 1)
                                if ch == 0:
                                    wait(e, y_prod, g.n - 1)
                                e.activation(g_T[:, s, ch, :], p_f[ch][:], ACT.Gelu, bias=bf1[:, ch:ch + 1]).then_inc(gelu_ready, 1)

                    over_tiles(e, NG, GUN, LAG, step)

                @block.vector
                def _(e):
                    def norm_rows(into, rows_in, mean, scale, ready):
                        for a in range(GT):
                            ins = e.tensor_scalar(into[:, a * D:(a + 1) * D], rows_in[:, a * D:(a + 1) * D],
                                                  mean[:, a, 0:1], scale[:, a:a + 1], ALU.subtract, ALU.mult)
                        ins.then_inc(ready, 1)

                    def step(t):
                        if (g := t.ago(0)):
                            s = g.k % 2
                            e.wait_ge(x2_loaded[g.k], 16 * (g.b + 1))
                            for a in range(GT):
                                ins = e.bn_stats(stats[:, s, a, :], x2_in[:, g.k, a * D:(a + 1) * D])
                            ins.then_inc(stats_ready, 1)
                            e.wait_ge(stats_ready, g.n + 1)
                            gate(e)
                            for a in range(GT):
                                ins = e.bn_aggr(mv[:, g.k, a, :], stats[:, s, a, :])
                            ins.then_inc(mv_ready, 1)
                        if (g := t.ago(4)):
                            s = g.k % 2
                            e.wait_ge(y_turned, g.n + 1)
                            e.wait_ge(both_ready, g.n + 1)
                            e.tensor_tensor(ys[:, g.k, :], p_r[s][:], both[:, g.k, :], ALU.add).then_inc(sum_ready, 1)
                            e.wait_ge(sum_ready, g.n + 1)
                            for a in range(GT):
                                ins = e.bn_stats(stats2[:, s, a, :], ys[:, g.k, a * D:(a + 1) * D])
                            ins.then_inc(stats2_ready, 1)
                            e.wait_ge(stats2_ready, g.n + 1)
                            gate(e)
                            for a in range(GT):
                                ins = e.bn_aggr(mv2[:, g.k, a, :], stats2[:, s, a, :])
                            ins.then_inc(mv2_ready, 1)
                        if (g := t.ago(0)):
                            s = g.k % 2
                            e.wait_ge(rstd_ready, g.n + 1)
                            wait(e, n_turned, g.n - 1)
                            norm_rows(normed[:, s, :], x2_in[:, g.k, :], mv[:, g.k], rstd[:, g.k], normed_ready)
                        if (g := t.ago(5)):
                            e.wait_ge(rstd2_ready, g.n + 1)
                            norm_rows(res[:, g.k, :], ys[:, g.k, :], mv2[:, g.k], rstd2[:, g.k], res_ready)

                    over_tiles(e, NG, GUN, LAG, step)

        prepare()
        dense()
        for l in range(2):
            layer(l)
            layer_border(l)
        with ExitStack() as att:
            logits = sb("logits", [P, 2 * HEADS, COLS], F32, att)
            weight = sb("weight", [P, HEADS, COLS], F32, att)
            z_inv = sb("z_inv", [P, HEADS, COLS], F32, att)
            self_weight = sb("self_weight", [P, HEADS, COLS], F32, att)
            border_z = sb("border_z", [P, 3, HEADS], F32, att)
            values = sb("values", [P, COLS, D], F32, att)
            attention(values, logits)
            softmax(logits, weight, z_inv, self_weight, border_z)
            weighted(values, weight, z_inv, self_weight)
            weighted_border(border_z)
        ffn()


_INS = ['x', 'src', 'dst', 'edge_type_200', 'L0_gnn_rel_embed', 'L0_gnn_W_r1', 'L0_gnn_W_sl1', 'L0_gnn_W_el1',
        'L0_gnn_W_r2', 'L0_gnn_W_sl2', 'L0_gnn_W_el2', 'L1_gnn_Wq', 'L1_gnn_bq', 'L1_gnn_Wk', 'L1_gnn_bk',
        'L1_gnn_Wv', 'L1_gnn_bv', 'L1_gnn_Wo', 'L1_gnn_bo', 'L1_gnn_g1', 'L1_gnn_b1', 'L1_gnn_g2', 'L1_gnn_b2',
        'L1_gnn_W1', 'L1_gnn_bf1', 'L1_gnn_W2', 'L1_gnn_bf2']


def kernel(**inputs):
    import numpy as _np
    import concourse.bacc as _bacc
    from concourse import mybir as _mybir
    from concourse.bass_utils import run_bass_kernel_spmd as _run

    nc = _bacc.Bacc("TRN2", target_bir_lowering=False, num_devices=1)
    arrays, args = {}, []
    for name in _INS:
        a = _np.ascontiguousarray(inputs[name])
        arrays[f"in_{name}_dram"] = a
        args.append(nc.dram_tensor(f"in_{name}_dram", a.shape, _mybir.dt.from_np(a.dtype), kind="ExternalInput").ap())
    out = nc.dram_tensor("out_0_dram", inputs['x'].shape, _mybir.dt.float32, kind="ExternalOutput").ap()
    gnn_program(nc, *args, out)
    r = _run(nc, [arrays], core_ids=[0])
    return r.results[0]["out_0_dram"]
```

```python
from contextlib import ExitStack

import concourse.bass as bass
from concourse import mybir

F32 = mybir.dt.float32
I32 = mybir.dt.int32
ALU = mybir.AluOpType
ACT = mybir.ActivationFunctionType
AX_X = mybir.AxisListType.X

P = 128
D = 128
HEADS, HD = 8, 16
FFN = 512
FCH = FFN // P
EPS = 1e-5
SLOPE = (1.0 / 8.0 + 1.0 / 3.0) / 2.0
LOW = 1e30
SKIP = 60000

MUN = 20
UN = 10
GUN = 16
GT = 4
GROUP = GT * P


class Turn:

    def __init__(self, n, k, b, total, unroll):
        self.n, self.k, self.b, self.total, self.unroll = n, k, b, total, unroll

    def ago(self, lag, total=None):
        n = self.n - lag
        if isinstance(n, int) and not 0 <= n < (total or self.total):
            return None
        k = self.k - lag
        return Turn(n, k % self.unroll, self.b + k // self.unroll, self.total, self.unroll)

    def half(self):
        return self.b * (self.unroll // 2) + self.k // 2


def over_tiles(eng, total, unroll, lag, step, peeled=1):
    assert lag <= peeled * unroll
    for n in range(peeled * unroll):
        step(Turn(n, n % unroll, n // unroll, total, unroll))
    with eng.Fori(peeled, total // unroll) as b:
        for k in range(unroll):
            step(Turn(b * unroll + k, k, b, total, unroll))
    for n in range(total // unroll * unroll, total + lag):
        step(Turn(n, n % unroll, n // unroll, total, unroll))


class DmaSems(list):

    def __init__(self, sems, before=0):
        super().__init__(sems)
        self.before = before

    def first(self, n):
        return DmaSems(self[:n], self.before)

    def after(self, dmas):
        return self.before + 16 * dmas

    def passed(self, dmas):
        self.before += 16 * dmas


def wait(eng, sem, value):
    if not isinstance(value, int) or value > 0:
        eng.wait_ge(sem, value)


def col(t, j):
    return t[:, bass.ds(j, 1)]


def per_head(t, j):
    return t[:, :, bass.ds(j, 1)].to_broadcast([P, HEADS, HD])


def heads(ap):
    return ap.rearrange("p (h d) -> p h d", h=HEADS)


def gnn_program(nc, x, src, dst, edge_type_200, L0_gnn_rel_embed, L0_gnn_W_r1, L0_gnn_W_sl1, L0_gnn_W_el1,
                L0_gnn_W_r2, L0_gnn_W_sl2, L0_gnn_W_el2, L1_gnn_Wq, L1_gnn_bq, L1_gnn_Wk, L1_gnn_bk,
                L1_gnn_Wv, L1_gnn_bv, L1_gnn_Wo, L1_gnn_bo, L1_gnn_g1, L1_gnn_b1, L1_gnn_g2, L1_gnn_b2,
                L1_gnn_W1, L1_gnn_bf1, L1_gnn_W2, L1_gnn_bf2, out):
    N = x.shape[0]
    E = src.shape[0]
    COLS = 200
    EP = E // COLS
    assert EP * COLS == E and COLS % MUN == 0 and COLS % UN == 0
    ROWS = COLS * P
    RELS = L0_gnn_rel_embed.shape[0]
    NG = -(-N // GROUP)

    def group_rows(n):
        return n * GROUP if not isinstance(n, int) else min(n * GROUP, N - GROUP)

    h1_table = nc.dram_tensor("h1_table", [N, D], F32).ap()
    x1_table = nc.dram_tensor("x1_table", [N, D], F32).ap()
    x2_table = nc.dram_tensor("x2_table", [N, D], F32).ap()
    pair_sd = nc.dram_tensor("pair_sd", [COLS // 2 * P, 4 * D], F32).ap()
    tile_h = nc.dram_tensor("tile_h", [ROWS, D], F32).ap()
    tile_x1 = nc.dram_tensor("tile_x1", [ROWS, D], F32).ap()
    tile_xv = nc.dram_tensor("tile_xv", [ROWS, 2 * D], F32).ap()
    open_max = nc.dram_tensor("open_max", [2 * P, HEADS], F32).ap()

    root = ExitStack()
    with root:
        uses = {}

        def named(name):
            uses[name] = uses.get(name, 0) + 1
            return f"{name}_{uses[name]}"

        def sb(name, shape, dt=F32, ctx=root):
            return ctx.enter_context(nc.sbuf_tensor(named(name), shape, dt))

        def ps(name, ctx):
            return ctx.enter_context(nc.psum_tensor(named(name), [P, 512], F32))

        in_use = []

        def sem(name, ctx):
            in_use.append(ctx.enter_context(nc.semaphore(named(name))))
            return in_use[-1]

        def program(ctx):
            def clear():
                numbers = sorted(s.num for s in in_use)
                start = numbers[0]
                for n, after_n in zip(numbers, numbers[1:] + [None]):
                    if after_n != n + 1:
                        nc.sync.sem_clear(range(start, n + 1))
                        start = after_n
                nc.all_engine_barrier()
                in_use.clear()

            ctx.callback(clear)
            return ctx.enter_context(nc.Block())

        def sems(name, n, ctx):
            return [sem(f"{name}{k}", ctx) for k in range(n)]

        pair_gathered = DmaSems([sem(f"pair_gathered{k}", root) for k in range(GUN)])
        odd_gathered = DmaSems([sem(f"odd_gathered{k}", root) for k in range(MUN // 2)])
        gathered, scattered = (DmaSems([sem(f"{name}{k}", root) for k in range(MUN)]) for name in ("gathered", "scattered"))
        border_gathered, border_scattered = (DmaSems([sem(name, root)]) for name in ("border_gathered", "border_scattered"))
        passed = {engine: sem(f"passed_{engine}", root) for engine in ("sync", "gpsimd", "vector")}
        in_use.clear()

        def gate(eng):
            eng.sem_inc(passed[{nc.sync: "sync", nc.gpsimd: "gpsimd", nc.vector: "vector"}[eng]], 1)

        ident = sb("ident", [P, P])
        ones = sb("ones", [P, COLS])
        eps = sb("eps", [P, 1])
        minus_half = sb("minus_half", [P, GT])
        rel_ids = sb("rel_ids", [P, 2 * P])
        rel = sb("rel", [P, 2, D])
        w_r = [sb(f"w_r{l}", [D, D]) for l in range(2)]
        w_sl = [sb(f"w_sl{l}", [D, D]) for l in range(2)]
        w_el = [sb(f"w_el{l}", [D, D]) for l in range(2)]
        w_vqk = sb("w_vqk", [D, 3 * D])
        bias_vqk = sb("bias_vqk", [P, 4 * D])
        w_o = sb("w_o", [D, D])
        bo_rows = sb("bo_rows", [P, D])
        att_bias = sb("att_bias", [P, D])
        w_1 = sb("w_1", [D, FFN])
        w_2 = sb("w_2", [P, FCH, D])
        bf1 = sb("bf1", [P, FCH])
        bf2 = sb("bf2", [P, 1])
        type_f = sb("type_f", [P, COLS])
        same_prev = sb("same_prev", [P, COLS])
        same_next = sb("same_next", [P, COLS])
        is_end = sb("is_end", [P, COLS])
        keep_x = sb("keep_x", [P, COLS])
        cap_end = sb("cap_end", [P, COLS])
        cap_start = sb("cap_start", [P, COLS])
        in_first = sb("in_first", [P, COLS])
        in_last = sb("in_last", [P, COLS])
        norm = sb("norm", [P, COLS])
        idx = sb("idx", [P, 4, COLS], I32)
        SRC, DST, AT_END, AT_START = range(4)
        border = sb("border", [P, 6], I32)
        WR_FIRST, WR_LAST, RD_FIRST, RD_LAST, POS_FIRST, POS_LAST = range(6)
        after = sb("after", [P, P])
        before = sb("before", [P, P])
        border_norm = sb("border_norm", [P, 1])
        first_last = sb("first_last", [P, 2 * P])
        dst_fl = sb("dst_fl", [P, 2])
        open_acc = sb("open_acc", [P, 2, D])
        caught = sb("caught", [P, D])
        border_h = sb("border_h", [P, D])
        border_x = sb("border_x", [P, D])

        def prepare():
            with ExitStack() as c:
                src_i = sb("src_i", [P, COLS], I32, c)
                dst_i = sb("dst_i", [P, COLS], I32, c)
                type_i = sb("type_i", [P, COLS], I32, c)
                side_i = sb("side_i", [P, 2], I32, c)
                dst_f = sb("dst_f", [P, COLS], F32, c)
                side = sb("side", [P, 2], F32, c)
                first = sb("first", [P, COLS], F32, c)
                last = sb("last", [P, COLS], F32, c)
                real = sb("real", [P, COLS], F32, c)
                is_start = sb("is_start", [P, COLS], F32, c)
                goes = sb("goes", [P, 2], F32, c)
                tmp = sb("tmp", [P, COLS], F32, c)
                count = sb("count", [P, COLS], F32, c)
                pos = sb("pos", [P, COLS], F32, c)
                caught_count = sb("caught_count", [P, 1], F32, c)
                has = sb("has", [P, 2], F32, c)
                has_pos = sb("has_pos", [P, 2], F32, c)
                bcol = sb("bcol", [P, 1], F32, c)
                diag = sb("diag", [P, 2, P], F32, c)
                up = sb("up", [P, P], F32, c)
                down = sb("down", [P, P], F32, c)
                gcol = sb("gcol", [P, 4], F32, c)
                b1_cols = sb("b1_cols", [P, P], F32, c)
                vecs = sb("vecs", [P, 3, D], F32, c)
                bvT = sb("bvT", [P, P], F32, c)
                p_row = ps("p_row", c)
                p_cnt = ps("p_cnt", c)
                p_vqk = ps("p_vqk", c)
                p_bvT = ps("p_bvT", c)
                p_att = ps("p_att", c)
                p_bf1 = ps("p_bf1", c)
                filled = sem("filled", c)
                loaded = sem("loaded", c)
                edges_in = sem("edges_in", c)
                consts = sem("consts", c)
                dve_done = sem("dve_done", c)
                rows_ready = sem("rows_ready", c)
                diag_ready = sem("diag_ready", c)
                masks_ready = sem("masks_ready", c)
                cnt_ready = sem("cnt_ready", c)
                cnt_summed = sem("cnt_summed", c)
                root_ready = sem("root_ready", c)
                vecs_ready = sem("vecs_ready", c)
                b1_ready = sem("b1_ready", c)
                bv_ready = sem("bv_ready", c)
                bvT_ready = sem("bvT_ready", c)
                bvT_copied = sem("bvT_copied", c)
                att_ready = sem("att_ready", c)
                bf1_ready = sem("bf1_ready", c)
                block = program(c)

                @block.gpsimd
                def _(e):
                    e.memset(src_i[:], 0).then_inc(filled, 1)
                    e.memset(dst_i[:], N).then_inc(filled, 1)
                    e.memset(type_i[:], 0).then_inc(filled, 1)
                    e.memset(side_i[:], N).then_inc(filled, 1)
                    e.memset(rel[:], 0.0).then_inc(filled, 1)
                    e.memset(ident[:], 0.0).then_inc(consts, 1)
                    e.memset(up[:], 1.0).then_inc(consts, 1)
                    e.memset(down[:], 1.0).then_inc(consts, 1)
                    e.memset(ones[:], 1.0).then_inc(consts, 1)
                    e.memset(eps[:], EPS).then_inc(consts, 1)
                    e.memset(minus_half[:], -0.5).then_inc(consts, 1)
                    e.iota(rel_ids[:], pattern=[[1, 2 * P]], base=0, channel_multiplier=0,
                           allow_small_or_imprecise_dtypes=True).then_inc(consts, 1)
                    e.iota(pos[:], pattern=[[P, COLS]], base=0, channel_multiplier=1,
                           allow_small_or_imprecise_dtypes=True).then_inc(consts, 1)
                    e.wait_ge(consts, 3)
                    e.affine_select(out=ident[:], in_=ident[:], compare_op=ALU.not_equal, fill=1.0, base=0,
                                    pattern=[[-1, P]], channel_multiplier=1).then_inc(consts, 1)
                    e.affine_select(out=up[:], in_=up[:], compare_op=ALU.is_gt, fill=0.0, base=0,
                                    pattern=[[1, P]], channel_multiplier=-1).then_inc(consts, 1)
                    e.affine_select(out=down[:], in_=down[:], compare_op=ALU.is_gt, fill=0.0, base=0,
                                    pattern=[[-1, P]], channel_multiplier=1).then_inc(consts, 1)

                @block.sync
                def _(e):
                    e.wait_ge(filled, 5)
                    e.dma_start(dst_i[0:EP, :], dst.rearrange("(p j) -> p j", j=COLS)).then_inc(edges_in, 16)
                    e.dma_start(src_i[0:EP, :], src.rearrange("(p j) -> p j", j=COLS)).then_inc(edges_in, 16)
                    e.dma_start(type_i[0:EP, :], edge_type_200.rearrange("(p j) -> p j", j=COLS)).then_inc(edges_in, 16)
                    by_part = dst.rearrange("(p j) -> p j", j=COLS)
                    e.dma_start(side_i[1:EP, 0:1], by_part[0:EP - 1, COLS - 1:COLS], allow_slow_non_contiguous=True).then_inc(edges_in, 16)
                    e.dma_start(side_i[0:EP - 1, 1:2], by_part[1:EP, 0:1], allow_slow_non_contiguous=True).then_inc(edges_in, 16)
                    e.dma_start(rel[:, 0, :], L0_gnn_rel_embed[0:P, :]).then_inc(edges_in, 16)
                    e.dma_start(rel[0:RELS - P, 1, :], L0_gnn_rel_embed[P:RELS, :]).then_inc(edges_in, 16)
                    for t, a in ((w_r[0], L0_gnn_W_r1), (w_sl[0], L0_gnn_W_sl1), (w_el[0], L0_gnn_W_el1),
                                 (w_r[1], L0_gnn_W_r2), (w_sl[1], L0_gnn_W_sl2), (w_el[1], L0_gnn_W_el2)):
                        e.dma_start(t[:], a).then_inc(edges_in, 16)
                    e.wait_ge(edges_in, 13 * 16)

                @block.scalar
                def _(e):
                    for n, a in enumerate((L1_gnn_Wv, L1_gnn_Wq, L1_gnn_Wk)):
                        e.dma_start(w_vqk[:, n * D:(n + 1) * D], a).then_inc(loaded, 16)
                    for n, a in enumerate((L1_gnn_g1, L1_gnn_b1, L1_gnn_g2, L1_gnn_b2)):
                        e.dma_start(gcol[:, n:n + 1], a.rearrange("(p a) -> p a", a=1)).then_inc(loaded, 16)
                    e.dma_start(bf2[:], L1_gnn_bf2.rearrange("(p a) -> p a", a=1)).then_inc(loaded, 16)
                    for n, a in enumerate((L1_gnn_bv, L1_gnn_bq, L1_gnn_bk)):
                        e.dma_start(vecs[:, n, :], a.partition_broadcast(P)).then_inc(loaded, 16)
                    e.dma_start(bo_rows[:], L1_gnn_bo.partition_broadcast(P)).then_inc(loaded, 16)
                    e.dma_start(w_o[:], L1_gnn_Wo).then_inc(loaded, 16)
                    e.dma_start(w_1[:], L1_gnn_W1).then_inc(loaded, 16)
                    e.dma_start(w_2[:], L1_gnn_W2.rearrange("(c p) n -> p c n", p=P)).then_inc(loaded, 16)
                    e.dma_start(bf1[:], L1_gnn_bf1.rearrange("(c p) -> p c", p=P), allow_slow_non_contiguous=True).then_inc(loaded, 16)
                    e.wait_ge(cnt_summed, 2)
                    e.activation(norm[:], count[:], ACT.Sqrt).then_inc(root_ready, 1)
                    e.activation(border_norm[:], caught_count[:], ACT.Sqrt).then_inc(root_ready, 1)

                @block.tensor
                def _(e):
                    e.wait_ge(consts, 11)
                    e.wait_ge(diag_ready, 2)
                    for s in range(2):
                        mm = e.matmul(p_row[:, s * P:(s + 1) * P], ones[:, 0:P], diag[:, s, :], start=True, stop=True)
                    mm.then_inc(rows_ready, 1)
                    e.wait_ge(masks_ready, 1)
                    e.matmul(p_cnt[:, 0:1], after[:], count[:, COLS - 1:COLS], start=True, stop=True).then_inc(cnt_ready, 1)
                    e.wait_ge(b1_ready, 1)
                    e.matmul(p_vqk[:, 0:3 * D], b1_cols[:], w_vqk[:], start=True, stop=True).then_inc(vecs_ready, 1)
                    for ch in range(FCH):
                        mm = e.matmul(p_bf1[:, ch:ch + 1], w_1[:, ch * P:(ch + 1) * P], gcol[:, 3:4], start=True, stop=True)
                    mm.then_inc(bf1_ready, 1)
                    e.wait_ge(bv_ready, 1)
                    e.transpose(p_bvT[:, 0:P], bias_vqk[:, 0:D], ident[:]).then_inc(bvT_ready, 1)
                    e.wait_ge(bvT_copied, 1)
                    e.matmul(p_att[:, 0:D], bvT[:], w_o[:], start=True, stop=True).then_inc(att_ready, 1)

                @block.vector
                def _(e):
                    made = [0]

                    def chain(ins):
                        made[0] += 1
                        ins.then_inc(dve_done, 1)
                        e.wait_ge(dve_done, made[0])

                    e.wait_ge(edges_in, 13 * 16)
                    e.wait_ge(consts, 11)
                    e.tensor_copy(idx[:, SRC, :], src_i[:])
                    e.tensor_copy(type_f[:], type_i[:])
                    e.tensor_copy(side[:], side_i[:])
                    chain(e.tensor_copy(dst_f[:], dst_i[:]))
                    e.tensor_copy(dst_fl[:, 0:1], dst_f[:, 0:1])
                    chain(e.tensor_copy(dst_fl[:, 1:2], dst_f[:, COLS - 1:COLS]))
                    for s in range(2):
                        e.tensor_scalar(diag[:, s, :], ident[:], dst_fl[:, s:s + 1], None, ALU.mult).then_inc(diag_ready, 1)
                    e.memset(same_prev[:, 0:1], 0.0)
                    e.memset(same_next[:, COLS - 1:COLS], 0.0)
                    e.tensor_tensor(same_prev[:, 1:COLS], dst_f[:, 1:COLS], dst_f[:, 0:COLS - 1], ALU.is_equal)
                    e.tensor_tensor(same_next[:, 0:COLS - 1], dst_f[:, 1:COLS], dst_f[:, 0:COLS - 1], ALU.is_equal)
                    e.tensor_tensor(goes[:], side[:], dst_fl[:], ALU.is_equal)
                    e.tensor_scalar(first[:], dst_f[:], dst_fl[:, 0:1], None, ALU.is_equal)
                    e.tensor_scalar(last[:], dst_f[:], dst_fl[:, 1:2], None, ALU.is_equal)
                    e.tensor_scalar(idx[:, DST, :], dst_f[:], float(N - 1), None, ALU.min)
                    chain(e.tensor_scalar(real[:], dst_f[:], float(N), None, ALU.is_lt))
                    e.tensor_copy(keep_x[:], same_next[:])
                    e.tensor_scalar(in_first[:], first[:], -1.0, LOW, ALU.add, ALU.mult)
                    e.tensor_scalar(in_last[:], last[:], -1.0, LOW, ALU.add, ALU.mult)
                    e.tensor_scalar(is_end[:], same_next[:], -1.0, 1.0, ALU.mult, ALU.add)
                    chain(e.tensor_scalar(is_start[:], same_prev[:], -1.0, 1.0, ALU.mult, ALU.add))
                    e.tensor_copy(keep_x[:, COLS - 1:COLS], goes[:, 1:2])
                    e.tensor_scalar(is_end[:, COLS - 1:COLS], goes[:, 1:2], -1.0, 1.0, ALU.mult, ALU.add)
                    chain(e.tensor_scalar(is_start[:, 0:1], goes[:, 0:1], -1.0, 1.0, ALU.mult, ALU.add))
                    for n, (at, seg, cap, write) in enumerate(((is_end, first, cap_end, AT_END),
                                                               (is_start, last, cap_start, AT_START))):
                        chain(e.tensor_tensor(tmp[:], at[:], real[:], ALU.mult))
                        chain(e.scalar_tensor_tensor(out=cap[:], in0=seg[:], scalar=goes[:, n:n + 1], in1=tmp[:],
                                                     op0=ALU.mult, op1=ALU.mult))
                        chain(e.tensor_tensor(tmp[:], tmp[:], cap[:], ALU.subtract))
                        chain(e.scalar_tensor_tensor(out=tmp[:], in0=dst_f[:], scalar=-float(SKIP), in1=tmp[:],
                                                     op0=ALU.add, op1=ALU.mult))
                        chain(e.tensor_scalar(idx[:, write, :], tmp[:], float(SKIP), None, ALU.add))
                        chain(e.tensor_reduce(has[:, n:n + 1], cap[:], AX_X, ALU.add))
                        chain(e.tensor_tensor(tmp[:], cap[:], pos[:], ALU.mult))
                        chain(e.tensor_reduce(has_pos[:, n:n + 1], tmp[:], AX_X, ALU.add))
                        chain(e.scalar_tensor_tensor(out=bcol[:], in0=dst_fl[:, n:n + 1], scalar=-float(SKIP),
                                                     in1=has[:, n:n + 1], op0=ALU.add, op1=ALU.mult))
                        chain(e.tensor_scalar(border[:, WR_FIRST + n:WR_FIRST + n + 1], bcol[:], float(SKIP), None, ALU.add))
                        chain(e.tensor_scalar(border[:, RD_FIRST + n:RD_FIRST + n + 1], dst_fl[:, n:n + 1], float(N - 1), None, ALU.min))
                    chain(e.scalar_tensor_tensor(out=bcol[:], in0=has[:, 0:1], scalar=-float(SKIP), in1=has_pos[:, 0:1],
                                                 op0=ALU.mult, op1=ALU.add))
                    chain(e.tensor_scalar(border[:, POS_FIRST:POS_FIRST + 1], bcol[:], float(SKIP), None, ALU.add))
                    chain(e.tensor_copy(border[:, POS_LAST:POS_LAST + 1], has_pos[:, 1:2]))
                    chain(e.tensor_tensor_scan(count[:], same_prev[:], ones[:], 0.0, ALU.mult, ALU.add))
                    e.wait_ge(rows_ready, 1)
                    chain(e.tensor_copy(first_last[:], p_row[:, 0:2 * P]))
                    chain(e.scalar_tensor_tensor(out=after[:], in0=first_last[:, 0:P], scalar=dst_fl[:, 1:2], in1=up[:],
                                                 op0=ALU.is_equal, op1=ALU.mult))
                    e.scalar_tensor_tensor(out=before[:], in0=first_last[:, P:2 * P], scalar=dst_fl[:, 0:1], in1=down[:],
                                           op0=ALU.is_equal, op1=ALU.mult).then_inc(masks_ready, 1)
                    chain(e.tensor_tensor(tmp[:], cap_end[:], count[:], ALU.mult))
                    chain(e.tensor_reduce(caught_count[:], tmp[:], AX_X, ALU.add))
                    e.wait_ge(cnt_ready, 1)
                    e.tensor_scalar(count[:], count[:], 1.0, None, ALU.max).then_inc(cnt_summed, 1)
                    chain(e.tensor_tensor(caught_count[:], caught_count[:], p_cnt[:, 0:1], ALU.add))
                    e.tensor_scalar(caught_count[:], caught_count[:], 1.0, None, ALU.max).then_inc(cnt_summed, 1)
                    e.wait_ge(root_ready, 2)
                    e.reciprocal(norm[:], norm[:])
                    chain(e.reciprocal(border_norm[:], border_norm[:]))
                    e.wait_ge(loaded, 16 * 16)
                    e.tensor_scalar(b1_cols[:], ones[:, 0:P], gcol[:, 1:2], None, ALU.mult).then_inc(b1_ready, 1)
                    e.wait_ge(vecs_ready, 1)
                    e.tensor_tensor(bias_vqk[:, 0:3 * D], p_vqk[:, 0:3 * D], vecs[:].rearrange("p a d -> p (a d)"), ALU.add)\
                        .then_inc(bv_ready, 1)
                    e.wait_ge(bf1_ready, 1)
                    e.tensor_tensor(bias_vqk[:, 3 * D:4 * D], p_vqk[:, 2 * D:3 * D], vecs[:, 2, :], ALU.add)
                    e.tensor_tensor(bf1[:], bf1[:], p_bf1[:, 0:FCH], ALU.add)
                    e.tensor_scalar(w_vqk[:], w_vqk[:], gcol[:, 0:1], None, ALU.mult)
                    e.tensor_scalar(w_1[:], w_1[:], gcol[:, 2:3], None, ALU.mult)
                    e.wait_ge(bvT_ready, 1)
                    e.tensor_copy(bvT[:], p_bvT[:, 0:P]).then_inc(bvT_copied, 1)
                    e.wait_ge(att_ready, 1)
                    e.tensor_copy(att_bias[:], p_att[:, 0:D])

        def dense():
            PAIRS = COLS // 2
            with ExitStack() as c:
                x_in = sb("x_in", [P, GUN, GROUP], F32, c)
                pair = sb("pair", [P, GUN, 3 * D], F32, c)
                use = sb("use", [P, GUN, 2, 2], I32, c)
                xT = sb("xT", [P, 2, GROUP], F32, c)
                raw1 = sb("raw1", [P, 2, GROUP], F32, c)
                raw2 = sb("raw2", [P, 2, GROUP], F32, c)
                h1T = sb("h1T", [P, 2, GROUP], F32, c)
                h2T = sb("h2T", [P, 2, GROUP], F32, c)
                h1_rows = sb("h1_rows", [P, 2, GROUP], F32, c)
                stats = sb("stats", [P, 2, GT, 6], F32, c)
                mv = sb("mv", [P, 2, GT, 2], F32, c)
                std = sb("std", [P, 2, GT], F32, c)
                rstd = sb("rstd", [P, 2, GT], F32, c)
                shift = sb("shift", [P, 2, GT], F32, c)
                p_x = [ps(f"p_x{s}", c) for s in range(2)]
                p_1, p_2 = ps("p_1", c), ps("p_2", c)
                p_r1 = [ps(f"p_r1{s}", c) for s in range(2)]
                p_r2 = [ps(f"p_r2{s}", c) for s in range(2)]
                x_loaded = sems("x_loaded", GUN, c)
                h1_stored = sems("h1_stored", 2, c)
                x1_stored = sems("x1_stored", GUN, c)
                pair_stored = sems("pair_stored", GUN, c)
                use_ready = sem("use_ready", c)
                x_turned = sem("x_turned", c)
                xT_ready = sem("xT_ready", c)
                prod1, prod2 = sem("prod1", c), sem("prod2", c)
                raw1_ready, raw2_ready = sem("raw1_ready", c), sem("raw2_ready", c)
                h1T_ready, h2T_ready = sem("h1T_ready", c), sem("h2T_ready", c)
                h1_turned, h2_turned = sem("h1_turned", c), sem("h2_turned", c)
                h1_ready = sem("h1_ready", c)
                sum_ready = sem("sum_ready", c)
                stats_ready = sem("stats_ready", c)
                mv_ready = sem("mv_ready", c)
                std_ready = sem("std_ready", c)
                rstd_ready = sem("rstd_ready", c)
                shift_ready = sem("shift_ready", c)
                x1_ready = sem("x1_ready", c)
                x1_rest_ready = sem("x1_rest_ready", c)
                block = program(c)
                LAG = 14

                def rows(table, t):
                    return table[bass.ds(group_rows(t.n), GROUP), :].rearrange("(p a) d -> p (a d)", a=GT)

                @block.gpsimd
                def _(e):
                    def step(t):
                        if (m := t.ago(0, PAIRS)):
                            wait(e, pair_stored[m.k], 16 * m.b)
                            gate(e)
                            e.tensor_copy(use[:, m.k, :, :], idx[:, SRC:DST + 1, bass.ds(m.n * 2, 2)]).then_inc(use_ready, 1)
                            e.wait_ge(use_ready, m.n + 1)
                            gate(e)
                            for a in range(2):
                                for which in (SRC, DST)[:2 - a]:
                                    e.indirect_dma_start(out=pair[:, m.k, (2 * a + which) * D:(2 * a + which + 1) * D], out_offset=None, in_=x,
                                                         in_offset=bass.IndirectOffsetOnAxis(ap=use[:, m.k, which, a:a + 1], axis=0))\
                                        .then_inc(pair_gathered[m.k], 16)

                    over_tiles(e, NG, GUN, LAG, step)

                @block.sync
                def _(e):
                    def step(t):
                        if (g := t.ago(14)):
                            if isinstance(g.n, int) and g.n == NG - 1:
                                e.wait_ge(x1_stored[(g.n - 1) % GUN], 16 * ((g.n - 1) // GUN + 1))
                            gate(e)
                            e.wait_ge(x1_ready, g.n + 1)
                            gate(e)
                            e.wait_ge(x1_rest_ready, g.n + 1)
                            gate(e)
                            e.dma_start(rows(x1_table, g), x_in[:, g.k, :]).then_inc(x1_stored[g.k], 16)
                        if (g := t.ago(9)):
                            if isinstance(g.n, int) and g.n == NG - 1:
                                e.wait_ge(h1_stored[(g.n - 1) % 2], 16 * ((g.n - 1) // 2 + 1))
                            gate(e)
                            e.wait_ge(h1_ready, g.n + 1)
                            gate(e)
                            e.dma_start(rows(h1_table, g), h1_rows[:, g.k % 2, :]).then_inc(h1_stored[g.k % 2], 16)
                        if (m := t.ago(8, PAIRS)):
                            e.wait_ge(pair_gathered[m.k], pair_gathered.after(3 * (m.b + 1)))
                            gate(e)
                            e.dma_start(pair_sd[bass.ds(m.n * P, P), 0:3 * D], pair[:, m.k, :])\
                                .then_inc(pair_stored[m.k], 16)
                        if (g := t.ago(0)):
                            wait(e, x1_stored[g.k], 16 * g.b)
                            gate(e)
                            e.dma_start(x_in[:, g.k, :], rows(x, g)).then_inc(x_loaded[g.k], 16)

                    over_tiles(e, NG, GUN, LAG, step)
                    for k in range(GUN):
                        e.wait_ge(x1_stored[k], 16 * len(range(k, NG, GUN)))
                        e.wait_ge(pair_stored[k], 16 * len(range(k, PAIRS, GUN)))
                    for k in range(2):
                        e.wait_ge(h1_stored[k], 16 * len(range(k, NG, 2)))

                @block.tensor
                def _(e):
                    def step(t):
                        if (g := t.ago(0)):
                            s = g.k % 2
                            e.wait_ge(x_loaded[g.k], 16 * (g.b + 1))
                            wait(e, xT_ready, g.n - 1)
                            for a in range(GT):
                                mm = e.transpose(p_x[s][:, a * P:(a + 1) * P], x_in[:, g.k, a * D:(a + 1) * D], ident[:])
                            mm.then_inc(x_turned, 1)
                        if (g := t.ago(2)):
                            e.wait_ge(xT_ready, g.n + 1)
                            wait(e, raw1_ready, g.n)
                            e.matmul(p_1[:], w_el[0][:], xT[:, g.k % 2, :], start=True, stop=True).then_inc(prod1, 1)
                        if (g := t.ago(5)):
                            s = g.k % 2
                            e.wait_ge(h1T_ready, g.n + 1)
                            wait(e, h1_ready, g.n - 1)
                            for a in range(GT):
                                mm = e.transpose(p_r1[s][:, a * D:(a + 1) * D], h1T[:, s, a * P:(a + 1) * P], ident[:])
                            mm.then_inc(h1_turned, 1)
                            wait(e, raw2_ready, g.n)
                            e.matmul(p_2[:], w_el[1][:], h1T[:, s, :], start=True, stop=True).then_inc(prod2, 1)
                        if (g := t.ago(8)):
                            s = g.k % 2
                            e.wait_ge(h2T_ready, g.n + 1)
                            wait(e, sum_ready, g.n - 1)
                            for a in range(GT):
                                mm = e.transpose(p_r2[s][:, a * D:(a + 1) * D], h2T[:, s, a * P:(a + 1) * P], ident[:])
                            mm.then_inc(h2_turned, 1)

                    over_tiles(e, NG, GUN, LAG, step)

                @block.scalar
                def _(e):
                    def step(t):
                        if (g := t.ago(3)):
                            s = g.k % 2
                            e.wait_ge(prod1, g.n + 1)
                            wait(e, h1T_ready, g.n - 1)
                            e.activation(raw1[:, s, :], p_1[:], ACT.Copy).then_inc(raw1_ready, 1)
                        if (g := t.ago(6)):
                            s = g.k % 2
                            e.wait_ge(prod2, g.n + 1)
                            wait(e, h2T_ready, g.n - 1)
                            e.activation(raw2[:, s, :], p_2[:], ACT.Copy).then_inc(raw2_ready, 1)
                            wait(e, h1_stored[s], 16 * g.half())
                            e.activation(h1_rows[:, s, :], p_r1[s][:], ACT.Copy).then_inc(h1_ready, 1)
                        if (g := t.ago(1)):
                            s = g.k % 2
                            e.wait_ge(x_turned, g.n + 1)
                            wait(e, prod1, g.n - 1)
                            e.activation(xT[:, s, :], p_x[s][:], ACT.Copy).then_inc(xT_ready, 1)
                        if (g := t.ago(10)):
                            s = g.k % 2
                            e.wait_ge(mv_ready, g.n + 1)
                            wait(e, rstd_ready, g.n - 1)
                            e.activation(std[:, s, :], mv[:, s, :, 1], ACT.Sqrt, bias=eps[:]).then_inc(std_ready, 1)
                        if (g := t.ago(11)):
                            s = g.k % 2
                            e.wait_ge(shift_ready, g.n + 1)
                            for a in range(GT // 2):
                                row = x_in[:, g.k, a * D:(a + 1) * D]
                                ins = e.activation(row, row, ACT.Identity, scale=rstd[:, s, a:a + 1], bias=shift[:, s, a:a + 1])
                            ins.then_inc(x1_ready, 1)

                    over_tiles(e, NG, GUN, LAG, step)

                @block.vector
                def _(e):
                    def rrelu(into, raw, ready):
                        e.scalar_tensor_tensor(out=into, in0=raw, scalar=SLOPE, in1=raw, op0=ALU.mult, op1=ALU.max).then_inc(ready, 1)

                    def step(t):
                        if (g := t.ago(11)):
                            s = g.k % 2
                            e.wait_ge(std_ready, g.n + 1)
                            wait(e, x1_ready, g.n - 1)
                            wait(e, x1_rest_ready, g.n - 1)
                            e.reciprocal(rstd[:, s, :], std[:, s, :]).then_inc(rstd_ready, 1)
                        if (g := t.ago(9)):
                            s = g.k % 2
                            e.wait_ge(h2_turned, g.n + 1)
                            e.tensor_tensor(x_in[:, g.k, :], p_r2[s][:], x_in[:, g.k, :], ALU.add).then_inc(sum_ready, 1)
                        if (g := t.ago(11)):
                            s = g.k % 2
                            e.wait_ge(rstd_ready, g.n + 1)
                            e.scalar_tensor_tensor(out=shift[:, s, :], in0=mv[:, s, :, 0], scalar=-1.0, in1=rstd[:, s, :],
                                                   op0=ALU.mult, op1=ALU.mult).then_inc(shift_ready, 1)
                        if (g := t.ago(4)):
                            s = g.k % 2
                            e.wait_ge(raw1_ready, g.n + 1)
                            wait(e, prod2, g.n - 1)
                            wait(e, h1_turned, g.n - 1)
                            gate(e)
                            rrelu(h1T[:, s, :], raw1[:, s, :], h1T_ready)
                        if (g := t.ago(9)):
                            s = g.k % 2
                            e.wait_ge(sum_ready, g.n + 1)
                            wait(e, mv_ready, g.n - 1)
                            for a in range(GT):
                                ins = e.bn_stats(stats[:, s, a, :], x_in[:, g.k, a * D:(a + 1) * D])
                            ins.then_inc(stats_ready, 1)
                        if (g := t.ago(11)):
                            s = g.k % 2
                            for a in range(GT // 2, GT):
                                row = x_in[:, g.k, a * D:(a + 1) * D]
                                ins = e.tensor_scalar(row, row, mv[:, s, a, 0:1], rstd[:, s, a:a + 1], ALU.subtract, ALU.mult)
                            ins.then_inc(x1_rest_ready, 1)
                        if (g := t.ago(7)):
                            s = g.k % 2
                            e.wait_ge(raw2_ready, g.n + 1)
                            wait(e, h2_turned, g.n - 1)
                            gate(e)
                            rrelu(h2T[:, s, :], raw2[:, s, :], h2T_ready)
                        if (g := t.ago(9)):
                            s = g.k % 2
                            e.wait_ge(stats_ready, g.n + 1)
                            wait(e, x1_rest_ready, g.n - 1)
                            wait(e, std_ready, g.n - 1)
                            gate(e)
                            for a in range(GT):
                                ins = e.bn_aggr(mv[:, s, a, :], stats[:, s, a, :])
                            ins.then_inc(mv_ready, 1)

                    over_tiles(e, NG, GUN, LAG, step)

        def layer(l):
            target = (h1_table, x1_table)[l]
            with ExitStack() as c:
                rows_in = sb("rows_in", [P, MUN, 2, D], F32, c)
                h_dst = sb("h_dst", [P, MUN, D], F32, c)
                x1_out = sb("x1_out", [P, MUN, D], F32, c)
                use = sb("use", [P, MUN, 3], I32, c)
                hot = sb("hot", [P, 2, 2 * P], F32, c)
                hotT = sb("hotT", [P, 2, 2 * P], F32, c)
                acc_n = sb("acc_n", [P, 2, D], F32, c)
                turned = sb("turned", [P, 2, 2 * P], F32, c)
                h_raw = sb("h_raw", [P, 2, D], F32, c)
                h_out = sb("h_out", [P, 2, D], F32, c)
                xs = sb("xs", [P, 4, D], F32, c)
                stats = sb("stats", [P, 2, 6], F32, c)
                mv = sb("mv", [P, 4, 2], F32, c)
                std = sb("std", [P, 2], F32, c)
                rstd = sb("rstd", [P, 2], F32, c)
                p_hot = [ps(f"p_hot{s}", c) for s in range(2)]
                p_msg = [ps(f"p_msg{s}", c) for s in range(2)]
                p_turn = [ps(f"p_turn{s}", c) for s in range(2)]
                p_h = [ps(f"p_h{s}", c) for s in range(2)]
                src_in = gathered if l else DmaSems(sems("src_in", MUN, c))
                dst_in = sems("dst_in", MUN, c) if l else None
                stored = sems("stored", MUN, c)
                use_ready = sem("use_ready", c)
                hot_ready = sem("hot_ready", c)
                hot_turned = sem("hot_turned", c)
                hotT_ready = sem("hotT_ready", c)
                msg_ready = sem("msg_ready", c)
                cleared = sem("cleared", c)
                acc_ready = sem("acc_ready", c)
                catch_done = sem("catch_done", c)
                acc_n_ready = sem("acc_n_ready", c)
                both_turned = sem("both_turned", c)
                turned_ready = sem("turned_ready", c)
                h_prod = sem("h_prod", c)
                raw_ready = sem("raw_ready", c)
                h_ready = sem("h_ready", c)
                sum_ready = sem("sum_ready", c)
                stats_ready = sem("stats_ready", c)
                mv_ready = sem("mv_ready", c)
                std_ready = sem("std_ready", c)
                rstd_ready = sem("rstd_ready", c)
                row_ready = sem("row_ready", c) if l else h_ready
                block = program(c)
                OUT_LAG = 15 + l
                LAG = OUT_LAG

                def tile_rows(t, table):
                    return table[bass.ds(t.n * P, P), :]

                def stores(k):
                    return 32 if l == 0 and k % 2 == 1 else 16

                def pair_rows(t, first, last):
                    at = 2 * (t.k % 2)
                    return pair_sd[bass.ds(t.half() * P, P), (at + first) * D:(at + last + 1) * D]

                @block.gpsimd
                def _(e):
                    def step(t):
                        if (g := t.ago(0)):
                            if l == 1:
                                wait(e, scattered[g.k], scattered.after(g.b))
                                gate(e)
                                e.tensor_copy(use[:, g.k, :].unsqueeze(2), idx[:, 0:3, bass.ds(g.n, 1)]).then_inc(use_ready, 1)
                            if l == 0 and g.k % 2 == 1:
                                e.wait_ge(use_ready, g.n + 1)
                                wait(e, stored[g.k], 32 * g.b)
                                gate(e)
                                e.indirect_dma_start(out=rows_in[:, g.k, DST, :], out_offset=None, in_=x,
                                                     in_offset=bass.IndirectOffsetOnAxis(ap=use[:, g.k, DST:DST + 1], axis=0))\
                                    .then_inc(odd_gathered[g.k // 2], 16)
                            if l == 1:
                                e.wait_ge(use_ready, g.n + 1)
                                wait(e, msg_ready, g.n - MUN + 1)
                                gate(e)
                                e.indirect_dma_start(out=rows_in[:, g.k, SRC, :], out_offset=None, in_=h1_table,
                                                     in_offset=bass.IndirectOffsetOnAxis(ap=use[:, g.k, SRC:SRC + 1], axis=0))\
                                    .then_inc(src_in[g.k], 16)
                        if (g := t.ago(OUT_LAG)):
                            e.wait_ge(use_ready, g.n + 1)
                            e.wait_ge(row_ready, g.n + 1)
                            gate(e)
                            rows_out = h_dst[:, g.k, :] if l == 0 else x1_out[:, g.k, :]
                            e.indirect_dma_start(out=target, in_=rows_out, in_offset=None,
                                                 out_offset=bass.IndirectOffsetOnAxis(ap=use[:, g.k, AT_END:AT_END + 1], axis=0),
                                                 bounds_check=N - 1, oob_is_err=False).then_inc(scattered[g.k], 16)

                    over_tiles(e, COLS, MUN, LAG, step)
                    for k in range(MUN):
                        e.wait_ge(scattered[k], scattered.after(COLS // MUN))

                @block.sync
                def _(e):
                    def step(t):
                        if (g := t.ago(0)):
                            wait(e, row_ready, g.n - MUN + 1)
                            gate(e)
                            wait(e, stored[g.k], stores(g.k) * g.b)
                            gate(e)
                            wait(e, scattered[g.k], scattered.after(g.b))
                            gate(e)
                            if l == 0:
                                last = SRC if g.k % 2 else DST
                                e.dma_start(rows_in[:, g.k, 0:last + 1, :].rearrange("p w d -> p (w d)"), pair_rows(g, SRC, last))\
                                    .then_inc(src_in[g.k], 16)
                            else:
                                e.dma_start(h_dst[:, g.k, :], tile_rows(g, tile_h)).then_inc(dst_in[g.k], 16)
                                e.dma_start(rows_in[:, g.k, DST, :], pair_rows(g, DST, DST)).then_inc(dst_in[g.k], 16)
                        if (g := t.ago(OUT_LAG)):
                            e.wait_ge(row_ready, g.n + 1)
                            if l == 0:
                                e.dma_start(tile_rows(g, tile_h), h_dst[:, g.k, :]).then_inc(stored[g.k], 16)
                                if g.k % 2 == 1:
                                    e.dma_start(pair_rows(g, DST, DST), rows_in[:, g.k, DST, :]).then_inc(stored[g.k], 16)
                            else:
                                e.dma_start(tile_rows(g, tile_x1), x1_out[:, g.k, :]).then_inc(stored[g.k], 16)

                    over_tiles(e, COLS, MUN, LAG, step)
                    for k in range(MUN):
                        e.wait_ge(stored[k], stores(k) * (COLS // MUN))

                @block.tensor
                def _(e):
                    def step(t):
                        if (g := t.ago(1)):
                            s = g.k % 2
                            e.wait_ge(hot_ready, g.n + 1)
                            wait(e, hotT_ready, g.n - 1)
                            for a in range(2):
                                mm = e.transpose(p_hot[s][:, a * P:(a + 1) * P], hot[:, s, a * P:(a + 1) * P], ident[:])
                            mm.then_inc(hot_turned, 1)
                        if (g := t.ago(3)):
                            s = g.k % 2
                            e.wait_ge(hotT_ready, g.n + 1)
                            e.wait_ge(src_in[g.k], src_in.after(g.b + 1))
                            wait(e, acc_ready, g.n - 1)
                            e.matmul(p_msg[s][:, 0:D], hotT[:, s, 0:P], rel[:, 0, :], start=True, stop=False)
                            e.matmul(p_msg[s][:, 0:D], hotT[:, s, P:2 * P], rel[:, 1, :], start=False, stop=False)
                            e.matmul(p_msg[s][:, 0:D], ident[:], rows_in[:, g.k, SRC, :], start=False, stop=True).then_inc(msg_ready, 1)
                        if (g := t.ago(6)):
                            s = g.k % 2
                            e.wait_ge(acc_n_ready, g.n + 1)
                            if l == 1:
                                e.wait_ge(dst_in[g.k], 32 * (g.b + 1))
                            elif g.k % 2 == 1:
                                e.wait_ge(odd_gathered[g.k // 2], odd_gathered.after(g.b + 1))
                            wait(e, turned_ready, g.n - 1)
                            own = rows_in[:, g.k, DST, :] if l == 0 else h_dst[:, g.k, :]
                            e.transpose(p_turn[s][:, 0:P], acc_n[:, s, :], ident[:])
                            e.transpose(p_turn[s][:, P:2 * P], own, ident[:]).then_inc(both_turned, 1)
                        if (g := t.ago(8)):
                            s = g.k % 2
                            e.wait_ge(turned_ready, g.n + 1)
                            wait(e, raw_ready, g.n - 1)
                            e.matmul(p_h[s][:, 0:D], turned[:, s, 0:P], w_r[l][:], start=True, stop=False)
                            e.matmul(p_h[s][:, 0:D], turned[:, s, P:2 * P], w_sl[l][:], start=False, stop=True).then_inc(h_prod, 1)

                    over_tiles(e, COLS, MUN, LAG, step)

                @block.scalar
                def _(e):
                    def step(t):
                        if (g := t.ago(2)):
                            s = g.k % 2
                            e.wait_ge(hot_turned, g.n + 1)
                            wait(e, msg_ready, g.n - 1)
                            e.activation(hotT[:, s, :], p_hot[s][:, 0:2 * P], ACT.Copy).then_inc(hotT_ready, 1)
                        if (g := t.ago(5)):
                            s = g.k % 2
                            e.wait_ge(acc_ready, g.n + 1)
                            wait(e, both_turned, g.n - 1)
                            e.activation(acc_n[:, s, :], open_acc[:, s, :], ACT.Copy, scale=col(norm, g.n)).then_inc(acc_n_ready, 1)
                        if (g := t.ago(7)):
                            s = g.k % 2
                            e.wait_ge(both_turned, g.n + 1)
                            wait(e, h_prod, g.n - 1)
                            e.activation(turned[:, s, :], p_turn[s][:, 0:2 * P], ACT.Copy).then_inc(turned_ready, 1)
                        if (g := t.ago(9)):
                            s = g.k % 2
                            e.wait_ge(h_prod, g.n + 1)
                            wait(e, h_ready, g.n - 1)
                            e.activation(h_raw[:, s, :], p_h[s][:, 0:D], ACT.Copy).then_inc(raw_ready, 1)
                        if l == 1 and (g := t.ago(11)):
                            s = g.k % 2
                            e.wait_ge(mv_ready, g.n + 1)
                            wait(e, rstd_ready, g.n - 1)
                            e.activation(std[:, s:s + 1], mv[:, g.k % 4, 1:2], ACT.Sqrt, bias=eps[:]).then_inc(std_ready, 1)

                    over_tiles(e, COLS, MUN, LAG, step)

                @block.vector
                def _(e):
                    e.memset(open_acc[:], 0.0).then_inc(cleared, 1)
                    e.memset(caught[:], 0.0).then_inc(cleared, 1)

                    def step(t):
                        if l == 0 and (g := t.ago(0)):
                            wait(e, scattered[g.k], scattered.after(g.b))
                            gate(e)
                            e.tensor_copy(use[:, g.k, :].unsqueeze(2), idx[:, 0:3, bass.ds(g.n, 1)]).then_inc(use_ready, 1)
                        if (g := t.ago(0)):
                            s = g.k % 2
                            wait(e, hot_turned, g.n - 1)
                            gate(e)
                            e.tensor_scalar(hot[:, s, :], rel_ids[:], col(type_f, g.n), None, ALU.is_equal).then_inc(hot_ready, 1)
                        if (g := t.ago(10)):
                            s = g.k % 2
                            e.wait_ge(raw_ready, g.n + 1)
                            gate(e)
                            if l == 1:
                                wait(e, sum_ready, g.n - 1)
                            h_rows = h_dst[:, g.k, :] if l == 0 else h_out[:, s, :]
                            e.scalar_tensor_tensor(out=h_rows, in0=h_raw[:, s, :], scalar=SLOPE, in1=h_raw[:, s, :],
                                                   op0=ALU.mult, op1=ALU.max).then_inc(h_ready, 1)
                        if l == 1 and (g := t.ago(12)):
                            s = g.k % 2
                            e.wait_ge(std_ready, g.n + 1)
                            wait(e, row_ready, g.n - 1)
                            e.reciprocal(rstd[:, s:s + 1], std[:, s:s + 1]).then_inc(rstd_ready, 1)
                        if (g := t.ago(4)):
                            s = g.k % 2
                            e.wait_ge(msg_ready, g.n + 1)
                            if isinstance(g.n, int) and g.n == 0:
                                e.wait_ge(cleared, 2)
                            wait(e, acc_n_ready, g.n - 1)
                            wait(e, acc_ready, g.n)
                            wait(e, catch_done, g.n - 1)
                            gate(e)
                            e.scalar_tensor_tensor(out=open_acc[:, s, :], in0=open_acc[:, 1 - s, :], scalar=col(same_prev, g.n),
                                                   in1=p_msg[s][:, 0:D], op0=ALU.mult, op1=ALU.add).then_inc(acc_ready, 1)
                        if l == 1 and (g := t.ago(10)):
                            s = g.k % 2
                            e.wait_ge(h_ready, g.n + 1)
                            wait(e, row_ready, g.n - 3)
                            e.tensor_tensor(xs[:, g.k % 4, :], h_out[:, s, :], rows_in[:, g.k, DST, :], ALU.add).then_inc(sum_ready, 1)
                        if l == 1 and (g := t.ago(12)):
                            s = g.k % 2
                            e.wait_ge(rstd_ready, g.n + 1)
                            e.tensor_scalar(x1_out[:, g.k, :], xs[:, g.k % 4, :], mv[:, g.k % 4, 0:1], rstd[:, s:s + 1],
                                            ALU.subtract, ALU.mult).then_inc(row_ready, 1)
                        if l == 1 and (g := t.ago(10)):
                            s = g.k % 2
                            e.wait_ge(sum_ready, g.n + 1)
                            e.bn_stats(stats[:, s, :], xs[:, g.k % 4, :]).then_inc(stats_ready, 1)
                        if l == 1 and (g := t.ago(10)):
                            s = g.k % 2
                            e.wait_ge(stats_ready, g.n + 1)
                            gate(e)
                            e.bn_aggr(mv[:, g.k % 4, :], stats[:, s, :]).then_inc(mv_ready, 1)
                        if (g := t.ago(4)):
                            e.wait_ge(acc_ready, g.n + 1)
                            wait(e, catch_done, g.n)
                            gate(e)
                            e.scalar_tensor_tensor(out=caught[:], in0=open_acc[:, g.k % 2, :], scalar=col(cap_end, g.n),
                                                   in1=caught[:], op0=ALU.mult, op1=ALU.add).then_inc(catch_done, 1)

                    over_tiles(e, COLS, MUN, LAG, step)

            if l == 1:
                gathered.passed(COLS // MUN)
            scattered.passed(COLS // MUN)

        def layer_border(l):
            with ExitStack() as c:
                acc = sb("acc", [P, D], F32, c)
                acc_n = sb("acc_n", [P, D], F32, c)
                turned = sb("turned", [P, 2 * P], F32, c)
                low = sb("low", [P, D], F32, c)
                h = sb("h", [P, D], F32, c)
                xs = sb("xs", [P, D], F32, c)
                x1 = sb("x1", [P, D], F32, c)
                stats = sb("stats", [P, 6], F32, c)
                mv = sb("mv", [P, 2], F32, c)
                std = sb("std", [P, 1], F32, c)
                rstd = sb("rstd", [P, 1], F32, c)
                p_open = ps("p_open", c)
                p_turn = ps("p_turn", c)
                p_h = ps("p_h", c)
                x_in = border_gathered
                open_ready = sem("open_ready", c)
                acc_ready = sem("acc_ready", c)
                both_turned = sem("both_turned", c)
                turned_ready = sem("turned_ready", c)
                h_prod = sem("h_prod", c)
                low_ready = sem("low_ready", c)
                std_ready = sem("std_ready", c)
                mv_ready = sem("mv_ready", c)
                dve_done = sem("dve_done", c)
                row_ready = sem("row_ready", c)
                block = program(c)

                @block.gpsimd
                def _(e):
                    if l == 0:
                        e.indirect_dma_start(out=border_x[:], out_offset=None, in_=x,
                                             in_offset=bass.IndirectOffsetOnAxis(ap=border[:, RD_FIRST:RD_FIRST + 1], axis=0))\
                            .then_inc(x_in[0], 16)
                    e.wait_ge(row_ready, 1)
                    where = bass.IndirectOffsetOnAxis(ap=border[:, WR_FIRST:WR_FIRST + 1], axis=0)
                    if l == 0:
                        e.indirect_dma_start(out=h1_table, in_=border_h[:], in_offset=None, out_offset=where,
                                             bounds_check=N - 1, oob_is_err=False).then_inc(border_scattered[0], 16)
                        e.wait_ge(border_scattered[0], border_scattered.after(1))
                    else:
                        e.indirect_dma_start(out=x1_table, in_=x1[:], in_offset=None, out_offset=where,
                                             bounds_check=N - 1, oob_is_err=False).then_inc(border_scattered[0], 16)
                        e.indirect_dma_start(out=tile_x1, in_=x1[:], in_offset=None,
                                             out_offset=bass.IndirectOffsetOnAxis(ap=border[:, POS_FIRST:POS_FIRST + 1], axis=0),
                                             bounds_check=ROWS - 1, oob_is_err=False).then_inc(border_scattered[0], 16)
                        e.wait_ge(border_scattered[0], border_scattered.after(2))

                @block.tensor
                def _(e):
                    e.matmul(p_open[:, 0:D], after[:], open_acc[:, (COLS - 1) % 2, :], start=True, stop=True).then_inc(open_ready, 1)
                    e.wait_ge(acc_ready, 1)
                    if l == 0:
                        e.wait_ge(x_in[0], x_in.after(1))
                    e.transpose(p_turn[:, 0:P], acc_n[:], ident[:])
                    e.transpose(p_turn[:, P:2 * P], (border_x, border_h)[l][:], ident[:]).then_inc(both_turned, 1)
                    e.wait_ge(turned_ready, 1)
                    e.matmul(p_h[:, 0:D], turned[:, 0:P], w_r[l][:], start=True, stop=False)
                    e.matmul(p_h[:, 0:D], turned[:, P:2 * P], w_sl[l][:], start=False, stop=True).then_inc(h_prod, 1)

                @block.scalar
                def _(e):
                    e.wait_ge(both_turned, 1)
                    e.activation(turned[:], p_turn[:, 0:2 * P], ACT.Copy).then_inc(turned_ready, 1)
                    e.wait_ge(h_prod, 1)
                    e.activation(low[:], p_h[:, 0:D], ACT.Copy, scale=SLOPE).then_inc(low_ready, 1)
                    if l == 1:
                        e.wait_ge(mv_ready, 1)
                        e.activation(std[:], mv[:, 1:2], ACT.Sqrt, bias=eps[:]).then_inc(std_ready, 1)

                @block.vector
                def _(e):
                    e.wait_ge(open_ready, 1)
                    e.tensor_tensor(acc[:], p_open[:, 0:D], caught[:], ALU.add).then_inc(dve_done, 1)
                    e.wait_ge(dve_done, 1)
                    e.tensor_scalar(acc_n[:], acc[:], border_norm[:], None, ALU.mult).then_inc(acc_ready, 1)
                    e.wait_ge(low_ready, 1)
                    if l == 0:
                        e.tensor_tensor(border_h[:], low[:], p_h[:, 0:D], ALU.max).then_inc(row_ready, 1)
                        return
                    e.tensor_tensor(h[:], low[:], p_h[:, 0:D], ALU.max).then_inc(dve_done, 1)
                    e.wait_ge(dve_done, 2)
                    e.tensor_tensor(xs[:], h[:], border_x[:], ALU.add).then_inc(dve_done, 1)
                    e.wait_ge(dve_done, 3)
                    e.bn_stats(stats[:], xs[:]).then_inc(dve_done, 1)
                    e.wait_ge(dve_done, 4)
                    e.bn_aggr(mv[:], stats[:]).then_inc(mv_ready, 1)
                    e.wait_ge(std_ready, 1)
                    e.reciprocal(rstd[:], std[:]).then_inc(dve_done, 1)
                    e.wait_ge(dve_done, 5)
                    e.tensor_scalar(x1[:], xs[:], mv[:, 0:1], rstd[:], ALU.subtract, ALU.mult).then_inc(row_ready, 1)

            if l == 0:
                border_gathered.passed(1)
            border_scattered.passed(1 + l)

        def attention(values, logits):
            with ExitStack() as c:
                x_src = sb("x_src", [P, UN, D], F32, c)
                x_end = sb("x_end", [P, UN, D], F32, c)
                at_end = sb("at_end", [P, 2, D], F32, c)
                xv_dst = sb("xv_dst", [P, UN, 2, D], F32, c)
                qk = sb("qk", [P, 2, 3, D], F32, c)
                use = sb("use", [P, UN, 1], I32, c)
                x_open = sb("x_open", [P, D], F32, c)
                stats = sb("stats", [P, 2, 2, 6], F32, c)
                mv = sb("mv", [P, 2, 2, 2], F32, c)
                std = sb("std", [P, 2, 2], F32, c)
                rstd = sb("rstd", [P, 2, 2], F32, c)
                shift = sb("shift", [P, 2, 2], F32, c)
                normed = sb("normed", [P, 2, 2, D], F32, c)
                turned = sb("turned", [P, 2, 2 * P], F32, c)
                prod = sb("prod", [P, 2, 2, D], F32, c)
                p_turn = [ps(f"p_turn{s}", c) for s in range(2)]
                p_qk = [ps(f"p_qk{s}", c) for s in range(2)]
                p_v = [ps(f"p_v{s}", c) for s in range(2)]
                open_in = border_gathered
                src_in = gathered.first(UN)
                end_in = sems("end_in", UN, c)
                stored = sems("stored", UN, c)
                copied = sem("copied", c)
                use_ready = sem("use_ready", c)
                at_end_ready = sem("at_end_ready", c)
                x_ready = sem("x_ready", c)
                stats_ready = sem("stats_ready", c)
                mv_ready = sem("mv_ready", c)
                std_ready = sem("std_ready", c)
                rstd_ready = sem("rstd_ready", c)
                shift_ready = sem("shift_ready", c)
                normed_ready = sem("normed_ready", c)
                both_turned = sem("both_turned", c)
                turned_ready = sem("turned_ready", c)
                qkv_ready = sem("qkv_ready", c)
                qk_out = sem("qk_out", c)
                v_out = sem("v_out", c)
                prod_ready = sem("prod_ready", c)
                logit_ready = sem("logit_ready", c)
                block = program(c)
                LAG = 11

                def chunks(table):
                    return table.rearrange("n d -> (n d)").rearrange("(r c) -> r c", r=16 * COLS // 2)

                def j(g):
                    return COLS - 1 - g.n

                @block.gpsimd
                def _(e):
                    e.indirect_dma_start(out=x_open[:], out_offset=None, in_=x1_table,
                                         in_offset=bass.IndirectOffsetOnAxis(ap=border[:, RD_LAST:RD_LAST + 1], axis=0))\
                        .then_inc(open_in[0], 16)

                    def step(t):
                        if (g := t.ago(0)):
                            wait(e, normed_ready, g.n - UN + 1)
                            gate(e)
                            e.tensor_copy(use[:, g.k, :], col(idx[:, SRC, :], j(g))).then_inc(use_ready, 1)
                            e.wait_ge(use_ready, g.n + 1)
                            gate(e)
                            e.indirect_dma_start(out=x_src[:, g.k, :], out_offset=None, in_=x1_table,
                                                 in_offset=bass.IndirectOffsetOnAxis(ap=use[:, g.k, 0:1], axis=0))\
                                .then_inc(src_in[g.k], 16)
                        if (g := t.ago(10)):
                            s = g.k % 2
                            e.wait_ge(qk_out, g.n + 1)
                            wait(e, logit_ready, g.n - 1)
                            gate(e)
                            e.tensor_tensor(prod[:, s, :, :], qk[:, s, 1:3, :],
                                            qk[:, s, 0:1, :].to_broadcast([P, 2, D]), ALU.mult).then_inc(prod_ready, 1)

                    over_tiles(e, COLS, UN, LAG, step, peeled=2)

                @block.sync
                def _(e):
                    def step(t):
                        if (g := t.ago(0)) and g.k % 2 == 0:
                            chunk = bass.ds(g.half() * 16, 16)
                            e.dma_start(chunks(x2_table)[chunk, :], chunks(x1_table)[chunk, :]).then_inc(copied, 16)
                        if (g := t.ago(11)):
                            e.wait_ge(v_out, g.n + 1)
                            gate(e)
                            e.wait_ge(x_ready, g.n + 1)
                            gate(e)
                            e.dma_start(tile_xv[bass.ds(j(g) * P, P), :],
                                        xv_dst[:, g.k, :, :].rearrange("p a d -> p (a d)")).then_inc(stored[g.k], 16)
                        if (g := t.ago(0)):
                            wait(e, at_end_ready, g.n - UN + 1)
                            gate(e)
                            e.dma_start(x_end[:, g.k, :], tile_x1[bass.ds(j(g) * P, P), :]).then_inc(end_in[g.k], 16)

                    over_tiles(e, COLS, UN, LAG, step, peeled=2)
                    for k in range(UN):
                        e.wait_ge(stored[k], 16 * (COLS // UN))
                    e.wait_ge(copied, 16 * (COLS // 2))

                @block.tensor
                def _(e):
                    def step(t):
                        if (g := t.ago(8)):
                            s = g.k % 2
                            e.wait_ge(turned_ready, g.n + 1)
                            wait(e, qk_out, g.n - 1)
                            wait(e, v_out, g.n - 1)
                            dst_T, src_T = turned[:, s, 0:P], turned[:, s, P:2 * P]
                            e.matmul(p_qk[s][:, 0:2 * D], dst_T, w_vqk[:, D:3 * D], start=True, stop=True)
                            e.matmul(p_v[s][:, 0:D], dst_T, w_vqk[:, 0:D], start=True, stop=True)
                            e.matmul(p_qk[s][:, 2 * D:3 * D], src_T, w_vqk[:, 2 * D:3 * D], start=True, stop=True)
                            e.matmul(p_v[s][:, D:2 * D], src_T, w_vqk[:, 0:D], start=True, stop=True).then_inc(qkv_ready, 1)
                        if (g := t.ago(6)):
                            s = g.k % 2
                            e.wait_ge(normed_ready, g.n + 1)
                            wait(e, turned_ready, g.n - 1)
                            for a in range(2):
                                mm = e.transpose(p_turn[s][:, a * P:(a + 1) * P], normed[:, s, a, :], ident[:])
                            mm.then_inc(both_turned, 1)

                    over_tiles(e, COLS, UN, LAG, step, peeled=2)

                @block.scalar
                def _(e):
                    def step(t):
                        if (g := t.ago(1)):
                            s = g.k % 2
                            e.wait_ge(end_in[g.k], 16 * (g.b + 1))
                            wait(e, x_ready, g.n - 1)
                            e.activation(at_end[:, s, :], x_end[:, g.k, :], ACT.Copy, scale=col(is_end, j(g)))\
                                .then_inc(at_end_ready, 1)
                        if (g := t.ago(3)):
                            s = g.k % 2
                            e.wait_ge(mv_ready, g.n + 1)
                            wait(e, rstd_ready, g.n - 1)
                            e.activation(std[:, s, :], mv[:, s, :, 1], ACT.Sqrt, bias=eps[:]).then_inc(std_ready, 1)
                        if (g := t.ago(5)):
                            s = g.k % 2
                            e.wait_ge(shift_ready, g.n + 1)
                            wait(e, both_turned, g.n - 1)
                            for a, row in ((0, xv_dst[:, g.k, 0, :]), (1, x_src[:, g.k, :])):
                                ins = e.activation(normed[:, s, a, :], row, ACT.Identity, scale=rstd[:, s, a:a + 1],
                                                   bias=shift[:, s, a:a + 1])
                            ins.then_inc(normed_ready, 1)
                        if (g := t.ago(7)):
                            s = g.k % 2
                            e.wait_ge(both_turned, g.n + 1)
                            wait(e, qkv_ready, g.n - 1)
                            e.activation(turned[:, s, :], p_turn[s][:, 0:2 * P], ACT.Copy).then_inc(turned_ready, 1)
                        if (g := t.ago(9)):
                            s = g.k % 2
                            e.wait_ge(qkv_ready, g.n + 1)
                            e.activation(xv_dst[:, g.k, 1, :], p_v[s][:, 0:D], ACT.Copy)
                            e.activation(values[:, bass.ds(j(g), 1), :].rearrange("p a d -> p (a d)"), p_v[s][:, D:2 * D], ACT.Copy)\
                                .then_inc(v_out, 1)

                    over_tiles(e, COLS, UN, LAG, step, peeled=2)

                @block.vector
                def _(e):
                    def step(t):
                        if (g := t.ago(4)):
                            s = g.k % 2
                            e.wait_ge(std_ready, g.n + 1)
                            wait(e, normed_ready, g.n - 1)
                            e.reciprocal(rstd[:, s, :], std[:, s, :]).then_inc(rstd_ready, 1)
                        if (g := t.ago(9)):
                            s = g.k % 2
                            e.wait_ge(qkv_ready, g.n + 1)
                            wait(e, prod_ready, g.n - 1)
                            e.tensor_tensor(qk[:, s, :, :].rearrange("p a d -> p (a d)"),
                                            p_qk[s][:, 0:3 * D], bias_vqk[:, D:4 * D], ALU.add).then_inc(qk_out, 1)
                        if (g := t.ago(4)):
                            s = g.k % 2
                            e.wait_ge(rstd_ready, g.n + 1)
                            e.scalar_tensor_tensor(out=shift[:, s, :], in0=mv[:, s, :, 0], scalar=-1.0, in1=rstd[:, s, :],
                                                   op0=ALU.mult, op1=ALU.mult).then_inc(shift_ready, 1)
                        if (g := t.ago(2)):
                            s = g.k % 2
                            e.wait_ge(at_end_ready, g.n + 1)
                            if isinstance(g.n, int) and g.n == 0:
                                e.wait_ge(open_in[0], open_in.after(1))
                                before_row = x_open[:]
                            else:
                                before_row = xv_dst[:, (g.k - 1) % UN, 0, :]
                            wait(e, stored[g.k], 16 * g.b)
                            wait(e, x_ready, g.n)
                            gate(e)
                            e.scalar_tensor_tensor(out=xv_dst[:, g.k, 0, :], in0=before_row, scalar=col(keep_x, j(g)),
                                                   in1=at_end[:, s, :], op0=ALU.mult, op1=ALU.add).then_inc(x_ready, 1)
                        if (g := t.ago(2)):
                            s = g.k % 2
                            e.wait_ge(x_ready, g.n + 1)
                            e.wait_ge(src_in[g.k], src_in.after(g.b + 1))
                            wait(e, mv_ready, g.n - 1)
                            e.bn_stats(stats[:, s, 0, :], xv_dst[:, g.k, 0, :])
                            e.bn_stats(stats[:, s, 1, :], x_src[:, g.k, :]).then_inc(stats_ready, 1)
                        if (g := t.ago(11)):
                            s = g.k % 2
                            e.wait_ge(prod_ready, g.n + 1)
                            gate(e)
                            e.tensor_reduce(logits[:, :, bass.ds(j(g), 1)].rearrange("p h a -> p (h a)"),
                                            prod[:, s, :, :].rearrange("p a (h d) -> p (a h) d", h=HEADS), AX_X, ALU.add)\
                                .then_inc(logit_ready, 1)
                        if (g := t.ago(2)):
                            s = g.k % 2
                            e.wait_ge(stats_ready, g.n + 1)
                            wait(e, shift_ready, g.n - 1)
                            wait(e, std_ready, g.n - 1)
                            gate(e)
                            for a in range(2):
                                ins = e.bn_aggr(mv[:, s, a, :], stats[:, s, a, :])
                            ins.then_inc(mv_ready, 1)

                    over_tiles(e, COLS, UN, LAG, step, peeled=2)

            border_gathered.passed(1)

        def softmax(logits, weight, z_inv, self_weight, border_z):
            SCALE = 1.0 / HD ** 0.5
            with ExitStack() as c:
                both = sb("both", [P, HEADS, COLS], F32, c)
                gap_prev = sb("gap_prev", [P, HEADS, COLS], F32, c)
                gap_next = sb("gap_next", [P, HEADS, COLS], F32, c)
                top = z_inv
                top_next = self_weight
                sides = sb("sides", [P, 2, HEADS], F32, c)
                all_sides = sb("all_sides", [P, 2 * P, HEADS], F32, c)
                miss = sb("miss", [P, 2, 2 * P], F32, c)
                cand = sb("cand", [P, HEADS, 2 * P], F32, c)
                top_side = sb("top_side", [P, 2, HEADS], F32, c)
                dve_done = sem("dve_done", c)
                sides_ready = sem("sides_ready", c)
                sides_out = sem("sides_out", c)
                sides_in = sem("sides_in", c)
                gaps_ready = sem("gaps_ready", c)
                exp_done = sem("exp_done", c)
                block = program(c)
                self_logit, edge_logit = logits[:, 0:HEADS, :], logits[:, HEADS:2 * HEADS, :]

                def flat(t):
                    return t[:].rearrange("p h j -> p (h j)")

                def over_heads(mask):
                    return mask[:].unsqueeze(1).to_broadcast([P, HEADS, COLS])

                @block.sync
                def _(e):
                    e.wait_ge(sides_ready, 1)
                    for s in range(2):
                        e.dma_start(open_max[s * P:(s + 1) * P, :], sides[:, s, :]).then_inc(sides_out, 16)
                    e.wait_ge(sides_out, 32)
                    e.dma_start(all_sides[:].rearrange("p q h -> p (q h)"),
                                open_max.rearrange("q h -> (q h)").partition_broadcast(P)).then_inc(sides_in, 16)

                @block.scalar
                def _(e):
                    e.wait_ge(gaps_ready, 1)
                    e.activation(flat(weight), flat(both), ACT.Exp, scale=SCALE).then_inc(exp_done, 1)
                    e.activation(flat(self_weight), flat(gap_prev), ACT.Exp, scale=SCALE).then_inc(exp_done, 1)

                @block.vector
                def _(e):
                    made = [0]

                    def chain(ins):
                        made[0] += 1
                        ins.then_inc(dve_done, 1)
                        e.wait_ge(dve_done, made[0])

                    e.tensor_scalar(gap_prev[:], over_heads(same_prev), -1.0, LOW, ALU.add, ALU.mult)
                    e.tensor_scalar(gap_next[:], over_heads(same_next), -1.0, LOW, ALU.add, ALU.mult)
                    chain(e.tensor_tensor(both[:], self_logit, edge_logit, ALU.max))
                    e.tensor_tensor_scan(flat(top), flat(gap_prev), flat(both), -LOW, ALU.add, ALU.max)
                    chain(e.tensor_tensor_scan(flat(top_next)[:, ::-1], flat(gap_next)[:, ::-1], flat(both)[:, ::-1], -LOW,
                                               ALU.add, ALU.max))
                    e.tensor_copy(sides[:, 0, :], top_next[:, :, 0])
                    e.tensor_copy(sides[:, 1, :], top[:, :, COLS - 1]).then_inc(sides_ready, 1)
                    e.wait_ge(sides_ready, 1)
                    chain(e.tensor_tensor(flat(top), flat(top), flat(top_next), ALU.max))
                    for s in range(2):
                        ins = e.tensor_scalar(miss[:, s, :], first_last[:], dst_fl[:, s:s + 1], None, ALU.is_equal)
                    chain(ins)
                    e.wait_ge(sides_in, 16)
                    for s in range(2):
                        chain(e.tensor_scalar(miss[:, s, :], miss[:, s, :], -1.0, LOW, ALU.add, ALU.mult))
                        chain(e.tensor_tensor(cand[:], all_sides[:].rearrange("p q h -> p h q"),
                                              miss[:, s, :].unsqueeze(1).to_broadcast([P, HEADS, 2 * P]), ALU.add))
                        chain(e.tensor_reduce(top_side[:, s, :], cand[:], AX_X, ALU.max))
                    for s, inside in enumerate((in_first, in_last)):
                        for h in range(HEADS):
                            ins = e.scalar_tensor_tensor(out=top[:, h, :], in0=inside[:], scalar=top_side[:, s, h:h + 1],
                                                         in1=top[:, h, :], op0=ALU.add, op1=ALU.max)
                        chain(ins)
                    e.tensor_tensor(both[:], edge_logit, top[:], ALU.subtract)
                    e.tensor_tensor(gap_prev[:], self_logit, top[:], ALU.subtract).then_inc(gaps_ready, 1)
                    chain(e.tensor_copy(gap_next[:], over_heads(same_next)))
                    e.wait_ge(exp_done, 2)
                    z = z_inv
                    chain(e.tensor_tensor_scan(flat(z)[:, ::-1], flat(gap_next)[:, ::-1], flat(weight)[:, ::-1], 0.0,
                                               ALU.mult, ALU.add))
                    chain(e.tensor_tensor(both[:], z[:], over_heads(cap_start), ALU.mult))
                    e.tensor_reduce(border_z[:, 0, :], both[:], AX_X, ALU.add)
                    e.tensor_copy(border_z[:, 1, :], z[:, :, 0])
                    chain(e.tensor_tensor(gap_prev[:], self_weight[:], over_heads(cap_start), ALU.mult))
                    e.tensor_reduce(border_z[:, 2, :], gap_prev[:], AX_X, ALU.add)
                    chain(e.tensor_tensor(flat(z), flat(z), flat(self_weight), ALU.add))
                    chain(e.tensor_scalar(flat(z), flat(z), 1e-30, None, ALU.max))
                    chain(e.reciprocal(flat(z_inv), flat(z)))
                    chain(e.tensor_tensor(flat(self_weight), flat(self_weight), flat(z_inv), ALU.mult))

        def weighted(values, weight, z_inv, self_weight):
            with ExitStack() as c:
                xv = sb("xv", [P, UN, 2 * D], F32, c)
                use = sb("use", [P, UN, 1], I32, c)
                own = sb("own", [P, 2, D], F32, c)
                wv = sb("wv", [P, 2, D], F32, c)
                scaled = sb("scaled", [P, 2, D], F32, c)
                attT = sb("attT", [P, 2, P], F32, c)
                x2_out = sb("x2_out", [P, UN, D], F32, c)
                p_sum = [ps(f"p_sum{s}", c) for s in range(2)]
                p_out = [ps(f"p_out{s}", c) for s in range(2)]
                xv_in = sems("xv_in", UN, c)
                use_ready = sem("use_ready", c)
                x2_scattered = scattered.first(UN)
                own_ready = sem("own_ready", c)
                cleared = sem("cleared", c)
                wv_ready = sem("wv_ready", c)
                acc_ready = sem("acc_ready", c)
                catch_done = sem("catch_done", c)
                scaled_ready = sem("scaled_ready", c)
                sum_ready = sem("sum_ready", c)
                attT_ready = sem("attT_ready", c)
                prod_ready = sem("prod_ready", c)
                row_ready = sem("row_ready", c)
                block = program(c)
                LAG = 8

                def j(g):
                    return COLS - 1 - g.n

                @block.sync
                def _(e):
                    def step(t):
                        if (g := t.ago(0)):
                            wait(e, row_ready, g.n - UN + 1)
                            gate(e)
                            e.dma_start(xv[:, g.k, :], tile_xv[bass.ds(j(g) * P, P), :]).then_inc(xv_in[g.k], 16)

                    over_tiles(e, COLS, UN, LAG, step)

                @block.gpsimd
                def _(e):
                    def step(t):
                        if (g := t.ago(7)):
                            wait(e, x2_scattered[g.k], x2_scattered.after(g.b))
                            gate(e)
                            e.tensor_copy(use[:, g.k, :], col(idx[:, AT_START, :], j(g))).then_inc(use_ready, 1)
                        if (g := t.ago(8)):
                            e.wait_ge(use_ready, g.n + 1)
                            e.wait_ge(row_ready, g.n + 1)
                            gate(e)
                            e.indirect_dma_start(out=x2_table, in_=x2_out[:, g.k, :], in_offset=None,
                                                 out_offset=bass.IndirectOffsetOnAxis(ap=use[:, g.k, 0:1], axis=0),
                                                 bounds_check=N - 1, oob_is_err=False).then_inc(x2_scattered[g.k], 16)

                    over_tiles(e, COLS, UN, LAG, step)
                    for k in range(UN):
                        e.wait_ge(x2_scattered[k], x2_scattered.after(COLS // UN))

                @block.vector
                def _(e):
                    e.memset(open_acc[:], 0.0).then_inc(cleared, 1)
                    e.memset(caught[:], 0.0).then_inc(cleared, 1)

                    def step(t):
                        if (g := t.ago(2)):
                            s = g.k % 2
                            e.wait_ge(acc_ready, g.n + 1)
                            wait(e, sum_ready, g.n - 1)
                            gate(e)
                            e.tensor_tensor(heads(scaled[:, s, :]), heads(open_acc[:, s, :]), per_head(z_inv, j(g)), ALU.mult)\
                                .then_inc(scaled_ready, 1)
                        if (g := t.ago(1)):
                            s = g.k % 2
                            e.wait_ge(wv_ready, g.n + 1)
                            if isinstance(g.n, int) and g.n == 0:
                                e.wait_ge(cleared, 2)
                            wait(e, acc_ready, g.n)
                            wait(e, scaled_ready, g.n - 1)
                            wait(e, catch_done, g.n - 1)
                            gate(e)
                            e.scalar_tensor_tensor(out=open_acc[:, s, :], in0=open_acc[:, 1 - s, :], scalar=col(same_next, j(g)),
                                                   in1=wv[:, s, :], op0=ALU.mult, op1=ALU.add).then_inc(acc_ready, 1)
                        if (g := t.ago(0)):
                            s = g.k % 2
                            wait(e, acc_ready, g.n - 1)
                            gate(e)
                            e.tensor_tensor(heads(wv[:, s, :]), heads(values[:, bass.ds(j(g), 1), :].rearrange("p a d -> p (a d)")),
                                            per_head(weight, j(g)), ALU.mult).then_inc(wv_ready, 1)
                        if (g := t.ago(2)):
                            s = g.k % 2
                            e.wait_ge(xv_in[g.k], 16 * (g.b + 1))
                            gate(e)
                            e.tensor_tensor(heads(own[:, s, :]), heads(xv[:, g.k, D:2 * D]), per_head(self_weight, j(g)), ALU.mult)\
                                .then_inc(own_ready, 1)
                        if (g := t.ago(1)):
                            s = g.k % 2
                            e.wait_ge(acc_ready, g.n + 1)
                            wait(e, catch_done, g.n)
                            gate(e)
                            e.scalar_tensor_tensor(out=caught[:], in0=open_acc[:, s, :], scalar=col(cap_start, j(g)),
                                                   in1=caught[:], op0=ALU.mult, op1=ALU.add).then_inc(catch_done, 1)

                    over_tiles(e, COLS, UN, LAG, step)

                @block.tensor
                def _(e):
                    def step(t):
                        if (g := t.ago(3)):
                            s = g.k % 2
                            e.wait_ge(scaled_ready, g.n + 1)
                            e.wait_ge(own_ready, g.n + 1)
                            wait(e, attT_ready, g.n - 1)
                            e.matmul(p_sum[s][:, 0:P], scaled[:, s, :], ident[:], start=True, stop=False)
                            e.matmul(p_sum[s][:, 0:P], own[:, s, :], ident[:], start=False, stop=True).then_inc(sum_ready, 1)
                        if (g := t.ago(5)):
                            s = g.k % 2
                            e.wait_ge(attT_ready, g.n + 1)
                            wait(e, row_ready, g.n - 1)
                            e.matmul(p_out[s][:, 0:D], attT[:, s, :], w_o[:], start=True, stop=False)
                            e.matmul(p_out[s][:, 0:D], ident[:], xv[:, g.k, 0:D], start=False, stop=False)
                            e.matmul(p_out[s][:, 0:D], ident[:], att_bias[:], start=False, stop=True).then_inc(prod_ready, 1)

                    over_tiles(e, COLS, UN, LAG, step)

                @block.scalar
                def _(e):
                    def step(t):
                        if (g := t.ago(4)):
                            s = g.k % 2
                            e.wait_ge(sum_ready, g.n + 1)
                            wait(e, prod_ready, g.n - 1)
                            e.activation(attT[:, s, :], p_sum[s][:, 0:P], ACT.Copy).then_inc(attT_ready, 1)
                        if (g := t.ago(6)):
                            e.wait_ge(prod_ready, g.n + 1)
                            e.wait_ge(x2_scattered[g.k], x2_scattered.after(g.b))
                            e.activation(x2_out[:, g.k, :], p_out[g.k % 2][:, 0:D], ACT.Copy).then_inc(row_ready, 1)

                    over_tiles(e, COLS, UN, LAG, step)

        def weighted_border(border_z):
            with ExitStack() as c:
                xv = sb("xv", [P, 2 * D], F32, c)
                acc = sb("acc", [P, D], F32, c)
                own = sb("own", [P, D], F32, c)
                z = sb("z", [P, HEADS], F32, c)
                x_bias = sb("x_bias", [P, D], F32, c)
                attT = sb("attT", [P, P], F32, c)
                x2 = sb("x2", [P, D], F32, c)
                p_open = ps("p_open", c)
                p_z = ps("p_z", c)
                p_turn = ps("p_turn", c)
                p_out = ps("p_out", c)
                xv_in = border_gathered
                open_ready = sem("open_ready", c)
                dve_done = sem("dve_done", c)
                att_ready = sem("att_ready", c)
                att_turned = sem("att_turned", c)
                attT_ready = sem("attT_ready", c)
                prod_ready = sem("prod_ready", c)
                row_ready = sem("row_ready", c)
                block = program(c)

                @block.gpsimd
                def _(e):
                    e.indirect_dma_start(out=xv[:], out_offset=None, in_=tile_xv,
                                         in_offset=bass.IndirectOffsetOnAxis(ap=border[:, POS_LAST:POS_LAST + 1], axis=0))\
                        .then_inc(xv_in[0], 16)
                    e.wait_ge(row_ready, 1)
                    e.indirect_dma_start(out=x2_table, in_=x2[:], in_offset=None,
                                         out_offset=bass.IndirectOffsetOnAxis(ap=border[:, WR_LAST:WR_LAST + 1], axis=0),
                                         bounds_check=N - 1, oob_is_err=False).then_inc(border_scattered[0], 16)
                    e.wait_ge(border_scattered[0], border_scattered.after(1))

                @block.tensor
                def _(e):
                    e.matmul(p_open[:, 0:D], before[:], open_acc[:, (COLS - 1) % 2, :], start=True, stop=True)
                    e.matmul(p_z[:, 0:HEADS], before[:], border_z[:, 1, :], start=True, stop=True).then_inc(open_ready, 1)
                    e.wait_ge(att_ready, 1)
                    e.transpose(p_turn[:, 0:P], acc[:], ident[:]).then_inc(att_turned, 1)
                    e.wait_ge(attT_ready, 1)
                    e.matmul(p_out[:, 0:D], attT[:], w_o[:], start=True, stop=True).then_inc(prod_ready, 1)

                @block.scalar
                def _(e):
                    e.wait_ge(att_turned, 1)
                    e.activation(attT[:], p_turn[:, 0:P], ACT.Copy).then_inc(attT_ready, 1)

                @block.vector
                def _(e):
                    made = [0]

                    def chain(ins):
                        made[0] += 1
                        ins.then_inc(dve_done, 1)
                        e.wait_ge(dve_done, made[0])

                    def wide(w):
                        return w.unsqueeze(2).to_broadcast([P, HEADS, HD])

                    e.wait_ge(open_ready, 1)
                    e.wait_ge(xv_in[0], xv_in.after(1))
                    chain(e.tensor_tensor(acc[:], caught[:], p_open[:, 0:D], ALU.add))
                    chain(e.tensor_tensor(z[:], border_z[:, 0, :], p_z[:, 0:HEADS], ALU.add))
                    chain(e.tensor_tensor(z[:], z[:], border_z[:, 2, :], ALU.add))
                    chain(e.tensor_scalar(z[:], z[:], 1e-30, None, ALU.max))
                    chain(e.reciprocal(z[:], z[:]))
                    chain(e.tensor_tensor(heads(own[:]), heads(xv[:, D:2 * D]), wide(border_z[:, 2, :]), ALU.mult))
                    chain(e.tensor_tensor(acc[:], acc[:], own[:], ALU.add))
                    e.tensor_tensor(heads(acc[:]), heads(acc[:]), wide(z[:]), ALU.mult).then_inc(att_ready, 1)
                    chain(e.tensor_tensor(x_bias[:], xv[:, 0:D], att_bias[:], ALU.add))
                    e.wait_ge(prod_ready, 1)
                    e.tensor_tensor(x2[:], p_out[:, 0:D], x_bias[:], ALU.add).then_inc(row_ready, 1)

        def ffn():
            with ExitStack() as c:
                y_in = sb("y_in", [P, GUN, GROUP], F32, c)
                both = sb("both", [P, GUN, GROUP], F32, c)
                normed = sb("normed", [P, 2, GROUP], F32, c)
                nT = sb("nT", [P, 2, GROUP], F32, c)
                g_T = sb("g_T", [P, 2, FCH, GROUP], F32, c)
                yT = sb("yT", [P, 2, GROUP], F32, c)
                res = sb("res", [P, GUN, GROUP], F32, c)
                stats = sb("stats", [P, 2, GT, 6], F32, c)
                mv = sb("mv", [P, GUN, GT, 2], F32, c)
                var = sb("var", [P, 2, GT], F32, c)
                rstd = sb("rstd", [P, 2, GT], F32, c)
                stats2 = sb("stats2", [P, 2, GT, 6], F32, c)
                mv2 = sb("mv2", [P, GUN, GT, 2], F32, c)
                var2 = sb("var2", [P, 2, GT], F32, c)
                rstd2 = sb("rstd2", [P, 2, GT], F32, c)
                p_n = ps("p_n", c)
                p_f = [ps(f"p_f{s}", c) for s in range(4)]
                p_y = ps("p_y", c)
                p_r = [ps(f"p_r{s}", c) for s in range(2)]
                x1_loaded = sems("x1_loaded", GUN, c)
                y_loaded = sems("y_loaded", GUN, c)
                stored = sems("stored", GUN, c)
                x2_ready = sem("x2_ready", c)
                both_ready = sem("both_ready", c)
                stats_ready = sem("stats_ready", c)
                mv_ready = sem("mv_ready", c)
                var_ready = sem("var_ready", c)
                rstd_ready = sem("rstd_ready", c)
                normed_ready = sem("normed_ready", c)
                n_turned = sem("n_turned", c)
                nT_ready = sem("nT_ready", c)
                f_prod = sem("f_prod", c)
                gelu_ready = sem("gelu_ready", c)
                y_prod = sem("y_prod", c)
                yT_ready = sem("yT_ready", c)
                y_turned = sem("y_turned", c)
                sum_ready = sem("sum_ready", c)
                stats2_ready = sem("stats2_ready", c)
                mv2_ready = sem("mv2_ready", c)
                var2_ready = sem("var2_ready", c)
                rstd2_ready = sem("rstd2_ready", c)
                res_ready = sem("res_ready", c)
                block = program(c)
                LAG = 14

                def per_row(ap):
                    return ap.rearrange("p (a d) -> p a d", a=GT)

                def rows(table, t):
                    return table[bass.ds(group_rows(t.n), GROUP), :].rearrange("(p a) d -> p (a d)", a=GT)

                @block.sync
                def _(e):
                    def step(t):
                        if (g := t.ago(14)):
                            if isinstance(g.n, int) and g.n == NG - 1:
                                e.wait_ge(stored[(g.n - 1) % GUN], 16 * ((g.n - 1) // GUN + 1))
                            gate(e)
                            e.wait_ge(res_ready, g.n + 1)
                            gate(e)
                            e.dma_start(rows(out, g), res[:, g.k, :]).then_inc(stored[g.k], 16)
                        if (g := t.ago(0)):
                            wait(e, both_ready, g.n - GUN + 1)
                            gate(e)
                            wait(e, normed_ready, g.n - GUN + 1)
                            gate(e)
                            wait(e, res_ready, g.n - GUN + 1)
                            gate(e)
                            wait(e, stored[g.k], 16 * g.b)
                            gate(e)
                            e.dma_start(y_in[:, g.k, :], rows(x2_table, g)).then_inc(y_loaded[g.k], 16)
                            e.dma_start(both[:, g.k, :], rows(x1_table, g)).then_inc(x1_loaded[g.k], 16)

                    over_tiles(e, NG, GUN, LAG, step)
                    for k in range(GUN):
                        e.wait_ge(stored[k], 16 * len(range(k, NG, GUN)))

                @block.gpsimd
                def _(e):
                    def inverse_root(g, mean_var, var, rstd, mean_ready, var_ready, rstd_ready, used):
                        s = g.k % 2
                        e.wait_ge(mean_ready, g.n + 1)
                        wait(e, used, g.n - 1)
                        gate(e)
                        e.tensor_scalar(var[:, s, :], mean_var[:, g.k, :, 1], EPS, None, ALU.add).then_inc(var_ready, 1)
                        e.wait_ge(var_ready, g.n + 1)
                        gate(e)
                        e.tensor_tensor(rstd[:, s, :], var[:, s, :], minus_half[:], ALU.pow).then_inc(rstd_ready, 1)

                    def step(t):
                        if (g := t.ago(3)):
                            inverse_root(g, mv, var, rstd, mv_ready, var_ready, rstd_ready, normed_ready)
                        if (g := t.ago(0)):
                            e.wait_ge(y_loaded[g.k], 16 * (g.b + 1))
                            gate(e)
                            e.tensor_tensor(per_row(y_in[:, g.k, :]), per_row(y_in[:, g.k, :]),
                                            bo_rows[:].unsqueeze(1).to_broadcast([P, GT, D]), ALU.add).then_inc(x2_ready, 1)
                        if (g := t.ago(12)):
                            inverse_root(g, mv2, var2, rstd2, mv2_ready, var2_ready, rstd2_ready, res_ready)
                        if (g := t.ago(1)):
                            e.wait_ge(x1_loaded[g.k], 16 * (g.b + 1))
                            e.wait_ge(x2_ready, g.n + 1)
                            gate(e)
                            e.tensor_tensor(both[:, g.k, :], both[:, g.k, :], y_in[:, g.k, :], ALU.add).then_inc(both_ready, 1)

                    over_tiles(e, NG, GUN, LAG, step)

                @block.tensor
                def _(e):
                    def step(t):
                        if (g := t.ago(7)):
                            s = g.k % 2
                            e.wait_ge(nT_ready, g.n + 1)
                            for ch in range(FCH):
                                wait(e, gelu_ready, FCH * g.n + ch - 3)
                                e.matmul(p_f[ch][:], w_1[:, ch * P:(ch + 1) * P], nT[:, s, :], start=True, stop=True)\
                                    .then_inc(f_prod, 1)
                        if (g := t.ago(5)):
                            e.wait_ge(normed_ready, g.n + 1)
                            wait(e, nT_ready, g.n)
                            for a in range(GT):
                                mm = e.transpose(p_n[:, a * P:(a + 1) * P], normed[:, g.k % 2, a * D:(a + 1) * D], ident[:])
                            mm.then_inc(n_turned, 1)
                        if (g := t.ago(8)):
                            s = g.k % 2
                            wait(e, yT_ready, g.n)
                            for ch in range(FCH):
                                e.wait_ge(gelu_ready, FCH * g.n + ch + 1)
                                mm = e.matmul(p_y[:], w_2[:, ch, :], g_T[:, s, ch, :], start=(ch == 0), stop=(ch == FCH - 1))
                            mm.then_inc(y_prod, 1)
                        if (g := t.ago(10)):
                            s = g.k % 2
                            e.wait_ge(yT_ready, g.n + 1)
                            wait(e, sum_ready, g.n - 1)
                            for a in range(GT):
                                mm = e.transpose(p_r[s][:, a * D:(a + 1) * D], yT[:, s, a * P:(a + 1) * P], ident[:])
                            mm.then_inc(y_turned, 1)

                    over_tiles(e, NG, GUN, LAG, step)

                @block.scalar
                def _(e):
                    def step(t):
                        if (g := t.ago(9)):
                            s = g.k % 2
                            e.wait_ge(y_prod, g.n + 1)
                            wait(e, y_turned, g.n - 1)
                            e.activation(yT[:, s, :], p_y[:], ACT.Identity, bias=bf2[:]).then_inc(yT_ready, 1)
                        if (g := t.ago(6)):
                            s = g.k % 2
                            e.wait_ge(n_turned, g.n + 1)
                            wait(e, f_prod, FCH * (g.n - 1))
                            e.activation(nT[:, s, :], p_n[:], ACT.Copy).then_inc(nT_ready, 1)
                        if (g := t.ago(7)):
                            s = g.k % 2
                            for ch in range(FCH):
                                e.wait_ge(f_prod, FCH * g.n + ch + 1)
                                if ch == 0:
                                    wait(e, y_prod, g.n - 1)
                                e.activation(g_T[:, s, ch, :], p_f[ch][:], ACT.Gelu, bias=bf1[:, ch:ch + 1]).then_inc(gelu_ready, 1)

                    over_tiles(e, NG, GUN, LAG, step)

                @block.vector
                def _(e):
                    def norm_rows(into, rows_in, mean, scale, ready):
                        for a in range(GT):
                            ins = e.tensor_scalar(into[:, a * D:(a + 1) * D], rows_in[:, a * D:(a + 1) * D],
                                                  mean[:, a, 0:1], scale[:, a:a + 1], ALU.subtract, ALU.mult)
                        ins.then_inc(ready, 1)

                    def step(t):
                        if (g := t.ago(11)):
                            s = g.k % 2
                            e.wait_ge(y_turned, g.n + 1)
                            e.wait_ge(both_ready, g.n + 1)
                            e.tensor_tensor(both[:, g.k, :], p_r[s][:], both[:, g.k, :], ALU.add).then_inc(sum_ready, 1)
                        if (g := t.ago(2)):
                            s = g.k % 2
                            e.wait_ge(x2_ready, g.n + 1)
                            wait(e, mv_ready, g.n - 1)
                            for a in range(GT):
                                ins = e.bn_stats(stats[:, s, a, :], y_in[:, g.k, a * D:(a + 1) * D])
                            ins.then_inc(stats_ready, 1)
                        if (g := t.ago(11)):
                            s = g.k % 2
                            e.wait_ge(sum_ready, g.n + 1)
                            wait(e, mv2_ready, g.n - 1)
                            for a in range(GT):
                                ins = e.bn_stats(stats2[:, s, a, :], both[:, g.k, a * D:(a + 1) * D])
                            ins.then_inc(stats2_ready, 1)
                        if (g := t.ago(2)):
                            s = g.k % 2
                            e.wait_ge(stats_ready, g.n + 1)
                            gate(e)
                            for a in range(GT):
                                ins = e.bn_aggr(mv[:, g.k, a, :], stats[:, s, a, :])
                            ins.then_inc(mv_ready, 1)
                        if (g := t.ago(4)):
                            s = g.k % 2
                            e.wait_ge(rstd_ready, g.n + 1)
                            wait(e, n_turned, g.n - 1)
                            norm_rows(normed[:, s, :], y_in[:, g.k, :], mv[:, g.k], rstd[:, s], normed_ready)
                        if (g := t.ago(11)):
                            s = g.k % 2
                            e.wait_ge(stats2_ready, g.n + 1)
                            gate(e)
                            for a in range(GT):
                                ins = e.bn_aggr(mv2[:, g.k, a, :], stats2[:, s, a, :])
                            ins.then_inc(mv2_ready, 1)
                        if (g := t.ago(13)):
                            e.wait_ge(rstd2_ready, g.n + 1)
                            norm_rows(res[:, g.k, :], both[:, g.k, :], mv2[:, g.k], rstd2[:, g.k % 2], res_ready)

                    over_tiles(e, NG, GUN, LAG, step)

        prepare()
        dense()
        for l in range(2):
            layer(l)
            layer_border(l)
        with ExitStack() as att:
            logits = sb("logits", [P, 2 * HEADS, COLS], F32, att)
            weight = sb("weight", [P, HEADS, COLS], F32, att)
            z_inv = sb("z_inv", [P, HEADS, COLS], F32, att)
            self_weight = sb("self_weight", [P, HEADS, COLS], F32, att)
            border_z = sb("border_z", [P, 3, HEADS], F32, att)
            values = sb("values", [P, COLS, D], F32, att)
            attention(values, logits)
            softmax(logits, weight, z_inv, self_weight, border_z)
            weighted(values, weight, z_inv, self_weight)
            weighted_border(border_z)
        ffn()


_INS = ['x', 'src', 'dst', 'edge_type_200', 'L0_gnn_rel_embed', 'L0_gnn_W_r1', 'L0_gnn_W_sl1', 'L0_gnn_W_el1',
        'L0_gnn_W_r2', 'L0_gnn_W_sl2', 'L0_gnn_W_el2', 'L1_gnn_Wq', 'L1_gnn_bq', 'L1_gnn_Wk', 'L1_gnn_bk',
        'L1_gnn_Wv', 'L1_gnn_bv', 'L1_gnn_Wo', 'L1_gnn_bo', 'L1_gnn_g1', 'L1_gnn_b1', 'L1_gnn_g2', 'L1_gnn_b2',
        'L1_gnn_W1', 'L1_gnn_bf1', 'L1_gnn_W2', 'L1_gnn_bf2']


def kernel(**inputs):
    import numpy as _np
    import concourse.bacc as _bacc
    from concourse import mybir as _mybir
    from concourse.bass_utils import run_bass_kernel_spmd as _run

    nc = _bacc.Bacc("TRN2", target_bir_lowering=False, num_devices=1)
    arrays, args = {}, []
    for name in _INS:
        a = _np.ascontiguousarray(inputs[name])
        arrays[f"in_{name}_dram"] = a
        args.append(nc.dram_tensor(f"in_{name}_dram", a.shape, _mybir.dt.from_np(a.dtype), kind="ExternalInput").ap())
    out = nc.dram_tensor("out_0_dram", inputs['x'].shape, _mybir.dt.float32, kind="ExternalOutput").ap()
    gnn_program(nc, *args, out)
    r = _run(nc, [arrays], core_ids=[0])
    return r.results[0]["out_0_dram"]
```
